# Optimizing a Trainium2 kernel written in Bass

```python
import numpy as np
import jax
import jax.numpy as jnp

def _softmax(x, axis=-1):
    return jax.nn.softmax(x, axis=axis)

def _gelu(x):
    return jax.nn.gelu(x, approximate=True)

def _silu(x):
    return jax.nn.silu(x)

def _sigmoid(x):
    return jax.nn.sigmoid(x)

def _layernorm(x, axis=-1, eps=1e-05):
    m = jnp.mean(x, axis=axis, keepdims=True)
    v = jnp.var(x, axis=axis, keepdims=True)
    return (x - m) / jnp.sqrt(v + eps)

def _scatter_add(tgt, idx, src, axis=0):
    return tgt.at[idx].add(src)

def _segment_sum(src, seg, n):
    return jax.ops.segment_sum(src, seg, n)
kernel_name = 'mk_adaln_d2_jaxref_r8_b5ce16'

def setup_inputs(seed: int=0):
    np.random.seed(seed)
    _w = jnp.asarray

    def _L0_attn_setup():
        import jax, jax.numpy as jnp
        import numpy as np
        D_MODEL = 128
        NUM_HEADS = 16
        D_K = D_MODEL // NUM_HEADS
        BATCH, SEQ = (2, 256)
        key = jax.random.key(seed)
        k = jax.random.split(key, 5)
        std = np.sqrt(2.0 / (D_MODEL + D_MODEL)).astype(np.float32)
        return {'x': jax.random.normal(k[0], (BATCH, SEQ, D_MODEL), dtype=jnp.float32), 'WQ': jax.random.normal(k[1], (D_MODEL, D_MODEL), dtype=jnp.float32) * std, 'WK': jax.random.normal(k[2], (D_MODEL, D_MODEL), dtype=jnp.float32) * std, 'WV': jax.random.normal(k[3], (D_MODEL, D_MODEL), dtype=jnp.float32) * std, 'WO': jax.random.normal(k[4], (D_MODEL, D_MODEL), dtype=jnp.float32) * std}
    _L0_attn_in = _L0_attn_setup()

    def _L0_ffn_setup():
        import jax, jax.numpy as jnp
        import numpy as np
        B, S, D = (4, 256, 128)
        P = 9
        DM = D // 4
        EPS = 1e-05

        def _mix(x, mix_kernel):
            xp = jnp.pad(x, ((0, 0), (1, 1), (0, 0)))
            return mix_kernel[0] * xp[:, :-2] + mix_kernel[1] * xp[:, 1:-1] + mix_kernel[2] * xp[:, 2:]

        def _layernorm(h, gamma, beta):
            mu = jnp.mean(h, axis=-1, keepdims=True)
            var = jnp.var(h, axis=-1, keepdims=True)
            return (h - mu) * jax.lax.rsqrt(var + EPS) * gamma + beta
        key = jax.random.key(seed)
        ks = jax.random.split(key, 12)
        sc_in = 1.0 / np.sqrt(D)
        sc_mid = 1.0 / np.sqrt(DM)
        return {'x': jax.random.normal(ks[0], (B, S, D), dtype=jnp.float32), 'mix_kernel': jax.random.normal(ks[1], (3, D), dtype=jnp.float32) * 0.5, 'W1': jax.random.normal(ks[2], (P, D, DM), dtype=jnp.float32) * sc_in, 'b1': jnp.zeros((P, DM), dtype=jnp.float32), 'W2': jax.random.normal(ks[3], (P, DM, D), dtype=jnp.float32) * sc_mid, 'b2': jnp.zeros((P, D), dtype=jnp.float32), 'Wo1': jax.random.normal(ks[4], (D, DM), dtype=jnp.float32) * sc_in, 'bo1': jnp.zeros((DM,), dtype=jnp.float32), 'Wo2': jax.random.normal(ks[5], (DM, P), dtype=jnp.float32) * sc_mid, 'bo2': jnp.zeros((P,), dtype=jnp.float32), 'gamma': jnp.ones((D,), dtype=jnp.float32), 'beta': jnp.zeros((D,), dtype=jnp.float32)}
    _L0_ffn_in = _L0_ffn_setup()
    _L0_c = _w((lambda *s: np.random.randn(*s).astype(np.float32) * 0.05)(1, 128))
    _L0_wmod = _w((lambda *s: np.random.randn(*s).astype(np.float32) * 0.05)(128, 6 * 128) * 128 ** (-0.5))

    def _L1_attn_setup():
        import jax, jax.numpy as jnp
        import numpy as np
        HEADS = 8
        BLOCK = 32
        key = jax.random.key(seed)
        ks = jax.random.split(key, 4)
        b, n, d, f = (4, 512, 128, 128)
        x = jax.random.normal(ks[0], (b, n, d), dtype=jnp.float32)
        w_qkv = jax.random.normal(ks[1], (3 * d, d), dtype=jnp.float32) * d ** (-0.5)
        w_out = jax.random.normal(ks[2], (d, d), dtype=jnp.float32) * d ** (-0.5)
        b_out = jnp.zeros((d,), dtype=jnp.float32)
        proj = jax.random.normal(ks[3], (HEADS, d // HEADS, f), dtype=jnp.float32) * (d // HEADS) ** (-0.5)
        return {'x': x, 'w_qkv': w_qkv, 'w_out': w_out, 'b_out': b_out, 'proj': proj}
    _L1_attn_in = _L1_attn_setup()

    def _L1_ffn_setup():
        import math
        import jax, jax.numpy as jnp
        import numpy as np
        D_MODEL = 128
        D_HIDDEN = 512
        N_EXPERTS = 8
        TOP_K = 2
        CAPACITY_FACTOR = 1.25
        key = jax.random.key(seed)
        ks = jax.random.split(key, 8)
        s = 0.02
        x = jax.random.normal(ks[0], (4, 256, D_MODEL), dtype=jnp.float32)
        router_w = jax.random.normal(ks[1], (D_MODEL, N_EXPERTS), dtype=jnp.float32) * s
        router_b = jnp.zeros((N_EXPERTS,), dtype=jnp.float32)
        w1 = jax.random.normal(ks[2], (N_EXPERTS, D_MODEL, D_HIDDEN), dtype=jnp.float32) * s
        b1 = jnp.zeros((N_EXPERTS, D_HIDDEN), dtype=jnp.float32)
        w2 = jax.random.normal(ks[3], (N_EXPERTS, D_HIDDEN, D_MODEL), dtype=jnp.float32) * s
        b2 = jnp.zeros((N_EXPERTS, D_MODEL), dtype=jnp.float32)
        return {'x': x, 'router_w': router_w, 'router_b': router_b, 'w1': w1, 'b1': b1, 'w2': w2, 'b2': b2}
    _L1_ffn_in = _L1_ffn_setup()
    _L1_c = _w((lambda *s: np.random.randn(*s).astype(np.float32) * 0.05)(1, 128))
    _L1_wmod = _w((lambda *s: np.random.randn(*s).astype(np.float32) * 0.05)(128, 6 * 128) * 128 ** (-0.5))
    _d = {'L0_attn_x': _L0_attn_in['x'], 'L0_attn_WQ': _L0_attn_in['WQ'], 'L0_attn_WK': _L0_attn_in['WK'], 'L0_attn_WV': _L0_attn_in['WV'], 'L0_attn_WO': _L0_attn_in['WO'], 'L0_ffn_mix_kernel': _L0_ffn_in['mix_kernel'], 'L0_ffn_W1': _L0_ffn_in['W1'], 'L0_ffn_b1': _L0_ffn_in['b1'], 'L0_ffn_W2': _L0_ffn_in['W2'], 'L0_ffn_b2': _L0_ffn_in['b2'], 'L0_ffn_Wo1': _L0_ffn_in['Wo1'], 'L0_ffn_bo1': _L0_ffn_in['bo1'], 'L0_ffn_Wo2': _L0_ffn_in['Wo2'], 'L0_ffn_bo2': _L0_ffn_in['bo2'], 'L0_ffn_gamma': _L0_ffn_in['gamma'], 'L0_ffn_beta': _L0_ffn_in['beta'], 'L0_c': _L0_c, 'L0_wmod': _L0_wmod, 'L1_attn_w_qkv': _L1_attn_in['w_qkv'], 'L1_attn_w_out': _L1_attn_in['w_out'], 'L1_attn_b_out': _L1_attn_in['b_out'], 'L1_attn_proj': _L1_attn_in['proj'], 'L1_ffn_router_w': _L1_ffn_in['router_w'], 'L1_ffn_router_b': _L1_ffn_in['router_b'], 'L1_ffn_w1': _L1_ffn_in['w1'], 'L1_ffn_b1': _L1_ffn_in['b1'], 'L1_ffn_w2': _L1_ffn_in['w2'], 'L1_ffn_b2': _L1_ffn_in['b2'], 'L1_c': _L1_c, 'L1_wmod': _L1_wmod}
    _x0 = _d['L0_attn_x']
    _d['L0_attn_x'] = jax.random.normal(jax.random.fold_in(jax.random.key(seed), 1), (1, 2048, 128), dtype=_x0.dtype)
    del _x0
    return _d

def reference(L0_attn_x, L0_attn_WQ, L0_attn_WK, L0_attn_WV, L0_attn_WO, L0_ffn_mix_kernel, L0_ffn_W1, L0_ffn_b1, L0_ffn_W2, L0_ffn_b2, L0_ffn_Wo1, L0_ffn_bo1, L0_ffn_Wo2, L0_ffn_bo2, L0_ffn_gamma, L0_ffn_beta, L0_c, L0_wmod, L1_attn_w_qkv, L1_attn_w_out, L1_attn_b_out, L1_attn_proj, L1_ffn_router_w, L1_ffn_router_b, L1_ffn_w1, L1_ffn_b1, L1_ffn_w2, L1_ffn_b2, L1_c, L1_wmod):

    def _L0_attn_ref(x, WQ, WK, WV, WO):
        import jax, jax.numpy as jnp
        import numpy as np
        D_MODEL = 128
        NUM_HEADS = 16
        D_K = D_MODEL // NUM_HEADS
        BATCH, SEQ = (2, 256)
        B, S, E = x.shape
        mask = jnp.where(jnp.triu(jnp.ones((S, S), dtype=bool), k=1), -jnp.inf, 0.0).astype(x.dtype)

        def heads(W):
            return (x @ W).reshape(B, S, NUM_HEADS, D_K).transpose(0, 2, 1, 3)
        Q, K, V = (heads(WQ), heads(WK), heads(WV))
        score = jnp.einsum('bhqd,bhkd->bhqk', Q, K) / jnp.sqrt(jnp.asarray(D_K, x.dtype))
        score = score + mask
        score = score - jnp.max(score, axis=-1, keepdims=True)
        score = jnp.exp(score)
        score = score / jnp.sum(score, axis=-1, keepdims=True)
        out = jnp.einsum('bhqk,bhkd->bhqd', score, V)
        out = out.transpose(0, 2, 1, 3).reshape(B, S, E)
        return out @ WO

    def _L0_ffn_ref(x, mix_kernel, W1, b1, W2, b2, Wo1, bo1, Wo2, bo2, gamma, beta):
        import jax, jax.numpy as jnp
        import numpy as np
        B, S, D = (4, 256, 128)
        P = 9
        DM = D // 4
        EPS = 1e-05

        def _mix(x, mix_kernel):
            xp = jnp.pad(x, ((0, 0), (1, 1), (0, 0)))
            return mix_kernel[0] * xp[:, :-2] + mix_kernel[1] * xp[:, 1:-1] + mix_kernel[2] * xp[:, 2:]

        def _layernorm(h, gamma, beta):
            mu = jnp.mean(h, axis=-1, keepdims=True)
            var = jnp.var(h, axis=-1, keepdims=True)
            return (h - mu) * jax.lax.rsqrt(var + EPS) * gamma + beta
        x_mixed = _mix(x, mix_kernel)
        h = jnp.einsum('bsd,pdm->bspm', x_mixed, W1) + b1
        stacked_paths = jnp.einsum('bspm,pmd->bspd', h, W2) + b2
        scores = jnp.tanh(x_mixed @ Wo1 + bo1) @ Wo2 + bo2
        idx = jnp.argmax(scores, axis=-1)
        weights = jax.nn.one_hot(idx, P, dtype=stacked_paths.dtype)
        collapsed = jnp.einsum('bspd,bsp->bsd', stacked_paths, weights)
        return _layernorm(x + collapsed, gamma, beta)

    def _L1_attn_ref(x, w_qkv, w_out, b_out, proj):
        import jax, jax.numpy as jnp
        import numpy as np
        HEADS = 8
        BLOCK = 32
        b, n, d = x.shape
        h = HEADS
        hd = d // h
        nb = n // BLOCK
        qkv = x @ w_qkv.T
        q, k, v = jnp.split(qkv, 3, axis=-1)

        def to_blocks(t):
            return t.reshape(b, n, h, hd).transpose(0, 2, 1, 3).reshape(b, h, nb, BLOCK, hd)
        q, k, v = (to_blocks(q), to_blocks(k), to_blocks(v))
        qp = jax.nn.elu(jnp.einsum('bhcsd,hdf->bhcsf', q, proj)) + 1.0
        kp = jax.nn.elu(jnp.einsum('bhcsd,hdf->bhcsf', k, proj)) + 1.0
        kv = jnp.einsum('bhcsf,bhcsd->bhcfd', kp, v)
        num = jnp.einsum('bhcsf,bhcfd->bhcsd', qp, kv)
        ksum = kp.sum(axis=3)
        z = 1.0 / (jnp.einsum('bhcsf,bhcf->bhcs', qp, ksum) + 1e-08)
        out = num * z[..., None]
        out = out.reshape(b, h, n, hd).transpose(0, 2, 1, 3).reshape(b, n, d)
        return out @ w_out.T + b_out

    def _L1_ffn_ref(x, router_w, router_b, w1, b1, w2, b2):
        import math
        import jax, jax.numpy as jnp
        import numpy as np
        D_MODEL = 128
        D_HIDDEN = 512
        N_EXPERTS = 8
        TOP_K = 2
        CAPACITY_FACTOR = 1.25
        B, T, D = x.shape
        N = B * T
        E = N_EXPERTS
        capacity = max(1, math.ceil(N / E * CAPACITY_FACTOR))
        x_flat = x.reshape(N, D)
        logits = x_flat.astype(jnp.float32) @ router_w + router_b
        gates = jax.nn.softmax(logits, axis=-1)
        _, topk_idx = jax.lax.top_k(gates, TOP_K)
        expert_mask = jax.nn.one_hot(topk_idx, E, dtype=jnp.int32).sum(1)
        pos = jnp.cumsum(expert_mask, axis=0) - 1
        expert_mask = expert_mask * (pos < capacity)
        valid = expert_mask > 0
        pos_c = jnp.where(valid, pos, capacity)
        e_idx = jnp.broadcast_to(jnp.arange(E), (N, E))
        dispatched = x_flat[:, None, :] * valid[:, :, None].astype(x.dtype)
        buf = jnp.zeros((E, capacity + 1, D), x.dtype).at[e_idx.ravel(), pos_c.ravel()].add(dispatched.reshape(N * E, D))
        buf = buf[:, :capacity]
        h = jax.nn.gelu(jnp.einsum('ecd,edh->ech', buf, w1) + b1[:, None, :], approximate=False)
        out = jnp.einsum('ech,ehd->ecd', h, w2) + b2[:, None, :]
        pos_g = jnp.minimum(pos_c, capacity - 1)
        gathered = out[e_idx, pos_g]
        weights = (gates * valid).astype(x.dtype)
        y = jnp.einsum('ned,ne->nd', gathered, weights)
        return y.reshape(B, T, D)
    x = L0_attn_x
    mod = (_silu(L0_c) @ L0_wmod).reshape(L0_c.shape[0], 6, 1, -1)
    sa, ca, ga, sb, cb, gb = (mod[:, 0], mod[:, 1], mod[:, 2], mod[:, 3], mod[:, 4], mod[:, 5])
    ga = (2 * (ga >= 0) - 1) * jnp.maximum(jnp.abs(ga), 0.25)
    gb = (2 * (gb >= 0) - 1) * jnp.maximum(jnp.abs(gb), 0.25)
    h = _layernorm(x, axis=-1) * (1 + ca) + sa
    x = x + ga * _L0_attn_ref(h, L0_attn_WQ, L0_attn_WK, L0_attn_WV, L0_attn_WO)
    h = _layernorm(x, axis=-1) * (1 + cb) + sb
    x = x + gb * _L0_ffn_ref(h, L0_ffn_mix_kernel, L0_ffn_W1, L0_ffn_b1, L0_ffn_W2, L0_ffn_b2, L0_ffn_Wo1, L0_ffn_bo1, L0_ffn_Wo2, L0_ffn_bo2, L0_ffn_gamma, L0_ffn_beta)
    mod = (_silu(L1_c) @ L1_wmod).reshape(L1_c.shape[0], 6, 1, -1)
    sa, ca, ga, sb, cb, gb = (mod[:, 0], mod[:, 1], mod[:, 2], mod[:, 3], mod[:, 4], mod[:, 5])
    ga = (2 * (ga >= 0) - 1) * jnp.maximum(jnp.abs(ga), 0.25)
    gb = (2 * (gb >= 0) - 1) * jnp.maximum(jnp.abs(gb), 0.25)
    h = _layernorm(x, axis=-1) * (1 + ca) + sa
    x = x + ga * _L1_attn_ref(h, L1_attn_w_qkv, L1_attn_w_out, L1_attn_b_out, L1_attn_proj)
    h = _layernorm(x, axis=-1) * (1 + cb) + sb
    x = x + gb * _L1_ffn_ref(h, L1_ffn_router_w, L1_ffn_router_b, L1_ffn_w1, L1_ffn_b1, L1_ffn_w2, L1_ffn_b2)
    return x

_drawn_inputs = setup_inputs


def setup_inputs(seed=0):
    import zlib

    import numpy as np

    out = dict(_drawn_inputs(seed))
    spreads = {'L0_ffn_b1': (0.0, 0.431),
     'L0_ffn_b2': (0.0, 0.411),
     'L0_ffn_bo1': (0.0, 0.1),
     'L0_ffn_bo2': (0.0, 0.1),
     'L0_ffn_gamma': (1.0, 0.2),
     'L0_ffn_beta': (0.0, 0.301),
     'L1_attn_b_out': (0.0, 0.335),
     'L1_ffn_router_b': (0.0, 0.8),
     'L1_ffn_b1': (0.0, 0.8),
     'L1_ffn_b2': (0.0, 0.8)}
    factors = {'L1_attn_proj': 8.0, 'L1_ffn_router_w': 8.0, 'L1_ffn_w1': 8.0, 'L1_ffn_w2': 8.0}
    for name, (base, spread) in spreads.items():
        noise = np.random.default_rng([zlib.crc32(name.encode()), seed]).standard_normal(out[name].shape)
        drawn = base * np.exp(spread * noise) if base else spread * noise
        out[name] = jnp.asarray(drawn.astype(out[name].dtype))
    for name, factor in factors.items():
        out[name] = (out[name] * factor).astype(out[name].dtype)
    return out
```

```python
from contextlib import ExitStack

import concourse.bass as bass
from concourse import mybir

P = 128
ALU = mybir.AluOpType
ACT = mybir.ActivationFunctionType
AX = mybir.AxisListType
F32 = mybir.dt.float32
BF16 = mybir.dt.bfloat16
I32 = mybir.dt.int32
U32 = mybir.dt.uint32
EPS = 1e-5
MASKED = -1e30


def adaln_two_layers(
    nc: bass.Bass, x, WQ, WK, WV, WO, mix_kernel, W1, b1, W2, b2, Wo1, bo1, Wo2, bo2, gamma, beta,
    c0, wmod0, w_qkv_heads, w_v, w_out, b_out, proj, router_w, router_b, ew1, eb1, ew2, eb2, c1, wmod1, out,
):
    S, D = x.shape[1], x.shape[2]
    TILES = S // P
    CH = 4
    CT = TILES // CH
    CW = CT * P
    H0, DK = 16, D // 16
    HG = 4
    GROUPS = H0 // HG
    ROWS = 96
    SCALE = float(DK) ** -0.5
    NP, DM = W1.shape[1], W1.shape[2]
    PG = 3
    NG = NP // PG
    GR = PG * DM
    HD, H1 = proj.shape[0], proj.shape[1]
    BLK = 32
    E, HID = ew1.shape[1], ew1.shape[2]
    HC = HID // P
    CAP = max(1, -(-S * 5 // (E * 4)))
    SLOTS = E * CAP
    ST = SLOTS // P
    assert SLOTS % P == 0 and ST % 4 == 0 and D == P and TILES == CH * CT

    ctx = ExitStack()
    with ctx:
        def sb(name, shape, dt=F32):
            return ctx.enter_context(nc.sbuf_tensor(name, shape, dt))

        def sem(name):
            return ctx.enter_context(nc.semaphore(name))

        qk_dram = nc.dram_tensor("qk_parts_dram", (2, 3, D, S), BF16, kind="Internal").ap()
        slot_in = nc.dram_tensor("slot_in_dram", (SLOTS, D), F32, kind="Internal").ap()
        slot_out = nc.dram_tensor("slot_out_dram", (SLOTS, D), F32, kind="Internal").ap()

        ps = ctx.enter_context(nc.psum_tensor("ps", [P, 8, 512], F32))

        X = sb("X", [P, TILES, D])
        nrm = sb("nrm", [P, TILES, D])
        hT = sb("hT", [P, 2, S + 2])
        stats = sb("stats", [P, CT, 6])
        mv = sb("mv", [P, 2, CT, 2])
        ve = sb("ve", [P, 2, CT])
        rstd = sb("rstd", [P, 2, CT])
        cT = sb("cT", [P, 2, CW])
        identf = sb("identf", [P, P])
        identb = sb("identb", [P, P], BF16)
        onesf = sb("onesf", [P, P])
        onesb = sb("onesb", [P, P], BF16)
        causal = sb("causal", [P, P], BF16)
        blockmask = sb("blockmask", [P, P])
        upto = sb("upto", [P, P], BF16)
        spread = sb("spread", [NP, NP, DM], BF16)
        rank9 = sb("rank9", [P, CT, NP])
        rank8 = sb("rank8", [P, TILES, E])
        neghalf = sb("neghalf", [P, CT])
        onerow = hT[0:2, 1, 1:1 + S // 2].bitcast(BF16)
        ccol = sb("ccol", [P, 2])
        cexp = sb("cexp", [P, 2])
        cden = sb("cden", [P, 2])
        crec = sb("crec", [P, 2])
        scol = sb("scol", [P, 2])
        smat = sb("smat", [P, 2, P])
        wmod = sb("wmod", [P, 2, 6 * D])
        modc = sb("modc", [P, 2, 4])
        gate = sb("gate", [P, 4, D])
        wq = sb("wq", [P, 4, D])
        wog = sb("wog", [P, D])
        mixc = sb("mixc", [P, 3])
        w1s = sb("w1s", [P, NP, DM])
        b1c = sb("b1c", [GR, NG])
        w2s = sb("w2s", [GR, NG, D])
        b2s = sb("b2s", [NP, D])
        wo1 = sb("wo1", [P, DM])
        bo1c = sb("bo1c", [DM, 1])
        wo2 = sb("wo2", [DM + 1, NP])
        gb_rows = sb("gb_rows", [P, 2, D])
        gbg = sb("gbg", [P, 2, D])
        wvrow = sb("wvrow", [P, D])
        wvT = sb("wvT", [P, D])
        pfold = sb("pfold", [P, 2 * H1, P])
        woutT = sb("woutT", [P, 2, D])
        brow = sb("brow", [1, D])
        browg = sb("browg", [1, D])
        rw = sb("rw", [P, E])
        rb = sb("rb", [1, E])
        eb1c = sb("eb1c", [P, E, HC])
        eb2r = sb("eb2r", [1, E, D])
        KS = sb("KS", [P, 2, HG, S], BF16)
        QS = sb("QS", [P, 2, HG, S], BF16)
        vtok = sb("vtok", [P, TILES, D])
        Vg = sb("Vg", [P, 2, TILES, HG, 32])
        pT = sb("pT", [P, 3, HG, CW])
        tmax = sb("tmax", [P, 2, CT * HG, CH])
        negm = sb("negm", [P, CT * HG])
        mhl = sb("mhl", [P, CT, HG, 2], BF16)
        rden = sb("rden", [P, CT, HG])
        shared = sb("shared", [P, 8 * CW])
        parts = shared[:, 0:6 * CW].bitcast(BF16).rearrange(
            "p (a k b s) -> p a k b s", a=3, k=2, b=2)
        rest = shared[:, 6 * CW:8 * CW].rearrange("p (k s) -> p k s", k=2)
        oT = shared[:, 0:2 * CW].rearrange("p (b s) -> p b s", b=2)
        attn = shared[:, 2 * CW:6 * CW].rearrange("p (t d) -> p t d", t=TILES)
        taug = shared[0:DM + 1, 6 * CW:7 * CW]
        gsgn = rest[:, 0, :].rearrange("p (g d) -> p g d", g=4)
        gneg, gabs = (cT[:, b, :].rearrange("p (g d) -> p g d", g=4) for b in range(2))
        early = pT[:, :, :, :].rearrange("p a h s -> p (a h s)")
        wqkv16 = early[0:HD, 0:3 * H1 * D].rearrange("p (h d) -> p h d", h=3 * H1)
        proj_s = early[0:HD, 3 * H1 * D:4 * H1 * D].rearrange("p (h d) -> p h d", h=H1)
        woutp = early[:, 4 * H1 * D:4 * H1 * D + 32 * H1].rearrange("p (h c) -> p h c", h=H1)
        eq9 = sb("eq9", [P, CT, NP])
        top9 = sb("top9", [P, CT])
        best9 = sb("best9", [P, CT])
        hot9 = sb("hot9", [P, CT, 16], BF16)
        hotT = sb("hotT", [NP, CW], BF16)
        hotTf = shared[0:NP, 7 * CW:8 * CW]

        KSf = KS[:, :, :, :].rearrange("p b h s -> p (b h s)").bitcast(F32)
        QSf = QS[:, :, :, :].rearrange("p b h s -> p (b h s)").bitcast(F32)
        assert H0 * S // 4 >= E * HC * D
        hid = pT[0:GR, 0, 0:NG, :]
        hsel = pT[0:GR, 1, 0:NG, :]
        tmp = pT[:, 2, :, 0:D]
        expq = KSf[:, 0:2 * 2 * CW].rearrange("p (b k s) -> p b k s", b=2, k=2)
        feat = KSf[:, 2 * 2 * CW:4 * 2 * CW].rearrange("p (b k s) -> p b k s", b=2, k=2)
        am = pT[:, 0, 0:2, :]
        recd = pT[:, 0, 2, :]
        onT = pT[:, 1, 0:2, :]
        vaug = Vg[:, 0, 0:CT, :, :].rearrange("p t h c -> p (t h c)")
        vpad = Vg[:, 0, 0:2 * CT, :, :].rearrange("p (t k) h c -> p t (k h) c", k=2)
        ew1s = QSf[:, 0:E * HID].rearrange("p (e h) -> p e h", e=E)
        ew2s = QSf[:, E * HID:2 * E * HID].rearrange("p (e c d) -> p e c d", e=E, c=HC)

        x_loaded = sem("x_loaded")
        mod_loaded = sem("mod_loaded")
        w_loaded = sem("w_loaded")
        w2_loaded = sem("w2_loaded")
        ex_loaded = sem("ex_loaded")
        consts = sem("consts")
        pchain = sem("pchain")
        dchain = sem("dchain")
        achain = sem("achain")
        c_exp = sem("c_exp")
        silu_ready = sem("silu_ready")
        mod_mm = sem("mod_mm")
        mod_ready = sem("mod_ready")
        fold_mm = sem("fold_mm")
        fold_ready = sem("fold_ready")
        ve_ready = sem("ve_ready")
        rstd_ready = sem("rstd_ready")
        nrm_ready = sem("nrm_ready")
        tposed = sem("tposed")
        hT_ready = sem("hT_ready")
        qk_mm = sem("qk_mm")
        qk_hi = sem("qk_hi")
        qk_rest = sem("qk_rest")
        qk_mid = sem("qk_mid")
        qk_lo = sem("qk_lo")
        qk_stored = [sem(f"qk_stored{i}") for i in range(2)]
        v_ready = sem("v_ready")
        heads_loaded = [sem(f"heads_loaded{i}") for i in range(2)]
        vg_ready = sem("vg_ready")
        heads_free = [sem(f"heads_free{i}") for i in range(2)]
        a_ready = sem("a_ready")
        a_maxed = sem("a_maxed")
        m_parts = sem("m_parts")
        m_turned = sem("m_turned")
        m_rows = sem("m_rows")
        m_neg = sem("m_neg")
        b_ready = sem("b_ready")
        b_exped = sem("b_exped")
        diag_cut = sem("diag_cut")
        pv_done = sem("pv_done")
        o_copied = sem("o_copied")
        o_turned = sem("o_turned")
        o_rden = sem("o_rden")
        o_normed = sem("o_normed")
        at_turned = sem("at_turned")
        at_ready = sem("at_ready")
        y_mm = sem("y_mm")
        y_read = sem("y_read")
        conv_first = sem("conv_first")
        conv_ready = sem("conv_ready")
        u_mm = sem("u_mm")
        t_ready = sem("t_ready")
        hid_mm = sem("hid_mm")
        hid_ready = sem("hid_ready")
        sc_mm = sem("sc_mm")
        hot_ready = sem("hot_ready")
        hot_turned = sem("hot_turned")
        hot_copied = sem("hot_copied")
        mask_mm = sem("mask_mm")
        hsel_ready = sem("hsel_ready")
        ffn_mm = sem("ffn_mm")
        ffn_read = sem("ffn_read")
        v1_mm = sem("v1_mm")
        v1_ready = sem("v1_ready")
        f_mm = sem("f_mm")
        f_exp = sem("f_exp")
        f_ready = sem("f_ready")
        s_mm = sem("s_mm")
        s_ready = sem("s_ready")
        av_mm = sem("av_mm")
        on_ready = sem("on_ready")
        y1_mm = sem("y1_mm")
        y1_read = sem("y1_read")
        lg_mm = sem("lg_mm")
        r_exped = sem("r_exped")
        r_shift = sem("r_shift")
        r_mask = sem("r_mask")
        pos_mm = sem("pos_mm")
        slots_ready = sem("slots_ready")
        zero_filled = sem("zero_filled")
        scattered = sem("scattered")
        slots_loaded = sem("slots_loaded")
        xs_turned = sem("xs_turned")
        xs_ready = sem("xs_ready")
        e1_mm = sem("e1_mm")
        gelu_ready = sem("gelu_ready")
        e2_mm = sem("e2_mm")
        eo_ready = sem("eo_ready")
        eo_stored = [sem(f"eo_stored{i}") for i in range(2)]
        gathered = [sem(f"gathered{i}") for i in range(CH)]
        out_ready = sem("out_ready")
        out_stored = sem("out_stored")

        lg = sb("lg", [P, TILES, E])
        gates = sb("gates", [P, TILES, E])
        red = sb("red", [P, 12, TILES])
        hot = sb("hot", [P, 2, TILES, E])
        sel = sb("sel", [P, 2, TILES, E])
        chosen = sb("chosen", [P, TILES, E], BF16)
        slotf = sb("slotf", [P, 2, TILES])
        slot_w = sb("slot_w", [P, 2, TILES], U32)
        slot_r = sb("slot_r", [P, 2, TILES], U32)
        wsel = sb("wsel", [P, 2, TILES])
        slotrows = KSf[:, 0:ST * D].rearrange("p (t d) -> p t d", t=ST)
        gath = KSf[:, ST * D:ST * D + 2 * TILES * D].rearrange("p (k t d) -> p k t d", k=2, t=TILES)
        xsT = Vg[:, :, :, :, :].rearrange("p a t h c -> p (a t h c)")[:, 0:SLOTS]
        gT = pT[:, :, :, :].rearrange("p a h s -> p (a h s)")[:, 0:2 * HC * CAP].rearrange(
            "p (b c s) -> p b c s", b=2, c=HC)
        eo = oT[:, :, 0:3 * D].rearrange("p b (s d) -> p b s d", s=3)
        zeros = attn

        A_TOTAL = 2 * sum(CT * HG * (c + 1) for c in range(CH))
        ITEMS = 2 * CH
        UNITS = 2 * sum(CT * (c + 1) for c in range(CH))
        DIAGS = 2 * CH * CT
        items = [(0, c) for c in range(CH)] + [(1, c) for c in reversed(range(CH))]

        def pieces(it):
            g, c = items[it]
            return [(g, c, qi, j, kc) for qi in range(CT) for j in range(HG) for kc in range(c + 1)]

        a_start = [sum(len(pieces(n)) for n in range(it)) for it in range(ITEMS + 1)]
        units = [(it, kb) for it in range(ITEMS) for kb in range(CT * (items[it][1] + 1))]
        diag_no = {u: n for n, u in enumerate(u for u, (it, kb) in enumerate(units) if kb >= CT * items[it][1])}
        last_unit = {it: max(u for u, x_ in enumerate(units) if x_[0] == it) for it in range(ITEMS)}

        def hosted(it, k):
            if it + 1 == ITEMS:
                return range(0, 0)
            n, u = len(pieces(it + 1)), CT * (items[it][1] + 1) - 1
            return range(min(n, -(-n * k // u)), min(n, -(-n * (k + 1) // u)))

        mps = ps[:, 6, :].bitcast(BF16)
        hps = ps[:, 7, :].bitcast(BF16)

        block = ctx.enter_context(nc.Block())

        @block.sync
        def _(sp):
            def load(dst, src, s):
                sp.dma_start(dst, src).then_inc(s, 16)

            def row(v):
                return v.rearrange("(a n) -> a n", a=1)

            xt = x[0].rearrange("(t p) d -> p t d", p=P)
            for t in range(CH):
                load(X[:, CT * t:CT * t + CT, :], xt[:, CT * t:CT * t + CT, :], x_loaded)
            load(ccol[:, 0:1], c0.rearrange("a d -> d a"), mod_loaded)
            load(ccol[:, 1:2], c1.rearrange("a d -> d a"), mod_loaded)
            load(wmod[:, 0, :], wmod0, mod_loaded)
            load(wmod[:, 1, :], wmod1, mod_loaded)
            for i, w in enumerate((WQ, WK, WV, WO)):
                load(wq[:, i, :], w, w_loaded)
            load(mixc[:, :], mix_kernel, w2_loaded)
            load(w1s[:, :, :], W1, w2_loaded)
            load(b1c[:, :], b1, w2_loaded)
            load(w2s[:, :, :], W2, w2_loaded)
            load(b2s[:, :], b2, w2_loaded)
            load(wo1[:, :], Wo1, w2_loaded)
            load(bo1c[:, :], bo1.rearrange("(n a) -> n a", a=1), w2_loaded)
            load(wo2[0:DM, :], Wo2, w2_loaded)
            load(wo2[DM:DM + 1, :], row(bo2), w2_loaded)
            load(gb_rows[:, 0, :], row(gamma).to_broadcast([P, D]), w2_loaded)
            load(gb_rows[:, 1, :], row(beta).to_broadcast([P, D]), w2_loaded)
            load(wqkv16[:, :, :], w_qkv_heads, w2_loaded)
            load(wvrow[:, :], w_v, w2_loaded)
            load(proj_s[:, :, :], proj, w2_loaded)
            sp.wait_ge(consts, 1)
            load(woutp[:, :, 0:HD], w_out.rearrange("o (h d) -> o h d", h=H1), w2_loaded)
            load(brow[:, :], row(b_out), w2_loaded)
            load(rw[:, :], router_w, w2_loaded)
            load(rb[:, :], row(router_b), w2_loaded)
            load(eb1c[:, :, :], eb1, w2_loaded)
            load(eb2r[:, :, :], eb2.rearrange("(a e) d -> a e d", a=1), w2_loaded)
            for t in range(CH):
                for k in range(2):
                    sp.wait_ge(qk_lo, 2 * t + k + 1)
                    load(qk_dram[k, :, :, CW * t:CW * t + CW].rearrange("a d s -> d a s"),
                         parts[:, :, k, t % 2, :], qk_stored[t % 2])
            for s in heads_free:
                sp.wait_ge(s, 1)
            for b in range(2):
                for j in range(HG):
                    load(KS[ROWS + 2 * j:ROWS + 2 * j + 2, b, j, :], onerow[:, :], heads_loaded[b])
            for s in qk_stored:
                sp.wait_ge(s, 16 * CH)
            with sp.Fori(0, GROUPS // 2) as i:
                for b in range(2):
                    sp.wait_ge(heads_free[b], i + 1)
                    src = qk_dram[:, :, bass.ds(2 * HG * DK * i + HG * DK * b, HG * DK), :]
                    kv = src[1].rearrange("a (j d) s -> a d j s", j=HG)
                    qv = src[0].rearrange("a (j d) s -> a d j s", j=HG)
                    n = 0
                    for rows in (3, 2, 1):
                        for r in range(rows):
                            at = DK * n
                            load(KS[at:at + DK, b, :, :], kv[r], heads_loaded[b])
                            load(QS[at:at + DK, b, :, :], qv[3 - rows], heads_loaded[b])
                            n += 1
            for s in heads_free:
                sp.wait_ge(s, GROUPS // 2 + 1)
            load(ew1s, ew1, ex_loaded)
            load(ew2s, ew2, ex_loaded)
            sp.wait_ge(zero_filled, 1)
            load(slot_in[0:TILES * P, :].rearrange("(t p) d -> p t d", p=P), zeros[:, :, :], zero_filled)
            load(slot_in[TILES * P:SLOTS, :].rearrange("(t p) d -> p t d", p=P),
                 zeros[:, 0:ST - TILES, :], zero_filled)
            sp.wait_ge(scattered, 16 * 2 * TILES)
            load(slotrows, slot_in.rearrange("(t p) d -> p t d", p=P), slots_loaded)
            for e in range(E):
                sp.wait_ge(eo_ready, e + 1)
                load(slot_out[CAP * e:CAP * e + 2 * P, :].rearrange("(t p) d -> p t d", p=P),
                     eo[:, e % 2, 0:2, :], eo_stored[e % 2])
                load(slot_out[CAP * e + 2 * P:CAP * e + CAP, :], eo[0:CAP - 2 * P, e % 2, 2, :], eo_stored[e % 2])
            for t in range(CH):
                sp.wait_ge(out_ready, t + 1)
                load(out[0].rearrange("(t p) d -> p t d", p=P)[:, CT * t:CT * t + CT, :],
                     X[:, CT * t:CT * t + CT, :], out_stored)
            sp.wait_ge(out_stored, 16 * CH)

        @block.gpsimd
        def _(pool):
            step = [0]

            def link(ins):
                step[0] += 1
                ins.then_inc(pchain, 1)
                pool.wait_ge(pchain, step[0])

            def pattern(t, base, pat, cm, op, fill):
                link(pool.affine_select(out=t, in_=t, compare_op=op, fill=fill, base=base, pattern=pat,
                                        channel_multiplier=cm))

            pool.memset(neghalf[:, :], -0.5).then_inc(pchain, 1)
            step[0] += 1
            link(pool.memset(identf[:, :], 0.0))
            pattern(identf[:, :], 0, [[-1, P]], 1, ALU.not_equal, 1.0)
            link(pool.memset(woutp[:, :, :], 0.0))
            link(pool.memset(onesf[:, :], 1.0))
            pool.memset(onesb[:, :], 1.0).then_inc(consts, 1)
            pool.wait_ge(consts, 1)

            def rstd_of(k):
                pool.wait_ge(ve_ready, k + 1)
                pool.tensor_tensor(rstd[:, k % 2, :], ve[:, k % 2, :], neghalf[:, :], ALU.pow).then_inc(rstd_ready, 1)
                pool.wait_ge(rstd_ready, k + 1)

            for t in range(CH):
                rstd_of(t)
            link(pool.memset(identb[:, :], 0.0))
            pattern(identb[:, :], 0, [[-1, P]], 1, ALU.not_equal, 1.0)
            link(pool.memset(causal[:, :], 0.0))
            pattern(causal[:, :], 0, [[-1, P]], 1, ALU.is_ge, MASKED)
            link(pool.memset(onerow[:, :], 1.0))
            for b in range(2):
                link(pool.memset(KS[:, b, :, :].rearrange("p h s -> p (h s)").bitcast(F32), 0.0))
                link(pool.memset(QS[:, b, :, :].rearrange("p h s -> p (h s)").bitcast(F32), 0.0))
            for b in range(2):
                link(pool.memset(Vg[:, b, :, :, :], 0.0))
                link(pool.memset(Vg[:, b, :, :, DK:DK + 1], 1.0))
            for b in range(2):
                pool.memset(hT[:, b, 0:S + 2:S + 1], 0.0).then_inc(heads_free[b], 1)
                pool.wait_ge(heads_free[b], 1)
            link(pool.memset(blockmask[:, :], 0.0))
            for j in range(P // BLK):
                link(pool.memset(blockmask[BLK * j:BLK * j + BLK, BLK * j:BLK * j + BLK], 1.0))
            link(pool.memset(upto[:, :], 1.0))
            pattern(upto[:, :], 0, [[1, P]], -1, ALU.is_ge, 0.0)
            link(pool.memset(spread[:, :, :], 0.0))
            pattern(spread[:, :, :], 0, [[-1, NP], [0, DM]], 1, ALU.not_equal, 1.0)
            for p in range(NP):
                link(pool.memset(rank9[:, :, p:p + 1], float(NP - p)))
            for e in range(E):
                link(pool.memset(rank8[:, :, e:e + 1], float(E - e)))
            link(pool.memset(hot9[:, :, :], 0.0))
            pool.wait_ge(qk_lo, 2 * CH)
            pool.memset(taug[DM:DM + 1, :], 1.0).then_inc(consts, 1)
            pool.wait_ge(consts, 2)

            pool.wait_ge(v_ready, CH)
            def copy_v(i, b):
                pool.wait_ge(heads_free[b], i + 1)
                at = HG * DK * (2 * i + b)
                pool.tensor_copy(Vg[:, b, :, :, 0:DK], vtok[:, :, at:at + HG * DK].rearrange(
                    "p t (h c) -> p t h c", h=HG)).then_inc(vg_ready, 1)
                pool.wait_ge(vg_ready, 2 * i + b + 1)

            copy_v(0, 0)
            copy_v(0, 1)
            for i in range(GROUPS // 2):
                for u, n in diag_no.items():
                    it, kb = units[u]
                    if i + 1 < GROUPS // 2 and n == DIAGS // 2:
                        copy_v(i + 1, 0)
                    off = P * (kb - CT * items[it][1])
                    pool.wait_ge(b_exped, HG * (UNITS * i + u + 1))
                    pm = pT[:, u % 3, :, off:off + P]
                    pool.affine_select(out=pm, in_=pm, compare_op=ALU.is_ge, fill=0.0, base=0,
                                       pattern=[[0, HG], [1, P]], channel_multiplier=-1).then_inc(diag_cut, 1)
                    pool.wait_ge(diag_cut, DIAGS * i + n + 1)
                if i + 1 < GROUPS // 2:
                    copy_v(i + 1, 1)
            for k in range(CH, 5 * CH):
                if k == 2 * CH:
                    pool.wait_ge(y_read, CH)
                    pool.memset(zeros[:, :, :], 0.0).then_inc(zero_filled, 1)
                    pool.wait_ge(zero_filled, 1)
                    pool.memset(vpad[:, :, :, :], 0.0).then_inc(consts, 1)
                    pool.wait_ge(consts, 3)
                rstd_of(k)
            pool.wait_ge(slots_ready, 1)
            pool.wait_ge(zero_filled, 33)
            pool.wait_ge(nrm_ready, 4 * CH)
            for t in range(TILES):
                for k in range(2):
                    pool.indirect_dma_start(
                        slot_in[:, :], bass.IndirectOffsetOnAxis(ap=slot_w[:, k, t:t + 1], axis=0),
                        nrm[:, t, :], None, bounds_check=SLOTS - 1, oob_is_err=False).then_inc(scattered, 16)
            for s in eo_stored:
                pool.wait_ge(s, 16 * E)
            for t in range(TILES):
                for k in range(2):
                    pool.indirect_dma_start(
                        gath[:, k, t, :], None, slot_out[:, :],
                        bass.IndirectOffsetOnAxis(ap=slot_r[:, k, t:t + 1], axis=0)).then_inc(gathered[t // CT], 16)

        @block.scalar
        def _(act):
            step = [0]

            def link(ins):
                step[0] += 1
                ins.then_inc(achain, 1)
                act.wait_ge(achain, step[0])

            act.wait_ge(mod_loaded, 16 * 4)
            act.activation(cexp[:, :], ccol[:, :], ACT.Exp, scale=-1.0).then_inc(c_exp, 1)

            def modulate(m, t, layer, which, bank):
                act.wait_ge(tposed, CH * m + t + 1)
                if m == 0 and t == 0:
                    act.wait_ge(mod_ready, 1)
                act.activation(hT[:, m % 2, 1 + CW * t:1 + CW * t + CW], ps[:, bank, :], ACT.Identity,
                               bias=modc[:, layer, 2 * which:2 * which + 1],
                               scale=modc[:, layer, 2 * which + 1:2 * which + 2]).then_inc(hT_ready, 1)

            for t in range(CH):
                modulate(0, t, 0, 0, t % 2)
                for k in range(2):
                    act.wait_ge(qk_mm, 2 * t + k + 1)
                    if t >= 2:
                        act.wait_ge(qk_stored[t % 2], 16 * 2 * (t // 2))
                    act.activation(parts[:, 0, k, t % 2, :], ps[:, 2 + k, :], ACT.Copy).then_inc(qk_hi, 1)
                    act.wait_ge(qk_rest, 2 * t + k + 1)
                    act.activation(parts[:, 1, k, t % 2, :], rest[:, k, :], ACT.Copy).then_inc(qk_mid, 1)
                act.wait_ge(v1_mm, t + 1)
                act.activation(vtok[:, CT * t:CT * t + CT, :], ps[:, 4, :].rearrange("p (t d) -> p t d", t=CT),
                               ACT.Copy).then_inc(v_ready, 1)

            for g in range(2 * H1 // 4):
                act.wait_ge(fold_mm, g + 1)
                act.activation(pfold[:, 4 * g:4 * g + 4, :], ps[:, g, :].rearrange("p (h f) -> p h f", h=4),
                               ACT.Copy).then_inc(fold_ready, 1)

            with act.Fori(0, GROUPS // 2) as i:
                for u, (it, kb) in enumerate(units):
                    off = P * max(0, kb - CT * items[it][1])
                    if u >= 3:
                        act.wait_ge(pv_done, UNITS * i + u - 2)
                    for j in range(HG):
                        n = HG * u + j
                        act.wait_ge(b_ready, HG * UNITS * i + n + 1)
                        act.activation(pT[:, u % 3, j, off:CW], ps[:, n % 3, off:CW], ACT.Exp, scale=SCALE)\
                           .then_inc(b_exped, 1)

            for t in range(CH):
                act.wait_ge(at_turned, t + 1)
                if t >= 2:
                    act.wait_ge(y_mm, t - 1)
                act.activation(cT[:, t % 2, :], ps[:, t % 2, :], ACT.Copy).then_inc(at_ready, 1)
                if t >= 1:
                    modulate(1, t - 1, 0, 1, 4 + (t - 1) % 2)
            modulate(1, CH - 1, 0, 1, 4 + (CH - 1) % 2)

            for t in range(CH):
                act.wait_ge(w2_loaded, 16 * 20)
                act.wait_ge(hT_ready, CH + t + 1)
                if t >= 2:
                    act.wait_ge(hid_mm, t - 1)
                act.activation(cT[:, t % 2, :], hT[:, 1, 1 + CW * t:1 + CW * t + CW], ACT.Copy,
                               scale=mixc[:, 1:2]).then_inc(conv_first, 1)
                act.wait_ge(u_mm, t + 1)
                act.wait_ge(sc_mm, t)
                act.activation(taug[0:DM, :], ps[0:DM, 7, :], ACT.Tanh, bias=bo1c[:, 0:1])\
                   .then_inc(t_ready, 1)
                act.wait_ge(hid_mm, t + 1)
                if t >= 1:
                    act.wait_ge(hsel_ready, t)
                for g in range(NG):
                    ins = act.activation(hid[:, g, :], ps[0:GR, g, :], ACT.Identity, bias=b1c[:, g:g + 1])
                    ins.then_inc(hid_ready, 1)

            for t in range(CH):
                modulate(2, t, 1, 0, 0)
                act.wait_ge(v1_mm, CH + t + 1)
                act.wait_ge(consts, 3)
                if t >= 1:
                    act.wait_ge(av_mm, H1 * t)
                act.activation(vpad[:, :, :, 0:HD], ps[:, 1, :].rearrange("p (t h d) -> p t h d", t=CT, h=H1),
                               ACT.Copy).then_inc(v1_ready, 1)
                for h in range(H1):
                    n = H1 * t + h
                    act.wait_ge(f_mm, n + 1)
                    if n >= 2:
                        act.wait_ge(f_ready, n - 1)
                    eq_ = expq[:, h % 2, :, :]
                    link(act.activation(eq_, ps[:, 2 + 2 * (h % 2):4 + 2 * (h % 2), :], ACT.Relu, scale=-1.0))
                    act.activation(eq_, eq_, ACT.Exp, scale=-1.0).then_inc(f_exp, 1)

            for t in range(CH):
                modulate(3, t, 1, 1, t % 2)
            act.wait_ge(r_shift, 1)
            act.activation(gates[:, :, :], lg[:, :, :], ACT.Exp).then_inc(r_exped, 1)
            for g in range(ST // 4):
                act.wait_ge(xs_turned, g + 1)
                act.activation(xsT[:, 4 * P * g:4 * P * g + 4 * P], ps[:, g % 2, :], ACT.Identity,
                               bias=modc[:, 1, 2:3], scale=modc[:, 1, 3:4]).then_inc(xs_ready, 1)
            for e in range(E):
                for c in range(HC):
                    act.wait_ge(e1_mm, HC * e + c + 1)
                    if e >= 2 and c == 0:
                        act.wait_ge(e2_mm, e - 1)
                    act.activation(gT[:, e % 2, c, :], ps[:, 2 + c, 0:CAP], ACT.Gelu, bias=eb1c[:, e, c:c + 1])\
                       .then_inc(gelu_ready, 1)

        @block.vector
        def _(dve):
            step = [0]

            def link(ins):
                step[0] += 1
                ins.then_inc(dchain, 1)
                dve.wait_ge(dchain, step[0])

            def stats_of(k, rows):
                for i in range(CT):
                    ins = dve.bn_stats(stats[:, i, :], rows(i))
                    step[0] += 1
                    ins.then_inc(dchain, 1)
                dve.wait_ge(dchain, step[0])
                for i in range(CT):
                    ins = dve.bn_aggr(mv[:, k % 2, i, :], stats[:, i, :])
                    step[0] += 1
                    ins.then_inc(dchain, 1)
                dve.wait_ge(dchain, step[0])
                dve.tensor_scalar(ve[:, k % 2, :], mv[:, k % 2, :, 1], EPS, None, ALU.add).then_inc(ve_ready, 1)

            def normalise(k, t, rows, dst, done):
                dve.wait_ge(rstd_ready, k + 1)
                for i in range(CT):
                    ins = dve.tensor_scalar(dst(i), rows(i), mv[:, k % 2, i, 0:1],
                                            rstd[:, k % 2, i:i + 1], ALU.subtract, ALU.mult)
                    if done is None:
                        step[0] += 1
                        ins.then_inc(dchain, 1)
                if done is None:
                    dve.wait_ge(dchain, step[0])
                else:
                    ins.then_inc(done, 1)

            def x_row(t):
                return lambda i: X[:, CT * t + i, :]

            def nrm_row(t):
                return lambda i: nrm[:, CT * t + i, :]

            dve.wait_ge(c_exp, 1)
            link(dve.tensor_scalar(cden[:, :], cexp[:, :], 1.0, None, ALU.add))
            link(dve.reciprocal(crec[:, :], cden[:, :]))
            link(dve.tensor_tensor(scol[:, :], ccol[:, :], crec[:, :], ALU.mult))
            dve.wait_ge(consts, 1)
            for l in range(2):
                ins = dve.tensor_scalar(smat[:, l, :], onesf[:, :], scol[:, l:l + 1], None, ALU.mult)
                ins.then_inc(silu_ready, 1)
            dve.wait_ge(x_loaded, 16 * CH)
            stats_of(0, x_row(0))
            dve.wait_ge(mod_mm, 1)
            cols = ps[:, 7, 0:8].rearrange("p (l c) -> p l c", l=2)
            link(dve.tensor_copy(modc[:, :, :], cols))
            dve.tensor_scalar(modc[:, :, 1:4:2], cols[:, :, 1:4:2], 1.0, None, ALU.add).then_inc(mod_ready, 1)
            g4 = ps[:, 6, :].rearrange("p (g d) -> p g d", g=4)
            link(dve.tensor_scalar(gneg[:, :, :], g4, -1.0, 0.25, ALU.mult, ALU.max))
            link(dve.tensor_tensor(gabs[:, :, :], g4, gneg[:, :, :], ALU.max))
            link(dve.tensor_scalar(gsgn[:, :, :], g4, 0.0, 2.0, ALU.is_ge, ALU.mult))
            link(dve.scalar_tensor_tensor(gate[:, :, :], gsgn[:, :, :], -1.0, gabs[:, :, :], ALU.add, ALU.mult))
            dve.wait_ge(w_loaded, 16 * 4)

            def split(t):
                for k in range(2):
                    dve.wait_ge(qk_hi, 2 * t + k + 1)
                    if t >= 1:
                        dve.wait_ge(qk_lo, 2 * t + k - 1)
                    dve.tensor_tensor(rest[:, k, :], ps[:, 2 + k, :], parts[:, 0, k, t % 2, :], ALU.subtract)\
                       .then_inc(qk_rest, 1)
                    dve.wait_ge(qk_mid, 2 * t + k + 1)
                    dve.tensor_tensor(parts[:, 2, k, t % 2, :], rest[:, k, :], parts[:, 1, k, t % 2, :],
                                      ALU.subtract).then_inc(qk_lo, 1)

            normalise(0, 0, x_row(0), nrm_row(0), nrm_ready)
            stats_of(1, x_row(1))
            for t in range(CH):
                if t + 1 < CH:
                    normalise(t + 1, t + 1, x_row(t + 1), nrm_row(t + 1), nrm_ready)
                if t + 2 < CH:
                    stats_of(t + 2, x_row(t + 2))
                split(t)

            dve.wait_ge(w2_loaded, 16 * 20)
            dve.wait_ge(fold_mm, 2 * H1 // 4 + 1)
            dve.tensor_tensor(wog[:, :], wq[:, 3, :], gate[:, 0, :], ALU.mult).then_inc(fold_ready, 1)
            dve.tensor_copy(wvT[:, :], ps[:, 4, 0:P]).then_inc(fold_ready, 1)
            for g in range(2):
                dve.tensor_tensor(woutT[:, g, :], ps[:, 4, P + P * g:2 * P + P * g], gate[:, 2, :], ALU.mult)\
                   .then_inc(fold_ready, 1)
                dve.tensor_tensor(gbg[:, g, :], gb_rows[:, g, :], gate[:, 1, :], ALU.mult).then_inc(fold_ready, 1)
            dve.tensor_tensor(browg[:, :], brow[:, :], gate[0:1, 2, :], ALU.mult).then_inc(fold_ready, 1)

            with dve.Fori(0, GROUPS // 2) as i:
                def maxima(it, numbers):
                    for n in numbers:
                        g, c, qi, j, kc = pieces(it)[n]
                        a = a_start[it] + n
                        w = CW if kc < c else P * (qi + 1)
                        dve.wait_ge(a_ready, A_TOTAL * i + a + 1)
                        dve.tensor_reduce(tmax[:, it % 2, HG * qi + j, kc:kc + 1], ps[:, 3 + a % 3, 0:w],
                                          AX.X, ALU.max).then_inc(a_maxed, 1)

                def subtract_rows(it):
                    g, c = items[it]
                    dve.wait_ge(a_maxed, A_TOTAL * i + a_start[it + 1])
                    dve.tensor_reduce(negm[:, :], tmax[:, it % 2, :, 0:c + 1], AX.X, ALU.max, negate=True)\
                       .then_inc(m_neg, 1)
                    dve.wait_ge(m_neg, 2 * ITEMS * i + 2 * it + 1)
                    nm = negm[:, :].rearrange("p (t h) -> p t h", h=HG)
                    dve.tensor_copy(mhl[:, :, :, 0], nm).then_inc(m_neg, 1)
                    dve.wait_ge(m_neg, 2 * ITEMS * i + 2 * it + 2)
                    dve.tensor_tensor(mhl[:, :, :, 1], nm, mhl[:, :, :, 0], ALU.subtract).then_inc(m_parts, 1)
                    dve.wait_ge(m_turned, ITEMS * i + it + 1)
                    dve.tensor_copy(QS[ROWS:ROWS + 2 * HG, g, :, CW * c:CW * c + CW],
                                    mps[ROWS:ROWS + 2 * HG, 0:CW].unsqueeze(1).to_broadcast([2 * HG, HG, CW]))\
                       .then_inc(m_rows, 1)

                def copy_item(it):
                    dve.wait_ge(pv_done, UNITS * i + last_unit[it] + 1)
                    dve.tensor_copy(oT[:, it % 2, :], ps[:, 7, :]).then_inc(o_copied, 1)

                def finish_item(it):
                    g, c = items[it]
                    dve.wait_ge(o_turned, ITEMS * i + it + 1)
                    o4 = ps[:, 6, :].rearrange("p (t h c) -> p t h c", t=CT, h=HG)
                    if it > 0:
                        dve.wait_ge(o_normed, ITEMS * i + it)
                    dve.reciprocal(rden[:, :, :], o4[:, :, :, DK]).then_inc(o_rden, 1)
                    dve.wait_ge(o_rden, ITEMS * i + it + 1)
                    dve.tensor_tensor(
                        attn[:, CT * c:CT * c + CT,
                             bass.ds(2 * HG * DK * i + HG * DK * g, HG * DK)].rearrange("p t (h c) -> p t h c", h=HG),
                        o4[:, :, :, 0:DK], rden[:, :, :].unsqueeze(3).to_broadcast([P, CT, HG, DK]), ALU.mult)\
                       .then_inc(o_normed, 1)

                maxima(0, range(len(pieces(0))))
                subtract_rows(0)
                for it in range(ITEMS):
                    for k in range(CT * (items[it][1] + 1)):
                        if k == 2 and it > 0:
                            finish_item(it - 1)
                        maxima(it + 1, hosted(it, k))
                    if it + 1 < ITEMS:
                        subtract_rows(it + 1)
                    copy_item(it)
                finish_item(ITEMS - 1)

            for t in range(CH):
                dve.wait_ge(y_mm, t + 1)
                xc = X[:, CT * t:CT * t + CT, :]
                dve.tensor_tensor(xc, ps[:, 2 + t % 2, :].rearrange("p (t d) -> p t d", t=CT), xc, ALU.add)\
                   .then_inc(y_read, 1)
                dve.wait_ge(y_read, t + 1)
                stats_of(CH + t, x_row(t))
                if t >= 1:
                    normalise(CH + t - 1, t - 1, x_row(t - 1), nrm_row(t - 1), nrm_ready)
            normalise(2 * CH - 1, CH - 1, x_row(CH - 1), nrm_row(CH - 1), nrm_ready)

            for t in range(CH):
                dve.wait_ge(conv_first, t + 1)
                dve.wait_ge(hT_ready, CH + min(t + 2, CH))
                xm = cT[:, t % 2, :]
                link(dve.scalar_tensor_tensor(xm, hT[:, 1, CW * t:CW * t + CW], mixc[:, 0:1], xm, ALU.mult, ALU.add))
                dve.scalar_tensor_tensor(xm, hT[:, 1, CW * t + 2:CW * t + 2 + CW], mixc[:, 2:3], xm,
                                         ALU.mult, ALU.add).then_inc(conv_ready, 1)
                dve.wait_ge(sc_mm, t + 1)
                s9 = ps[:, 7, 0:CT * NP].rearrange("p (t k) -> p t k", t=CT)
                wide = [P, CT, NP]
                link(dve.tensor_reduce(top9[:, :], s9, AX.X, ALU.max))
                link(dve.tensor_tensor(eq9[:, :, :], s9, top9[:, :].unsqueeze(2).to_broadcast(wide), ALU.is_equal))
                link(dve.tensor_tensor(eq9[:, :, :], eq9[:, :, :], rank9[:, :, :], ALU.mult))
                link(dve.tensor_reduce(best9[:, :], eq9[:, :, :], AX.X, ALU.max))
                dve.tensor_tensor(hot9[:, :, 0:NP], eq9[:, :, :], best9[:, :].unsqueeze(2).to_broadcast(wide),
                                  ALU.is_equal).then_inc(hot_ready, 1)
                dve.wait_ge(hot_turned, t + 1)
                dve.tensor_copy(hotT[:, :], hps[0:NP, CW:2 * CW]).then_inc(hot_copied, 1)
                dve.tensor_copy(hotTf[:, :], hps[0:NP, CW:2 * CW]).then_inc(hot_copied, 1)
                dve.wait_ge(mask_mm, t + 1)
                dve.wait_ge(hid_ready, NG * (t + 1))
                for g in range(NG):
                    ins = dve.tensor_tensor(hsel[:, g, :], hid[:, g, :], ps[0:GR, 3 + g, :], ALU.mult)
                ins.then_inc(hsel_ready, 1)
                dve.wait_ge(ffn_mm, t + 1)

                def f_row(i):
                    return ps[:, 6, P * i:P * i + P]

                stats_of(2 * CH + 2 * t, f_row)
                normalise(2 * CH + 2 * t, t, f_row, lambda i: tmp[:, i, :], None)
                four = [P, CT, D]
                link(dve.tensor_tensor(tmp, tmp, gbg[:, 0:1, :].to_broadcast(four), ALU.mult))
                link(dve.tensor_tensor(tmp, tmp, gbg[:, 1:2, :].to_broadcast(four), ALU.add))
                xc = X[:, CT * t:CT * t + CT, :]
                dve.tensor_tensor(xc, xc, tmp, ALU.add).then_inc(ffn_read, 1)
                dve.wait_ge(ffn_read, t + 1)
                stats_of(2 * CH + 2 * t + 1, x_row(t))
                normalise(2 * CH + 2 * t + 1, t, x_row(t), nrm_row(t), nrm_ready)

            for t in range(CH):
                for h in range(H1 + 1):
                    if h < H1:
                        n = H1 * t + h
                        dve.wait_ge(f_exp, n + 1)
                        eq_ = expq[:, h % 2, :, :]
                        if n >= 2:
                            dve.wait_ge(s_mm, n - 1)
                        dve.scalar_tensor_tensor(feat[:, h % 2, :, :], ps[:, 2 + 2 * (h % 2):4 + 2 * (h % 2), :],
                                                 1.0, eq_, ALU.add, ALU.max).then_inc(f_ready, 1)
                    if h >= 1:
                        n = H1 * t + h - 1
                        dve.wait_ge(s_mm, n + 1)
                        if n >= 2:
                            dve.wait_ge(av_mm, n - 1)
                        dve.tensor_tensor(
                            am[:, n % 2, :].rearrange("p (t q) -> p t q", t=CT),
                            ps[:, 6, :].rearrange("p (t q) -> p t q", t=CT),
                            blockmask[:, :].unsqueeze(1).to_broadcast([P, CT, P]), ALU.mult).then_inc(s_ready, 1)
                    if h in (4, 8):
                        dve.wait_ge(av_mm, H1 * t + h)
                        link(dve.tensor_scalar(recd, ps[:, 1, :], 1e-8, None, ALU.add))
                        link(dve.reciprocal(recd, recd))
                        if t >= 1:
                            dve.wait_ge(y1_mm, t)
                        dve.tensor_tensor(onT[:, h // 4 - 1, :], ps[:, 7, :], recd, ALU.mult).then_inc(on_ready, 1)
                dve.wait_ge(y1_mm, t + 1)
                xc = X[:, CT * t:CT * t + CT, :]
                dve.tensor_tensor(xc, ps[:, 0, :].rearrange("p (t d) -> p t d", t=CT), xc, ALU.add)\
                   .then_inc(y1_read, 1)
                dve.wait_ge(y1_read, t + 1)
                stats_of(4 * CH + t, x_row(t))
                normalise(4 * CH + t, t, x_row(t), nrm_row(t), nrm_ready)

            dve.wait_ge(lg_mm, TILES)
            logits = ps[:, 2, 0:TILES * E].rearrange("p (t e) -> p t e", t=TILES)
            wide = [P, TILES, E]

            def over(r):
                return red[:, r, :].unsqueeze(2).to_broadcast(wide)

            link(dve.tensor_reduce(red[:, 0, :], logits, AX.X, ALU.max))
            dve.tensor_tensor(lg[:, :, :], logits, over(0), ALU.subtract).then_inc(r_shift, 1)
            dve.wait_ge(r_exped, 1)
            link(dve.tensor_reduce(red[:, 1, :], gates[:, :, :], AX.X, ALU.add))
            link(dve.reciprocal(red[:, 2, :], red[:, 1, :]))
            link(dve.tensor_tensor(gates[:, :, :], gates[:, :, :], over(2), ALU.mult))
            src = gates[:, :, :]
            for k in range(2):
                link(dve.tensor_reduce(wsel[:, k, :], src, AX.X, ALU.max))
                link(dve.tensor_tensor(sel[:, k, :, :], src, wsel[:, k, :].unsqueeze(2).to_broadcast(wide),
                                       ALU.is_equal))
                link(dve.tensor_tensor(sel[:, k, :, :], sel[:, k, :, :], rank8[:, :, :], ALU.mult))
                link(dve.tensor_reduce(red[:, 3 + k, :], sel[:, k, :, :], AX.X, ALU.max))
                link(dve.tensor_tensor(hot[:, k, :, :], sel[:, k, :, :], over(3 + k), ALU.is_equal))
                if k == 0:
                    link(dve.scalar_tensor_tensor(lg[:, :, :], hot[:, 0, :, :], -2.0, src, ALU.mult, ALU.add))
                    src = lg[:, :, :]
            dve.tensor_tensor(chosen[:, :, :], hot[:, 0, :, :], hot[:, 1, :, :], ALU.add).then_inc(r_mask, 1)
            dve.wait_ge(pos_mm, 1)
            place = ps[:, 3, 0:TILES * E].rearrange("p (t e) -> p t e", t=TILES)
            for k in range(2):
                link(dve.tensor_tensor(sel[:, k, :, :], hot[:, k, :, :], place, ALU.mult))
                link(dve.tensor_reduce(red[:, 5, :], sel[:, k, :, :], AX.X, ALU.add))
                link(dve.tensor_scalar(red[:, 6, :], red[:, 3 + k, :], float(-CAP), float(E * CAP - 1),
                                       ALU.mult, ALU.add))
                link(dve.tensor_scalar(red[:, 7, :], red[:, 5, :], float(CAP), None, ALU.is_le))
                link(dve.tensor_tensor(wsel[:, k, :], wsel[:, k, :], red[:, 7, :], ALU.mult))
                link(dve.tensor_scalar(red[:, 8, :], red[:, 5, :], float(CAP), None, ALU.min))
                link(dve.tensor_tensor(slotf[:, k, :], red[:, 6, :], red[:, 8, :], ALU.add))
                link(dve.tensor_copy(slot_r[:, k, :], slotf[:, k, :]))
                link(dve.tensor_scalar(red[:, 9, :], red[:, 7, :], float(-SLOTS), float(SLOTS), ALU.mult, ALU.add))
                link(dve.tensor_tensor(slotf[:, k, :], slotf[:, k, :], red[:, 9, :], ALU.add))
                link(dve.tensor_copy(slot_w[:, k, :], slotf[:, k, :]))
            dve.tensor_copy(red[:, 10, :], red[:, 9, :]).then_inc(slots_ready, 1)

            for e in range(E):
                dve.wait_ge(e2_mm, e + 1)
                if e >= 2:
                    dve.wait_ge(eo_stored[e % 2], 32 * (e // 2))
                link(dve.tensor_copy(eo[:, e % 2, 0:2, :], ps[:, 6 + e % 2, 0:2 * P].rearrange(
                    "p (s d) -> p s d", s=2)))
                dve.tensor_copy(eo[0:CAP - 2 * P, e % 2, 2, :], ps[0:CAP - 2 * P, 6 + e % 2, 2 * P:3 * P])\
                   .then_inc(eo_ready, 1)
            for t in range(CH):
                dve.wait_ge(gathered[t], 16 * 2 * CT)
                for i in range(CT * t, CT * t + CT):
                    link(dve.tensor_scalar(gath[:, 0, i, :], gath[:, 0, i, :], wsel[:, 0, i:i + 1], None, ALU.mult))
                    link(dve.scalar_tensor_tensor(gath[:, 0, i, :], gath[:, 1, i, :], wsel[:, 1, i:i + 1],
                                                  gath[:, 0, i, :], ALU.mult, ALU.add))
                gc = gath[:, 0, CT * t:CT * t + CT, :]
                link(dve.tensor_tensor(gc, gc, gate[:, 3:4, :].to_broadcast([P, CT, D]), ALU.mult))
                xc = X[:, CT * t:CT * t + CT, :]
                dve.tensor_tensor(xc, xc, gc, ALU.add).then_inc(out_ready, 1)

        @block.tensor
        def _(pe):
            def mm(o, lhsT, rhs, start=True, stop=True):
                return pe.matmul(o, lhsT, rhs, start=start, stop=stop, skip_group_check=True)

            pe.wait_ge(silu_ready, 2)
            for l in range(2):
                for n, which in enumerate((0, 1, 3, 4)):
                    mm(ps[:, 7, 4 * l + n:4 * l + n + 1], wmod[:, l, D * which:D * which + D], scol[:, l:l + 1])
                for n, which in enumerate((2, 5)):
                    ins = mm(ps[:, 6, D * (2 * l + n):D * (2 * l + n) + D], smat[:, l, :],
                             wmod[:, l, D * which:D * which + D])
            ins.then_inc(mod_mm, 1)

            def turn(m, t, bank):
                pe.wait_ge(nrm_ready, CH * m + t + 1)
                for i in range(CT):
                    ins = pe.transpose(ps[:, bank, P * i:P * i + P], nrm[:, CT * t + i, :], identf[:, :])
                ins.then_inc(tposed, 1)

            pe.wait_ge(consts, 1)
            turn(0, 0, 0)
            pe.wait_ge(w_loaded, 16 * 4)
            for t in range(CH):
                if t + 1 < CH:
                    if t >= 1:
                        pe.wait_ge(hT_ready, t)
                    turn(0, t + 1, (t + 1) % 2)
                pe.wait_ge(hT_ready, t + 1)
                rows = hT[:, 0, 1 + CW * t:1 + CW * t + CW]
                for k in range(2):
                    if t >= 1:
                        pe.wait_ge(qk_rest, 2 * t + k - 1)
                    mm(ps[:, 2 + k, :], wq[:, k, :], rows).then_inc(qk_mm, 1)
                if t >= 1:
                    pe.wait_ge(v_ready, t)
                for i in range(CT):
                    ins = mm(ps[:, 4, P * i:P * i + P], rows[:, P * i:P * i + P], wq[:, 2, :])
                ins.then_inc(v1_mm, 1)

            pe.wait_ge(w2_loaded, 16 * 20)
            pe.wait_ge(qk_rest, 2 * CH)
            pe.wait_ge(v_ready, CH)
            for g in range(2 * H1 // 4):
                for n in range(4 * g, 4 * g + 4):
                    ins = mm(ps[:, g, P * (n % 4):P * (n % 4) + P], wqkv16[:, n, :], proj_s[:, n % H1, :])
                ins.then_inc(fold_mm, 1)
            pe.transpose(ps[:, 4, 0:P], wvrow[:, :], identf[:, :])
            for g in range(2):
                ins = pe.transpose(ps[:, 4, P + P * g:2 * P + P * g],
                                   woutp[:, 4 * g:4 * g + 4, :].rearrange("p h c -> p (h c)"), identf[:, :])
            ins.then_inc(fold_mm, 1)
            pe.wait_ge(fold_ready, 11)

            pieces_reg = nc.alloc_register(pe.engine, "pieces_before")
            heads_reg = nc.alloc_register(pe.engine, "heads_before")
            with pe.Fori(0, GROUPS // 2) as i:
                pe.reg_mov(pieces_reg, A_TOTAL * i)
                pe.reg_mov(heads_reg, HG * UNITS * i)
                pieces_before = pe.snap(pieces_reg, min_val=0, max_val=A_TOTAL)
                heads_before = pe.snap(heads_reg, min_val=0, max_val=HG * UNITS)

                def score_piece(it, n):
                    g, c, qi, j, kc = pieces(it)[n]
                    a = a_start[it] + n
                    w = CW if kc < c else P * (qi + 1)
                    if a >= 3:
                        pe.wait_ge(a_maxed, pieces_before + a - 2)
                    o = ps[:, 3 + a % 3, 0:w]
                    ins = mm(o, QS[0:ROWS, g, j, P * (CT * c + qi):P * (CT * c + qi) + P],
                             KS[0:ROWS, g, j, CW * kc:CW * kc + w], True, kc < c)
                    if kc == c:
                        ins = mm(o[:, w - P:w], identb[:, :], causal[:, :], False, True)
                    ins.then_inc(a_ready, 1)

                def turn_maxima(it):
                    pe.wait_ge(m_parts, ITEMS * i + it + 1)
                    if it >= 2:
                        pe.wait_ge(o_normed, ITEMS * i + it - 1)
                    for qi in range(CT):
                        ins = pe.transpose(mps[ROWS:ROWS + 2 * HG, P * qi:P * qi + P],
                                           mhl[:, qi, :, :].rearrange("p h c -> p (h c)"), identb[:, :])
                    ins.then_inc(m_turned, 1)

                def scores(u, j):
                    it, kb = units[u]
                    g, c = items[it]
                    off = P * max(0, kb - CT * c)
                    n = HG * u + j
                    if n >= 3:
                        pe.wait_ge(b_exped, heads_before + n - 2)
                    mm(ps[:, n % 3, off:CW], KS[0:ROWS + 2 * HG, g, j, P * kb:P * kb + P],
                       QS[0:ROWS + 2 * HG, g, j, CW * c + off:CW * c + CW]).then_inc(b_ready, 1)

                def values(u, j):
                    it, kb = units[u]
                    g, c = items[it]
                    off = P * max(0, kb - CT * c)
                    if u == last_unit[it]:
                        pe.wait_ge(b_exped, heads_before + HG * u + j + 1)
                    if j == 0:
                        if u in diag_no:
                            pe.wait_ge(diag_cut, DIAGS * i + diag_no[u] + 1)
                        if kb == 0 and it > 0:
                            pe.wait_ge(o_copied, ITEMS * i + it)
                    ins = mm(ps[32 * j:32 * j + 32, 7, off:CW], Vg[:, g, kb, j, :], pT[:, u % 3, j, off:CW],
                             kb == 0, kb == CT * c + CT - 1)
                    if j == HG - 1:
                        ins.then_inc(pv_done, 1)

                def turn_item(it):
                    pe.wait_ge(o_copied, ITEMS * i + it + 1)
                    pe.wait_ge(m_rows, ITEMS * i + min(it + 2, ITEMS))
                    for q in range(CT):
                        ins = pe.transpose(ps[:, 6, P * q:P * q + P], oT[:, it % 2, P * q:P * q + P], identf[:, :])
                        if q == 0 and it == CH - 1:
                            ins.then_inc(heads_free[0], 1)
                    ins.then_inc(o_turned, 1)

                for b in range(2):
                    pe.wait_ge(heads_loaded[b], 16 * 12 * i + 16 * (HG + 12))
                    pe.wait_ge(vg_ready, 2 * i + b + 1)
                    if b == 0:
                        for n in range(len(pieces(0))):
                            score_piece(0, n)
                        turn_maxima(0)
                    for it in range(CH * b, CH * b + CH):
                        if b == 0 and it == CH - 1:
                            pe.wait_ge(heads_loaded[1], 16 * 12 * i + 16 * (HG + 12))
                        first = units.index((it, 0))
                        nu = CT * (items[it][1] + 1)
                        pe.wait_ge(m_rows, ITEMS * i + it + 1)
                        for k in range(nu):
                            if k == 2 and it > 0:
                                turn_item(it - 1)
                            steps = [(scores, first + k, j) for j in range(HG)]
                            if k >= 1:
                                steps += [(values, first + k - 1, j) for j in range(HG)]
                            hs = hosted(it, k)
                            for n, (what, u, j) in enumerate(steps):
                                what(u, j)
                                for h in hs[len(hs) * n // len(steps):len(hs) * (n + 1) // len(steps)]:
                                    score_piece(it + 1, h)
                        if it + 1 < ITEMS:
                            turn_maxima(it + 1)
                        for j in range(HG):
                            values(first + nu - 1, j)
                turn_item(ITEMS - 1)
                pe.wait_ge(o_normed, ITEMS * i + ITEMS)
                pe.transpose(mps[0:2 * HG, 0:P], mhl[:, 0, :, :].rearrange("p h c -> p (h c)"), identb[:, :])\
                  .then_inc(heads_free[1], 1)

            def turn_attn(t):
                for i in range(CT):
                    ins = pe.transpose(ps[:, t % 2, P * i:P * i + P], attn[:, CT * t + i, :], identf[:, :])
                ins.then_inc(at_turned, 1)

            pe.wait_ge(o_normed, ITEMS * (GROUPS // 2))
            turn_attn(0)
            for t in range(CH):
                if t + 1 < CH:
                    if t >= 1:
                        pe.wait_ge(at_ready, t)
                    turn_attn(t + 1)
                pe.wait_ge(at_ready, t + 1)
                if t >= 2:
                    pe.wait_ge(y_read, t - 1)
                for i in range(CT):
                    ins = mm(ps[:, 2 + t % 2, P * i:P * i + P], cT[:, t % 2, P * i:P * i + P], wog[:, :])
                ins.then_inc(y_mm, 1)
                if t >= 1:
                    if t >= 3:
                        pe.wait_ge(hT_ready, CH + t - 2)
                    turn(1, t - 1, 4 + (t - 1) % 2)
            pe.wait_ge(hT_ready, CH + 2)
            turn(1, CH - 1, 4 + (CH - 1) % 2)

            pe.wait_ge(consts, 2)
            for t in range(CH):
                xm = cT[:, t % 2, :]
                pe.wait_ge(conv_ready, t + 1)
                if t == 0:
                    pe.wait_ge(hT_ready, 2 * CH)
                if t >= 1:
                    pe.wait_ge(hot_copied, 2 * t)
                mm(ps[0:DM, 7, :], wo1[:, :], xm).then_inc(u_mm, 1)
                if t >= 1:
                    pe.wait_ge(hid_ready, NG * t)
                for g in range(NG):
                    ins = mm(ps[0:GR, g, :], w1s[:, PG * g:PG * g + PG, :].rearrange("p a m -> p (a m)"), xm)
                ins.then_inc(hid_mm, 1)
                pe.wait_ge(t_ready, t + 1)
                for i in range(CT):
                    ins = mm(ps[:, 7, NP * i:NP * i + NP], taug[:, P * i:P * i + P], wo2[:, :])
                ins.then_inc(sc_mm, 1)
                pe.wait_ge(hot_ready, t + 1)
                for i in range(CT):
                    ins = pe.transpose(hps[0:16, CW + P * i:CW + P * i + P], hot9[:, i, :], identb[:, :])
                ins.then_inc(hot_turned, 1)
                pe.wait_ge(hot_copied, 2 * t + 2)
                if t >= 1:
                    pe.wait_ge(hsel_ready, t)
                for g in range(NG):
                    ins = mm(ps[0:GR, 3 + g, :], spread[:, PG * g:PG * g + PG, :].rearrange("p a m -> p (a m)"),
                             hotT[:, :])
                ins.then_inc(mask_mm, 1)
                pe.wait_ge(hsel_ready, t + 1)
                if t >= 1:
                    pe.wait_ge(ffn_read, t)
                for i in range(CT):
                    o = ps[:, 6, P * i:P * i + P]
                    s_ = slice(P * i, P * i + P)
                    mm(o, hT[:, 1, 1 + CW * t + P * i:1 + CW * t + P * i + P], identf[:, :], True, False)
                    mm(o, hotTf[:, s_], b2s[:, :], False, False)
                    for g in range(NG):
                        ins = mm(o, hsel[:, g, s_], w2s[:, g, :], False, g == NG - 1)
                ins.then_inc(ffn_mm, 1)

            for t in range(CH):
                if t >= 1:
                    pe.wait_ge(y1_read, t)
                else:
                    pe.wait_ge(ffn_read, CH)
                turn(2, t, 0)
                pe.wait_ge(hT_ready, 2 * CH + t + 1)
                rows = hT[:, 0, 1 + CW * t:1 + CW * t + CW]
                if t >= 1:
                    pe.wait_ge(on_ready, 2 * t)
                for i in range(CT):
                    ins = mm(ps[:, 1, P * i:P * i + P], rows[:, P * i:P * i + P], wvT[:, :])
                ins.then_inc(v1_mm, 1)

                def features(h):
                    n = H1 * t + h
                    if n >= 2:
                        pe.wait_ge(f_ready, n - 1)
                    for k in range(2):
                        ins = mm(ps[:, 2 + 2 * (h % 2) + k, :], pfold[:, H1 * k + h, :], rows)
                    ins.then_inc(f_mm, 1)

                def block_scores(h):
                    n = H1 * t + h
                    pe.wait_ge(f_ready, n + 1)
                    if n >= 1:
                        pe.wait_ge(s_ready, n)
                    for i in range(CT):
                        s_ = slice(P * i, P * i + P)
                        ins = mm(ps[:, 6, s_], feat[:, h % 2, 1, s_], feat[:, h % 2, 0, s_])
                    ins.then_inc(s_mm, 1)

                def block_values(h):
                    n = H1 * t + h
                    pe.wait_ge(s_ready, n + 1)
                    j = h % 4
                    if h == 0:
                        pe.wait_ge(v1_ready, t + 1)
                        if t >= 1:
                            pe.wait_ge(on_ready, 2 * t)
                    if h == 4:
                        pe.wait_ge(on_ready, 2 * t + 1)
                    for i in range(CT):
                        s_ = slice(P * i, P * i + P)
                        mm(ps[32 * j:32 * j + 32, 7, s_], vpad[:, i, h, :], am[:, h % 2, s_])
                        ins = mm(ps[32 * j:32 * j + 32, 1, s_], onesf[:, 0:32], am[:, h % 2, s_])
                    ins.then_inc(av_mm, 1)

                features(0)
                for h in range(H1):
                    if h + 1 < H1:
                        features(h + 1)
                    block_scores(h)
                    if h >= 1:
                        block_values(h - 1)
                block_values(H1 - 1)
                pe.wait_ge(on_ready, 2 * t + 2)
                for i in range(CT):
                    o = ps[:, 0, P * i:P * i + P]
                    for g in range(2):
                        mm(o, onT[:, g, P * i:P * i + P], woutT[:, g, :], g == 0, False)
                    ins = mm(o, onesf[0:1, :], browg[:, :], False, True)
                ins.then_inc(y1_mm, 1)

            pe.wait_ge(y1_read, CH)
            for t in range(CH):
                if t >= 2:
                    pe.wait_ge(hT_ready, 3 * CH + t - 1)
                turn(3, t, t % 2)
                pe.wait_ge(hT_ready, 3 * CH + t + 1)
                for i in range(CT):
                    n = CT * t + i
                    o = ps[:, 2, E * n:E * n + E]
                    mm(o, hT[:, 1, 1 + P * n:1 + P * n + P], rw[:, :], True, False)
                    mm(o, onesf[0:1, :], rb[:, :], False, True).then_inc(lg_mm, 1)
            pe.wait_ge(r_mask, 1)
            ch = chosen[:, :, :].rearrange("p t e -> p (t e)")
            mm(ps[:, 3, 0:TILES * E], upto[:, :], ch, True, False)
            for s_ in range(1, TILES):
                ins = mm(ps[:, 3, E * s_:TILES * E], onesb[:, :], ch[:, 0:E * (TILES - s_)], False, s_ == TILES - 1)
            ins.then_inc(pos_mm, 1)
            pe.wait_ge(slots_loaded, 16)
            for g in range(ST // 4):
                if g >= 2:
                    pe.wait_ge(xs_ready, g - 1)
                for i in range(4):
                    ins = pe.transpose(ps[:, g % 2, P * i:P * i + P], slotrows[:, 4 * g + i, :], identf[:, :])
                ins.then_inc(xs_turned, 1)
            pe.wait_ge(ex_loaded, 32)

            def expert_up(e):
                pe.wait_ge(xs_ready, min(ST // 4, -(-CAP * (e + 1) // (4 * P))))
                for c in range(HC):
                    if e >= 1:
                        pe.wait_ge(gelu_ready, HC * (e - 1) + c + 1)
                    mm(ps[:, 2 + c, 0:CAP], ew1s[:, e, P * c:P * c + P], xsT[:, CAP * e:CAP * e + CAP])\
                        .then_inc(e1_mm, 1)

            def expert_down(e):
                pe.wait_ge(gelu_ready, HC * (e + 1))
                if e >= 2:
                    pe.wait_ge(eo_ready, e - 1)
                for s_ in range(3):
                    m = min(P, CAP - P * s_)
                    o = ps[0:m, 6 + e % 2, P * s_:P * s_ + P]
                    for c in range(HC):
                        mm(o, gT[:, e % 2, c, P * s_:P * s_ + m], ew2s[:, e, c, :], c == 0, False)
                    ins = mm(o, onesf[0:1, 0:m], eb2r[:, e, :], False, True)
                ins.then_inc(e2_mm, 1)

            expert_up(0)
            for e in range(E):
                if e + 1 < E:
                    expert_up(e + 1)
                expert_down(e)


_INS = ['L0_attn_x', 'L0_attn_WQ', 'L0_attn_WK', 'L0_attn_WV', 'L0_attn_WO', 'L0_ffn_mix_kernel', 'L0_ffn_W1',
        'L0_ffn_b1', 'L0_ffn_W2', 'L0_ffn_b2', 'L0_ffn_Wo1', 'L0_ffn_bo1', 'L0_ffn_Wo2', 'L0_ffn_bo2',
        'L0_ffn_gamma', 'L0_ffn_beta', 'L0_c', 'L0_wmod', 'w_qkv_heads', 'w_v', 'L1_attn_w_out', 'L1_attn_b_out',
        'L1_attn_proj', 'L1_ffn_router_w', 'L1_ffn_router_b', 'L1_ffn_w1', 'L1_ffn_b1', 'L1_ffn_w2',
        'L1_ffn_b2', 'L1_c', 'L1_wmod']


def _laid_out(a):
    import numpy as np

    a = {n: np.asarray(v) for n, v in a.items()}
    a['L0_ffn_mix_kernel'] = a['L0_ffn_mix_kernel'].T
    a['L0_ffn_W1'] = a['L0_ffn_W1'].transpose(1, 0, 2)
    a['L0_ffn_b1'] = a['L0_ffn_b1'].reshape(3, 96).T
    a['L0_ffn_W2'] = a['L0_ffn_W2'].reshape(3, 96, 128).transpose(1, 0, 2)
    w = a.pop('L1_attn_w_qkv')
    a['w_qkv_heads'] = w.reshape(24, 16, 128).transpose(1, 0, 2)
    a['w_v'] = w[256:]
    a['L1_attn_proj'] = a['L1_attn_proj'].transpose(1, 0, 2)
    a['L1_ffn_w1'] = a['L1_ffn_w1'].transpose(1, 0, 2)
    a['L1_ffn_b1'] = a['L1_ffn_b1'].reshape(8, 4, 128).transpose(2, 0, 1)
    a['L1_ffn_w2'] = a['L1_ffn_w2'].reshape(8, 4, 128, 128).transpose(2, 0, 1, 3)
    return a


_OUTS = [((1, 2048, 128), 'float32')]


def kernel(**inputs):
    import numpy as _np
    import concourse.bacc as _bacc
    from concourse import mybir as _mybir
    from concourse.bass_utils import run_bass_kernel_spmd as _run

    nc = _bacc.Bacc("TRN2", target_bir_lowering=False, num_devices=1)
    arrays, args = {}, []
    inputs = _laid_out(inputs)
    for name in _INS:
        a = _np.ascontiguousarray(inputs[name])
        arrays[f"in_{name}_dram"] = a
        args.append(nc.dram_tensor(f"in_{name}_dram", a.shape, _mybir.dt.from_np(a.dtype), kind="ExternalInput").ap())
    for i, (shape, dtype) in enumerate(_OUTS):
        dt = _mybir.dt.from_np(_np.dtype(dtype))
        args.append(nc.dram_tensor(f"out_{i}_dram", shape, dt, kind="ExternalOutput").ap())
    adaln_two_layers(nc, *args)
    r = _run(nc, [arrays], core_ids=[0])
    got = tuple(r.results[0][f"out_{i}_dram"] for i in range(len(_OUTS)))
    return got[0]
```

```python
from contextlib import ExitStack

import concourse.bass as bass
from concourse import mybir

P = 128
ALU = mybir.AluOpType
ACT = mybir.ActivationFunctionType
AX = mybir.AxisListType
F32 = mybir.dt.float32
BF16 = mybir.dt.bfloat16
I32 = mybir.dt.int32
U32 = mybir.dt.uint32
EPS = 1e-5
MASKED = -1e30


def adaln_two_layers(
    nc: bass.Bass, x, WQ, WK, WV, WO, mix_kernel, W1, b1, W2, b2, Wo1, bo1, Wo2, bo2, gamma, beta,
    c0, wmod0, w_qkv_heads, w_v, w_out, b_out, proj, router_w, router_b, ew1, eb1, ew2, eb2, c1, wmod1, out,
):
    S, D = x.shape[1], x.shape[2]
    TILES = S // P
    CH = 4
    CT = TILES // CH
    CW = CT * P
    H0, DK = 16, D // 16
    HG = 4
    GROUPS = H0 // HG
    ROWS = 96
    SCALE = float(DK) ** -0.5
    NP, DM = W1.shape[1], W1.shape[2]
    PG = 3
    NG = NP // PG
    GR = PG * DM
    HD, H1 = proj.shape[0], proj.shape[1]
    BLK = 32
    E, HID = ew1.shape[1], ew1.shape[2]
    HH = H1 // 2
    HC = HID // P
    CAP = max(1, -(-S * 5 // (E * 4)))
    SLOTS = E * CAP
    ET = -(-CAP // P)
    LAST = CAP - P * (ET - 1)
    META = 4
    assert SLOTS % P == 0 and D == P and TILES == CH * CT and LAST % 32 == 0

    ctx = ExitStack()
    with ctx:
        def sb(name, shape, dt=F32):
            return ctx.enter_context(nc.sbuf_tensor(name, shape, dt))

        def sem(name):
            return ctx.enter_context(nc.semaphore(name))

        qk_dram = nc.dram_tensor("qk_parts_dram", (2, 3, D, S), BF16, kind="Internal").ap()
        slot_in = nc.dram_tensor("slot_in_dram", (SLOTS, D + META), F32, kind="Internal").ap()
        picked = nc.dram_tensor("picked_dram", (2 * S, D), F32, kind="Internal").ap()

        ps = ctx.enter_context(nc.psum_tensor("ps", [P, 8, 512], F32))

        X = sb("X", [P, TILES, D])
        nrm = sb("nrm", [P, TILES, D + META])
        zeros = sb("zeros", [P, D + META])
        hT = sb("hT", [P, 2, S + 2])
        stats = sb("stats", [P, CT, 6])
        mv = sb("mv", [P, 2, CT, 2])
        ve = sb("ve", [P, 2, CT])
        rstd = sb("rstd", [P, 2, CT])
        cT = sb("cT", [P, 2, CW])
        identf = sb("identf", [P, P])
        identb = sb("identb", [P, P], BF16)
        onesf = sb("onesf", [P, P])
        onesb = sb("onesb", [P, P], BF16)
        causal = sb("causal", [P, P], BF16)
        blockmask = sb("blockmask", [P, P])
        upto = sb("upto", [P, P], BF16)
        spread = sb("spread", [NP, NP, DM], BF16)
        rank9 = sb("rank9", [P, CT, NP])
        rank8 = sb("rank8", [P, TILES, E])
        neghalf = sb("neghalf", [P, CT])
        onerow = hT[0:2, 1, 1:1 + S // 2].bitcast(BF16)
        ccol = sb("ccol", [P, 2])
        cexp = sb("cexp", [P, 2])
        cden = sb("cden", [P, 2])
        crec = sb("crec", [P, 2])
        scol = sb("scol", [P, 2])
        smat = sb("smat", [P, 2, P])
        wmod = sb("wmod", [P, 2, 6 * D])
        modc = sb("modc", [P, 2, 4])
        gate = sb("gate", [P, 4, D])
        wq = sb("wq", [P, 4, D])
        wog = sb("wog", [P, D])
        mixc = sb("mixc", [P, 3])
        w1s = sb("w1s", [P, NP, DM])
        b1c = sb("b1c", [GR, NG])
        w2s = sb("w2s", [GR, NG, D])
        b2s = sb("b2s", [NP, D])
        wo1 = sb("wo1", [P, DM])
        bo1c = sb("bo1c", [DM, 1])
        wo2 = sb("wo2", [DM + 1, NP])
        gb_rows = sb("gb_rows", [P, 2, D])
        gbg = sb("gbg", [P, 2, D])
        wvrow = sb("wvrow", [P, D])
        wvT = sb("wvT", [P, D])
        pfold = sb("pfold", [P, 2 * H1, P])
        woutT = sb("woutT", [P, D])
        brow = sb("brow", [1, D])
        browg = sb("browg", [1, D])
        rw = sb("rw", [P, E])
        rb = sb("rb", [1, E])
        eb1c = sb("eb1c", [P, E, HC])
        eb2r = sb("eb2r", [1, E, D])
        KS = sb("KS", [P, 2, HG, S], BF16)
        QS = sb("QS", [P, 2, HG, S], BF16)
        vtok = sb("vtok", [P, TILES, D])
        Vg = sb("Vg", [P, 2, TILES, HG, 32])
        pT = sb("pT", [P, 3, HG, CW])
        tmax = sb("tmax", [P, 2, CT * HG, CH])
        negm = sb("negm", [P, CT * HG])
        mhl = sb("mhl", [P, CT, HG, 2], BF16)
        rden = sb("rden", [P, CT, HG])
        den1 = sb("den1", [P, CT, HH])
        shared = sb("shared", [P, 8 * CW])
        parts = shared[:, 0:6 * CW].bitcast(BF16).rearrange(
            "p (a k b s) -> p a k b s", a=3, k=2, b=2)
        rest = shared[:, 6 * CW:8 * CW].rearrange("p (k s) -> p k s", k=2)
        oT = shared[:, 0:2 * CW].rearrange("p (b s) -> p b s", b=2)
        attn = shared[:, 2 * CW:6 * CW].rearrange("p (t d) -> p t d", t=TILES)
        taug = shared[0:DM + 1, 6 * CW:7 * CW]
        gsgn = rest[:, 0, :].rearrange("p (g d) -> p g d", g=4)
        gneg, gabs = (cT[:, b, :].rearrange("p (g d) -> p g d", g=4) for b in range(2))
        early = pT[:, :, :, :].rearrange("p a h s -> p (a h s)")
        wqkv16 = early[0:HD, 0:3 * H1 * D].rearrange("p (h d) -> p h d", h=3 * H1)
        proj_s = early[0:HD, 3 * H1 * D:4 * H1 * D].rearrange("p (h d) -> p h d", h=H1)
        woutr = early[:, 4 * H1 * D:4 * H1 * D + D]
        eq9 = sb("eq9", [P, CT, NP])
        top9 = sb("top9", [P, CT])
        best9 = sb("best9", [P, CT])
        hot9 = sb("hot9", [P, CT, 16], BF16)
        hotT = sb("hotT", [NP, CW], BF16)
        hotTf = shared[0:NP, 7 * CW:8 * CW]

        KSf = KS[:, :, :, :].rearrange("p b h s -> p (b h s)").bitcast(F32)
        QSf = QS[:, :, :, :].rearrange("p b h s -> p (b h s)").bitcast(F32)
        assert H0 * S // 4 >= E * HC * D
        hid = pT[0:GR, 0, 0:NG, :]
        hsel = pT[0:GR, 1, 0:NG, :]
        tmp = pT[:, 2, :, 0:D]
        expq = KSf[:, 0:2 * 2 * CW].rearrange("p (b k s) -> p b k s", b=2, k=2)
        feat = KSf[:, 2 * 2 * CW:4 * 2 * CW].rearrange("p (b k s) -> p b k s", b=2, k=2)
        am = pT[:, 0, 0:2, :]
        onT = pT[:, 0, 2, :]
        on = pT[:, 1, 0, :].rearrange("p (t d) -> p t d", t=CT)
        vgf = Vg[:, :, :, :, :].rearrange("p a t h c -> p (a t h c)")
        vone = vgf[:, SLOTS:SLOTS + 2 * CT * H1 * (HD + 1)].rearrange(
            "p (b t h c) -> p b t h c", b=2, t=CT, h=H1)
        ew1s = QSf[:, 0:E * HID].rearrange("p (e h) -> p e h", e=E)
        ew2s = QSf[:, E * HID:2 * E * HID].rearrange("p (e c d) -> p e c d", e=E, c=HC)

        x_loaded = sem("x_loaded")
        mod_loaded = sem("mod_loaded")
        w_loaded = sem("w_loaded")
        w2_loaded = sem("w2_loaded")
        ex_loaded = sem("ex_loaded")
        consts = sem("consts")
        pchain = sem("pchain")
        dchain = sem("dchain")
        achain = sem("achain")
        c_exp = sem("c_exp")
        silu_ready = sem("silu_ready")
        mod_mm = sem("mod_mm")
        mod_ready = sem("mod_ready")
        fold_mm = sem("fold_mm")
        fold_ready = sem("fold_ready")
        ve_ready = sem("ve_ready")
        rstd_ready = sem("rstd_ready")
        nrm_ready = sem("nrm_ready")
        tposed = sem("tposed")
        hT_ready = sem("hT_ready")
        qk_mm = sem("qk_mm")
        qk_hi = sem("qk_hi")
        qk_rest = sem("qk_rest")
        qk_mid = sem("qk_mid")
        qk_lo = sem("qk_lo")
        qk_stored = [sem(f"qk_stored{i}") for i in range(2)]
        v_ready = sem("v_ready")
        heads_loaded = [sem(f"heads_loaded{i}") for i in range(2)]
        vg_ready = sem("vg_ready")
        heads_free = [sem(f"heads_free{i}") for i in range(2)]
        a_ready = sem("a_ready")
        a_maxed = sem("a_maxed")
        m_parts = sem("m_parts")
        m_turned = sem("m_turned")
        m_rows = sem("m_rows")
        m_neg = sem("m_neg")
        b_ready = sem("b_ready")
        b_exped = sem("b_exped")
        diag_cut = sem("diag_cut")
        pv_done = sem("pv_done")
        o_copied = sem("o_copied")
        o_turned = sem("o_turned")
        o_rden = sem("o_rden")
        o_normed = sem("o_normed")
        at_turned = sem("at_turned")
        at_ready = sem("at_ready")
        y_mm = sem("y_mm")
        y_read = sem("y_read")
        conv_first = sem("conv_first")
        conv_ready = sem("conv_ready")
        u_mm = sem("u_mm")
        t_ready = sem("t_ready")
        hid_mm = sem("hid_mm")
        hid_ready = sem("hid_ready")
        sc_mm = sem("sc_mm")
        hot_ready = sem("hot_ready")
        hot_turned = sem("hot_turned")
        hot_copied = sem("hot_copied")
        mask_mm = sem("mask_mm")
        hsel_ready = sem("hsel_ready")
        ffn_mm = sem("ffn_mm")
        ffn_read = sem("ffn_read")
        v1_mm = sem("v1_mm")
        v2_mm = sem("v2_mm")
        v2_ready = sem("v2_ready")
        f_mm = sem("f_mm")
        f_exp = sem("f_exp")
        f_ready = sem("f_ready")
        s_mm = sem("s_mm")
        s_ready = sem("s_ready")
        av_mm = sem("av_mm")
        on_ready = sem("on_ready")
        on_turned = sem("on_turned")
        onT_ready = sem("onT_ready")
        turned2 = [sem(f"turned2_{i}") for i in range(2)]
        hT2_ready = [sem(f"hT2_ready{i}") for i in range(2)]
        y1_mm = sem("y1_mm")
        y1_read = sem("y1_read")
        lg_mm = sem("lg_mm")
        r_exped = sem("r_exped")
        r_shift = sem("r_shift")
        r_mask = sem("r_mask")
        pos_mm = sem("pos_mm")
        slots_ready = sem("slots_ready")
        zero_filled = sem("zero_filled")
        scattered = sem("scattered")
        slots_loaded = [sem(f"slots_loaded{i}") for i in range(E)]
        meta_ready = sem("meta_ready")
        xs_turned = sem("xs_turned")
        xs_ready = sem("xs_ready")
        e1_mm = sem("e1_mm")
        gelu_ready = sem("gelu_ready")
        e2_mm = sem("e2_mm")
        eo_ready = sem("eo_ready")
        eo_sent = [sem(f"eo_sent{i}") for i in range(2)]
        picked_loaded = [sem(f"picked_loaded{i}") for i in range(CH)]
        out_ready = sem("out_ready")
        out_stored = sem("out_stored")

        lg = sb("lg", [P, TILES, E])
        gates = sb("gates", [P, TILES, E])
        red = sb("red", [P, 12, TILES])
        hot = sb("hot", [P, 2, TILES, E])
        sel = sb("sel", [P, 2, TILES, E])
        chosen = sb("chosen", [P, TILES, E + 1], BF16)
        slotf = sb("slotf", [P, 2, TILES])
        slot_w = sb("slot_w", [P, 2, TILES], U32)
        wsel = sb("wsel", [P, 2, TILES])
        smeta = sb("smeta", [P, 6, E, ET])
        to_row = sb("to_row", [P, E, ET], U32)
        slotrows = KSf[:, 4 * 2 * CW:4 * 2 * CW + E * ET * (D + META)].rearrange(
            "p (e t d) -> p e t d", e=E, t=ET)
        gath = KSf[:, 0:2 * TILES * D].rearrange("p (k t d) -> p k t d", k=2, t=TILES)
        xsT = vgf[:, 0:SLOTS]
        gT = pT[:, :, :, :].rearrange("p a h s -> p (a h s)")[:, 0:2 * HC * CAP].rearrange(
            "p (b c s) -> p b c s", b=2, c=HC)
        eo = oT[:, :, 0:ET * D].rearrange("p b (s d) -> p b s d", s=ET)

        A_TOTAL = 2 * sum(CT * HG * (c + 1) for c in range(CH))
        ITEMS = 2 * CH
        UNITS = 2 * sum(CT * (c + 1) for c in range(CH))
        DIAGS = 2 * CH * CT
        items = [(0, c) for c in range(CH)] + [(1, c) for c in reversed(range(CH))]

        def pieces(it):
            g, c = items[it]
            return [(g, c, qi, j, kc) for qi in range(CT) for j in range(HG) for kc in range(c + 1)]

        a_start = [sum(len(pieces(n)) for n in range(it)) for it in range(ITEMS + 1)]
        units = [(it, kb) for it in range(ITEMS) for kb in range(CT * (items[it][1] + 1))]
        diag_no = {u: n for n, u in enumerate(u for u, (it, kb) in enumerate(units) if kb >= CT * items[it][1])}
        last_unit = {it: max(u for u, x_ in enumerate(units) if x_[0] == it) for it in range(ITEMS)}

        def hosted(it, k):
            if it + 1 == ITEMS:
                return range(0, 0)
            n, u = len(pieces(it + 1)), CT * (items[it][1] + 1) - 1
            return range(min(n, -(-n * k // u)), min(n, -(-n * (k + 1) // u)))

        mps = ps[:, 6, :].bitcast(BF16)
        hps = ps[:, 7, :].bitcast(BF16)

        block = ctx.enter_context(nc.Block())

        @block.sync
        def _(sp):
            def load(dst, src, s):
                sp.dma_start(dst, src).then_inc(s, 16)

            def row(v):
                return v.rearrange("(a n) -> a n", a=1)

            xt = x[0].rearrange("(t p) d -> p t d", p=P)
            for t in range(CH):
                load(X[:, CT * t:CT * t + CT, :], xt[:, CT * t:CT * t + CT, :], x_loaded)
            load(ccol[:, 0:1], c0.rearrange("a d -> d a"), mod_loaded)
            load(ccol[:, 1:2], c1.rearrange("a d -> d a"), mod_loaded)
            load(wmod[:, 0, :], wmod0, mod_loaded)
            load(wmod[:, 1, :], wmod1, mod_loaded)
            for i, w in enumerate((WQ, WK, WV, WO)):
                load(wq[:, i, :], w, w_loaded)
            load(mixc[:, :], mix_kernel, w2_loaded)
            load(w1s[:, :, :], W1, w2_loaded)
            load(b1c[:, :], b1, w2_loaded)
            load(w2s[:, :, :], W2, w2_loaded)
            load(b2s[:, :], b2, w2_loaded)
            load(wo1[:, :], Wo1, w2_loaded)
            load(bo1c[:, :], bo1.rearrange("(n a) -> n a", a=1), w2_loaded)
            load(wo2[0:DM, :], Wo2, w2_loaded)
            load(wo2[DM:DM + 1, :], row(bo2), w2_loaded)
            load(gb_rows[:, 0, :], row(gamma).to_broadcast([P, D]), w2_loaded)
            load(gb_rows[:, 1, :], row(beta).to_broadcast([P, D]), w2_loaded)
            load(wqkv16[:, :, :], w_qkv_heads, w2_loaded)
            load(wvrow[:, :], w_v, w2_loaded)
            load(proj_s[:, :, :], proj, w2_loaded)
            load(woutr, w_out, w2_loaded)
            load(brow[:, :], row(b_out), w2_loaded)
            load(rw[:, :], router_w, w2_loaded)
            load(rb[:, :], row(router_b), w2_loaded)
            load(eb1c[:, :, :], eb1, w2_loaded)
            load(eb2r[:, :, :], eb2.rearrange("(a e) d -> a e d", a=1), w2_loaded)
            for t in range(CH):
                for k in range(2):
                    sp.wait_ge(qk_lo, 2 * t + k + 1)
                    load(qk_dram[k, :, :, CW * t:CW * t + CW].rearrange("a d s -> d a s"),
                         parts[:, :, k, t % 2, :], qk_stored[t % 2])
            for s in heads_free:
                sp.wait_ge(s, 1)
            for b in range(2):
                for j in range(HG):
                    load(KS[ROWS + 2 * j:ROWS + 2 * j + 2, b, j, :], onerow[:, :], heads_loaded[b])
            for s in qk_stored:
                sp.wait_ge(s, 16 * CH)
            with sp.Fori(0, GROUPS // 2) as i:
                for b in range(2):
                    sp.wait_ge(heads_free[b], i + 1)
                    src = qk_dram[:, :, bass.ds(2 * HG * DK * i + HG * DK * b, HG * DK), :]
                    kv = src[1].rearrange("a (j d) s -> a d j s", j=HG)
                    qv = src[0].rearrange("a (j d) s -> a d j s", j=HG)
                    n = 0
                    for rows in (3, 2, 1):
                        for r in range(rows):
                            at = DK * n
                            load(KS[at:at + DK, b, :, :], kv[r], heads_loaded[b])
                            load(QS[at:at + DK, b, :, :], qv[3 - rows], heads_loaded[b])
                            n += 1
            for s in heads_free:
                sp.wait_ge(s, GROUPS // 2 + 1)
            load(ew1s, ew1, ex_loaded)
            load(ew2s, ew2, ex_loaded)
            sp.wait_ge(consts, 1)
            for dst in (slot_in, picked):
                n = dst.shape[0] // P
                load(dst.rearrange("(t p) d -> p t d", p=P),
                     zeros[:, 0:dst.shape[1]].unsqueeze(1).to_broadcast([P, n, dst.shape[1]]), zero_filled)
            sp.wait_ge(scattered, 16 * 2 * TILES)
            for e in range(E):
                src = slot_in[CAP * e:CAP * e + CAP, :]
                load(slotrows[:, e, 0:ET - 1, :], src[0:P * (ET - 1), :].rearrange("(t p) d -> p t d", p=P),
                     slots_loaded[e])
                load(slotrows[0:LAST, e, ET - 1, :], src[P * (ET - 1):CAP, :], slots_loaded[e])
            for n, s in enumerate(eo_sent):
                sp.wait_ge(s, 16 * ET * E // 2)
            for t in range(CH):
                for k in range(2):
                    load(gath[:, k, CT * t:CT * t + CT, :],
                         picked[S * k + CW * t:S * k + CW * t + CW, :].rearrange("(t p) d -> p t d", p=P),
                         picked_loaded[t])
            for t in range(CH):
                sp.wait_ge(out_ready, t + 1)
                load(out[0].rearrange("(t p) d -> p t d", p=P)[:, CT * t:CT * t + CT, :],
                     X[:, CT * t:CT * t + CT, :], out_stored)
            sp.wait_ge(out_stored, 16 * CH)

        @block.gpsimd
        def _(pool):
            step = [0]

            def link(ins):
                step[0] += 1
                ins.then_inc(pchain, 1)
                pool.wait_ge(pchain, step[0])

            def pattern(t, base, pat, cm, op, fill):
                link(pool.affine_select(out=t, in_=t, compare_op=op, fill=fill, base=base, pattern=pat,
                                        channel_multiplier=cm))

            pool.memset(neghalf[:, :], -0.5).then_inc(pchain, 1)
            step[0] += 1
            link(pool.memset(identf[:, :], 0.0))
            pattern(identf[:, :], 0, [[-1, P]], 1, ALU.not_equal, 1.0)
            link(pool.memset(onesf[:, :], 1.0))
            link(pool.memset(zeros[:, :], 0.0))
            pool.memset(onesb[:, :], 1.0).then_inc(consts, 1)
            pool.wait_ge(consts, 1)

            def rstd_of(k):
                pool.wait_ge(ve_ready, k + 1)
                pool.tensor_tensor(rstd[:, k % 2, :], ve[:, k % 2, :], neghalf[:, :], ALU.pow).then_inc(rstd_ready, 1)
                pool.wait_ge(rstd_ready, k + 1)

            for t in range(CH):
                rstd_of(t)
            link(pool.memset(identb[:, :], 0.0))
            pattern(identb[:, :], 0, [[-1, P]], 1, ALU.not_equal, 1.0)
            link(pool.memset(causal[:, :], 0.0))
            pattern(causal[:, :], 0, [[-1, P]], 1, ALU.is_ge, MASKED)
            link(pool.memset(onerow[:, :], 1.0))
            for b in range(2):
                link(pool.memset(KS[:, b, :, :].rearrange("p h s -> p (h s)").bitcast(F32), 0.0))
                link(pool.memset(QS[:, b, :, :].rearrange("p h s -> p (h s)").bitcast(F32), 0.0))
            for b in range(2):
                link(pool.memset(Vg[:, b, :, :, :], 0.0))
                link(pool.memset(Vg[:, b, :, :, DK:DK + 1], 1.0))
            for b in range(2):
                pool.memset(hT[:, b, 0:S + 2:S + 1], 0.0).then_inc(heads_free[b], 1)
                pool.wait_ge(heads_free[b], 1)
            link(pool.memset(blockmask[:, :], 0.0))
            for j in range(P // BLK):
                link(pool.memset(blockmask[BLK * j:BLK * j + BLK, BLK * j:BLK * j + BLK], 1.0))
            link(pool.memset(upto[:, :], 1.0))
            pattern(upto[:, :], 0, [[1, P]], -1, ALU.is_ge, 0.0)
            link(pool.memset(spread[:, :, :], 0.0))
            pattern(spread[:, :, :], 0, [[-1, NP], [0, DM]], 1, ALU.not_equal, 1.0)
            for p in range(NP):
                link(pool.memset(rank9[:, :, p:p + 1], float(NP - p)))
            for e in range(E):
                link(pool.memset(rank8[:, :, e:e + 1], float(E - e)))
            link(pool.memset(hot9[:, :, :], 0.0))
            link(pool.memset(chosen[:, :, :], 1.0))
            pool.wait_ge(qk_lo, 2 * CH)
            pool.memset(taug[DM:DM + 1, :], 1.0).then_inc(consts, 1)
            pool.wait_ge(consts, 2)

            pool.wait_ge(v_ready, CH)
            def copy_v(i, b):
                pool.wait_ge(heads_free[b], i + 1)
                at = HG * DK * (2 * i + b)
                pool.tensor_copy(Vg[:, b, :, :, 0:DK], vtok[:, :, at:at + HG * DK].rearrange(
                    "p t (h c) -> p t h c", h=HG)).then_inc(vg_ready, 1)
                pool.wait_ge(vg_ready, 2 * i + b + 1)

            copy_v(0, 0)
            copy_v(0, 1)
            for i in range(GROUPS // 2):
                for u, n in diag_no.items():
                    it, kb = units[u]
                    if i + 1 < GROUPS // 2 and n == DIAGS // 2:
                        copy_v(i + 1, 0)
                    off = P * (kb - CT * items[it][1])
                    pool.wait_ge(b_exped, HG * (UNITS * i + u + 1))
                    pm = pT[:, u % 3, :, off:off + P]
                    pool.affine_select(out=pm, in_=pm, compare_op=ALU.is_ge, fill=0.0, base=0,
                                       pattern=[[0, HG], [1, P]], channel_multiplier=-1).then_inc(diag_cut, 1)
                    pool.wait_ge(diag_cut, DIAGS * i + n + 1)
                if i + 1 < GROUPS // 2:
                    copy_v(i + 1, 1)
            for k in range(CH, 4 * CH):
                if k == CH + 1:
                    pool.memset(vone[:, :, :, :, HD:HD + 1].rearrange("p b t h c -> p (b t h c)"), 1.0)\
                        .then_inc(consts, 1)
                    pool.wait_ge(consts, 3)
                    pool.memset(slotrows[LAST:P, :, ET - 1, :], 0.0).then_inc(consts, 1)
                    pool.wait_ge(consts, 4)
                rstd_of(k)

            def dispatch(t):
                pool.wait_ge(slots_ready, t + 1)
                if t == 0:
                    pool.wait_ge(zero_filled, 16 * 2)
                for i in range(CT * t, CT * t + CT):
                    for k in range(2):
                        pool.indirect_dma_start(
                            slot_in[:, :], bass.IndirectOffsetOnAxis(ap=slot_w[:, k, i:i + 1], axis=0),
                            nrm[:, i, :], None, bounds_check=SLOTS - 1, oob_is_err=False).then_inc(scattered, 16)

            for t in range(CH):
                rstd_of(4 * CH + t)
                if t >= 1:
                    dispatch(t - 1)
            dispatch(CH - 1)
            pool.wait_ge(meta_ready, 1)
            for e in range(E):
                pool.wait_ge(eo_ready, e + 1)
                for n in range(ET):
                    m = min(P, CAP - P * n)
                    pool.indirect_dma_start(
                        picked[:, :], bass.IndirectOffsetOnAxis(ap=to_row[0:m, e, n:n + 1], axis=0),
                        eo[0:m, e % 2, n, :], None, bounds_check=2 * S - 1, oob_is_err=False)\
                        .then_inc(eo_sent[e % 2], 16)

        @block.scalar
        def _(act):
            step = [0]

            def link(ins):
                step[0] += 1
                ins.then_inc(achain, 1)
                act.wait_ge(achain, step[0])

            act.wait_ge(mod_loaded, 16 * 4)
            act.activation(cexp[:, :], ccol[:, :], ACT.Exp, scale=-1.0).then_inc(c_exp, 1)

            def modulate(m, t, layer, which, bank):
                act.wait_ge(tposed, CH * m + t + 1)
                if m == 0 and t == 0:
                    act.wait_ge(mod_ready, 1)
                act.activation(hT[:, m % 2, 1 + CW * t:1 + CW * t + CW], ps[:, bank, :], ACT.Identity,
                               bias=modc[:, layer, 2 * which:2 * which + 1],
                               scale=modc[:, layer, 2 * which + 1:2 * which + 2]).then_inc(hT_ready, 1)

            for t in range(CH):
                modulate(0, t, 0, 0, t % 2)
                for k in range(2):
                    act.wait_ge(qk_mm, 2 * t + k + 1)
                    if t >= 2:
                        act.wait_ge(qk_stored[t % 2], 16 * 2 * (t // 2))
                    act.activation(parts[:, 0, k, t % 2, :], ps[:, 2 + k, :], ACT.Copy).then_inc(qk_hi, 1)
                    act.wait_ge(qk_rest, 2 * t + k + 1)
                    act.activation(parts[:, 1, k, t % 2, :], rest[:, k, :], ACT.Copy).then_inc(qk_mid, 1)
                act.wait_ge(v1_mm, t + 1)
                act.activation(vtok[:, CT * t:CT * t + CT, :], ps[:, 4, :].rearrange("p (t d) -> p t d", t=CT),
                               ACT.Copy).then_inc(v_ready, 1)

            for g in range(2 * H1 // 4):
                act.wait_ge(fold_mm, g + 1)
                act.activation(pfold[:, 4 * g:4 * g + 4, :], ps[:, g, :].rearrange("p (h f) -> p h f", h=4),
                               ACT.Copy).then_inc(fold_ready, 1)

            with act.Fori(0, GROUPS // 2) as i:
                for u, (it, kb) in enumerate(units):
                    off = P * max(0, kb - CT * items[it][1])
                    if u >= 3:
                        act.wait_ge(pv_done, UNITS * i + u - 2)
                    for j in range(HG):
                        n = HG * u + j
                        act.wait_ge(b_ready, HG * UNITS * i + n + 1)
                        act.activation(pT[:, u % 3, j, off:CW], ps[:, n % 3, off:CW], ACT.Exp, scale=SCALE)\
                           .then_inc(b_exped, 1)

            for t in range(CH):
                act.wait_ge(at_turned, t + 1)
                if t >= 2:
                    act.wait_ge(y_mm, t - 1)
                act.activation(cT[:, t % 2, :], ps[:, t % 2, :], ACT.Copy).then_inc(at_ready, 1)
                if t >= 1:
                    modulate(1, t - 1, 0, 1, 4 + (t - 1) % 2)
            modulate(1, CH - 1, 0, 1, 4 + (CH - 1) % 2)

            for t in range(CH):
                act.wait_ge(w2_loaded, 16 * 20)
                act.wait_ge(hT_ready, CH + t + 1)
                if t >= 2:
                    act.wait_ge(hid_mm, t - 1)
                act.activation(cT[:, t % 2, :], hT[:, 1, 1 + CW * t:1 + CW * t + CW], ACT.Copy,
                               scale=mixc[:, 1:2]).then_inc(conv_first, 1)
                act.wait_ge(u_mm, t + 1)
                act.wait_ge(sc_mm, t)
                act.activation(taug[0:DM, :], ps[0:DM, 7, :], ACT.Tanh, bias=bo1c[:, 0:1])\
                   .then_inc(t_ready, 1)
                act.wait_ge(hid_mm, t + 1)
                if t >= 1:
                    act.wait_ge(hsel_ready, t)
                for g in range(NG):
                    ins = act.activation(hid[:, g, :], ps[0:GR, g, :], ACT.Identity, bias=b1c[:, g:g + 1])
                    ins.then_inc(hid_ready, 1)

            def modulate2(which, t, bank):
                act.wait_ge(turned2[which], t + 1)
                act.activation(hT[:, which, 1 + CW * t:1 + CW * t + CW], ps[:, bank, :], ACT.Identity,
                               bias=modc[:, 1, 2 * which:2 * which + 1],
                               scale=modc[:, 1, 2 * which + 1:2 * which + 2]).then_inc(hT2_ready[which], 1)

            def copy_values(t):
                act.wait_ge(v2_mm, t + 1)
                act.wait_ge(consts, 3)
                if t >= 2:
                    act.wait_ge(av_mm, H1 * (t - 1))
                act.activation(vone[:, t % 2, :, :, 0:HD], ps[:, 0, :].rearrange("p (t h d) -> p t h d", t=CT, h=H1),
                               ACT.Copy).then_inc(v2_ready, 1)

            def exp_min(n):
                act.wait_ge(f_mm, n + 1)
                if n >= 2:
                    act.wait_ge(f_ready, n - 1)
                eq_ = expq[:, n % 2, :, :]
                link(act.activation(eq_, ps[:, 2 + 2 * (n % 2):4 + 2 * (n % 2), :], ACT.Relu, scale=-1.0))
                act.activation(eq_, eq_, ACT.Exp, scale=-1.0).then_inc(f_exp, 1)

            def between(t, h):
                if h == 1 and t >= 2:
                    act.wait_ge(r_shift, t - 1)
                    at = slice(CT * (t - 2), CT * (t - 1))
                    act.activation(gates[:, at, :], lg[:, at, :], ACT.Exp).then_inc(r_exped, 1)
                if h == 1 and 1 <= t <= CH:
                    act.wait_ge(on_turned, t)
                    if t >= 2:
                        act.wait_ge(y1_mm, t - 1)
                    act.activation(onT, ps[:, 0, :], ACT.Copy).then_inc(onT_ready, 1)
                if h == 4 and t + 1 < CH:
                    modulate2(0, t + 1, 0)
                if h == 5 and t + 1 < CH:
                    copy_values(t + 1)
                if h == 7 and 1 <= t <= CH:
                    modulate2(1, t - 1, 0)

            modulate2(0, 0, 0)
            copy_values(0)
            exp_min(0)
            exp_min(1)
            for t in range(CH + 2):
                for h in range(H1):
                    if H1 * t + h + 2 < H1 * CH:
                        exp_min(H1 * t + h + 2)
                    between(t, h)
            for e in range(E):
                act.wait_ge(xs_turned, e + 1)
                act.activation(xsT[:, CAP * e:CAP * e + CAP], ps[:, e % 2, 0:CAP], ACT.Identity,
                               bias=modc[:, 1, 2:3], scale=modc[:, 1, 3:4]).then_inc(xs_ready, 1)
            for e in range(E):
                for c in range(HC):
                    act.wait_ge(e1_mm, HC * e + c + 1)
                    if e >= 2 and c == 0:
                        act.wait_ge(e2_mm, e - 1)
                    act.activation(gT[:, e % 2, c, :], ps[:, 2 + c, 0:CAP], ACT.Gelu, bias=eb1c[:, e, c:c + 1])\
                       .then_inc(gelu_ready, 1)

        @block.vector
        def _(dve):
            step = [0]

            def link(ins):
                step[0] += 1
                ins.then_inc(dchain, 1)
                dve.wait_ge(dchain, step[0])

            def stats_of(k, rows):
                for i in range(CT):
                    ins = dve.bn_stats(stats[:, i, :], rows(i))
                    step[0] += 1
                    ins.then_inc(dchain, 1)
                dve.wait_ge(dchain, step[0])
                for i in range(CT):
                    ins = dve.bn_aggr(mv[:, k % 2, i, :], stats[:, i, :])
                    step[0] += 1
                    ins.then_inc(dchain, 1)
                dve.wait_ge(dchain, step[0])
                dve.tensor_scalar(ve[:, k % 2, :], mv[:, k % 2, :, 1], EPS, None, ALU.add).then_inc(ve_ready, 1)

            def normalise(k, t, rows, dst, done):
                dve.wait_ge(rstd_ready, k + 1)
                for i in range(CT):
                    ins = dve.tensor_scalar(dst(i), rows(i), mv[:, k % 2, i, 0:1],
                                            rstd[:, k % 2, i:i + 1], ALU.subtract, ALU.mult)
                    if done is None:
                        step[0] += 1
                        ins.then_inc(dchain, 1)
                if done is None:
                    dve.wait_ge(dchain, step[0])
                else:
                    ins.then_inc(done, 1)

            def x_row(t):
                return lambda i: X[:, CT * t + i, :]

            def nrm_row(t):
                return lambda i: nrm[:, CT * t + i, 0:D]

            dve.wait_ge(c_exp, 1)
            link(dve.tensor_scalar(cden[:, :], cexp[:, :], 1.0, None, ALU.add))
            link(dve.reciprocal(crec[:, :], cden[:, :]))
            link(dve.tensor_tensor(scol[:, :], ccol[:, :], crec[:, :], ALU.mult))
            dve.wait_ge(consts, 1)
            for l in range(2):
                ins = dve.tensor_scalar(smat[:, l, :], onesf[:, :], scol[:, l:l + 1], None, ALU.mult)
                ins.then_inc(silu_ready, 1)
            dve.wait_ge(x_loaded, 16 * CH)
            stats_of(0, x_row(0))
            dve.wait_ge(mod_mm, 1)
            cols = ps[:, 7, 0:8].rearrange("p (l c) -> p l c", l=2)
            link(dve.tensor_copy(modc[:, :, :], cols))
            dve.tensor_scalar(modc[:, :, 1:4:2], cols[:, :, 1:4:2], 1.0, None, ALU.add).then_inc(mod_ready, 1)
            g4 = ps[:, 6, :].rearrange("p (g d) -> p g d", g=4)
            link(dve.tensor_scalar(gneg[:, :, :], g4, -1.0, 0.25, ALU.mult, ALU.max))
            link(dve.tensor_tensor(gabs[:, :, :], g4, gneg[:, :, :], ALU.max))
            link(dve.tensor_scalar(gsgn[:, :, :], g4, 0.0, 2.0, ALU.is_ge, ALU.mult))
            link(dve.scalar_tensor_tensor(gate[:, :, :], gsgn[:, :, :], -1.0, gabs[:, :, :], ALU.add, ALU.mult))
            dve.wait_ge(w_loaded, 16 * 4)

            def split(t):
                for k in range(2):
                    dve.wait_ge(qk_hi, 2 * t + k + 1)
                    if t >= 1:
                        dve.wait_ge(qk_lo, 2 * t + k - 1)
                    dve.tensor_tensor(rest[:, k, :], ps[:, 2 + k, :], parts[:, 0, k, t % 2, :], ALU.subtract)\
                       .then_inc(qk_rest, 1)
                    dve.wait_ge(qk_mid, 2 * t + k + 1)
                    dve.tensor_tensor(parts[:, 2, k, t % 2, :], rest[:, k, :], parts[:, 1, k, t % 2, :],
                                      ALU.subtract).then_inc(qk_lo, 1)

            normalise(0, 0, x_row(0), nrm_row(0), nrm_ready)
            stats_of(1, x_row(1))
            for t in range(CH):
                if t + 1 < CH:
                    normalise(t + 1, t + 1, x_row(t + 1), nrm_row(t + 1), nrm_ready)
                if t + 2 < CH:
                    stats_of(t + 2, x_row(t + 2))
                split(t)

            dve.wait_ge(w2_loaded, 16 * 20)
            dve.wait_ge(fold_mm, 2 * H1 // 4 + 1)
            dve.tensor_tensor(wog[:, :], wq[:, 3, :], gate[:, 0, :], ALU.mult).then_inc(fold_ready, 1)
            dve.tensor_copy(wvT[:, :], ps[:, 4, 0:P]).then_inc(fold_ready, 1)
            dve.tensor_tensor(woutT[:, :], ps[:, 4, P:2 * P], gate[:, 2, :], ALU.mult).then_inc(fold_ready, 1)
            for g in range(2):
                dve.tensor_tensor(gbg[:, g, :], gb_rows[:, g, :], gate[:, 1, :], ALU.mult).then_inc(fold_ready, 1)
            dve.tensor_tensor(browg[:, :], brow[:, :], gate[0:1, 2, :], ALU.mult).then_inc(fold_ready, 1)

            with dve.Fori(0, GROUPS // 2) as i:
                def maxima(it, numbers):
                    for n in numbers:
                        g, c, qi, j, kc = pieces(it)[n]
                        a = a_start[it] + n
                        w = CW if kc < c else P * (qi + 1)
                        dve.wait_ge(a_ready, A_TOTAL * i + a + 1)
                        dve.tensor_reduce(tmax[:, it % 2, HG * qi + j, kc:kc + 1], ps[:, 3 + a % 3, 0:w],
                                          AX.X, ALU.max).then_inc(a_maxed, 1)

                def subtract_rows(it):
                    g, c = items[it]
                    dve.wait_ge(a_maxed, A_TOTAL * i + a_start[it + 1])
                    dve.tensor_reduce(negm[:, :], tmax[:, it % 2, :, 0:c + 1], AX.X, ALU.max, negate=True)\
                       .then_inc(m_neg, 1)
                    dve.wait_ge(m_neg, 2 * ITEMS * i + 2 * it + 1)
                    nm = negm[:, :].rearrange("p (t h) -> p t h", h=HG)
                    dve.tensor_copy(mhl[:, :, :, 0], nm).then_inc(m_neg, 1)
                    dve.wait_ge(m_neg, 2 * ITEMS * i + 2 * it + 2)
                    dve.tensor_tensor(mhl[:, :, :, 1], nm, mhl[:, :, :, 0], ALU.subtract).then_inc(m_parts, 1)
                    dve.wait_ge(m_turned, ITEMS * i + it + 1)
                    dve.tensor_copy(QS[ROWS:ROWS + 2 * HG, g, :, CW * c:CW * c + CW],
                                    mps[ROWS:ROWS + 2 * HG, 0:CW].unsqueeze(1).to_broadcast([2 * HG, HG, CW]))\
                       .then_inc(m_rows, 1)

                def copy_item(it):
                    dve.wait_ge(pv_done, UNITS * i + last_unit[it] + 1)
                    dve.tensor_copy(oT[:, it % 2, :], ps[:, 7, :]).then_inc(o_copied, 1)

                def finish_item(it):
                    g, c = items[it]
                    dve.wait_ge(o_turned, ITEMS * i + it + 1)
                    o4 = ps[:, 6, :].rearrange("p (t h c) -> p t h c", t=CT, h=HG)
                    if it > 0:
                        dve.wait_ge(o_normed, ITEMS * i + it)
                    dve.reciprocal(rden[:, :, :], o4[:, :, :, DK]).then_inc(o_rden, 1)
                    dve.wait_ge(o_rden, ITEMS * i + it + 1)
                    dve.tensor_tensor(
                        attn[:, CT * c:CT * c + CT,
                             bass.ds(2 * HG * DK * i + HG * DK * g, HG * DK)].rearrange("p t (h c) -> p t h c", h=HG),
                        o4[:, :, :, 0:DK], rden[:, :, :].unsqueeze(3).to_broadcast([P, CT, HG, DK]), ALU.mult)\
                       .then_inc(o_normed, 1)

                maxima(0, range(len(pieces(0))))
                subtract_rows(0)
                for it in range(ITEMS):
                    for k in range(CT * (items[it][1] + 1)):
                        if k == 2 and it > 0:
                            finish_item(it - 1)
                        maxima(it + 1, hosted(it, k))
                    if it + 1 < ITEMS:
                        subtract_rows(it + 1)
                    copy_item(it)
                finish_item(ITEMS - 1)

            for t in range(CH):
                dve.wait_ge(y_mm, t + 1)
                xc = X[:, CT * t:CT * t + CT, :]
                dve.tensor_tensor(xc, ps[:, 2 + t % 2, :].rearrange("p (t d) -> p t d", t=CT), xc, ALU.add)\
                   .then_inc(y_read, 1)
                dve.wait_ge(y_read, t + 1)
                stats_of(CH + t, x_row(t))
                if t >= 1:
                    normalise(CH + t - 1, t - 1, x_row(t - 1), nrm_row(t - 1), nrm_ready)
            normalise(2 * CH - 1, CH - 1, x_row(CH - 1), nrm_row(CH - 1), nrm_ready)

            for t in range(CH):
                dve.wait_ge(conv_first, t + 1)
                dve.wait_ge(hT_ready, CH + min(t + 2, CH))
                xm = cT[:, t % 2, :]
                link(dve.scalar_tensor_tensor(xm, hT[:, 1, CW * t:CW * t + CW], mixc[:, 0:1], xm, ALU.mult, ALU.add))
                dve.scalar_tensor_tensor(xm, hT[:, 1, CW * t + 2:CW * t + 2 + CW], mixc[:, 2:3], xm,
                                         ALU.mult, ALU.add).then_inc(conv_ready, 1)
                dve.wait_ge(sc_mm, t + 1)
                s9 = ps[:, 7, 0:CT * NP].rearrange("p (t k) -> p t k", t=CT)
                wide = [P, CT, NP]
                link(dve.tensor_reduce(top9[:, :], s9, AX.X, ALU.max))
                link(dve.tensor_tensor(eq9[:, :, :], s9, top9[:, :].unsqueeze(2).to_broadcast(wide), ALU.is_equal))
                link(dve.tensor_tensor(eq9[:, :, :], eq9[:, :, :], rank9[:, :, :], ALU.mult))
                link(dve.tensor_reduce(best9[:, :], eq9[:, :, :], AX.X, ALU.max))
                dve.tensor_tensor(hot9[:, :, 0:NP], eq9[:, :, :], best9[:, :].unsqueeze(2).to_broadcast(wide),
                                  ALU.is_equal).then_inc(hot_ready, 1)
                dve.wait_ge(hot_turned, t + 1)
                dve.tensor_copy(hotT[:, :], hps[0:NP, CW:2 * CW]).then_inc(hot_copied, 1)
                dve.tensor_copy(hotTf[:, :], hps[0:NP, CW:2 * CW]).then_inc(hot_copied, 1)
                dve.wait_ge(mask_mm, t + 1)
                dve.wait_ge(hid_ready, NG * (t + 1))
                for g in range(NG):
                    ins = dve.tensor_tensor(hsel[:, g, :], hid[:, g, :], ps[0:GR, 3 + g, :], ALU.mult)
                ins.then_inc(hsel_ready, 1)
                dve.wait_ge(ffn_mm, t + 1)

                def f_row(i):
                    return ps[:, 6, P * i:P * i + P]

                stats_of(2 * CH + 2 * t, f_row)
                normalise(2 * CH + 2 * t, t, f_row, lambda i: tmp[:, i, :], None)
                four = [P, CT, D]
                link(dve.tensor_tensor(tmp, tmp, gbg[:, 0:1, :].to_broadcast(four), ALU.mult))
                link(dve.tensor_tensor(tmp, tmp, gbg[:, 1:2, :].to_broadcast(four), ALU.add))
                xc = X[:, CT * t:CT * t + CT, :]
                dve.tensor_tensor(xc, xc, tmp, ALU.add).then_inc(ffn_read, 1)
                dve.wait_ge(ffn_read, t + 1)
                stats_of(2 * CH + 2 * t + 1, x_row(t))
                normalise(2 * CH + 2 * t + 1, t, x_row(t), nrm_row(t), nrm_ready)

            def feature(n):
                dve.wait_ge(f_exp, n + 1)
                if n >= 2:
                    dve.wait_ge(s_mm, n - 1)
                dve.scalar_tensor_tensor(feat[:, n % 2, :, :], ps[:, 2 + 2 * (n % 2):4 + 2 * (n % 2), :],
                                         1.0, expq[:, n % 2, :, :], ALU.add, ALU.max).then_inc(f_ready, 1)

            def same_block(n):
                dve.wait_ge(s_mm, n + 1)
                if n >= 2:
                    dve.wait_ge(av_mm, n - 1)
                dve.tensor_tensor(
                    am[:, n % 2, :].rearrange("p (t q) -> p t q", t=CT),
                    ps[:, 6, :].rearrange("p (t q) -> p t q", t=CT),
                    blockmask[:, :].unsqueeze(1).to_broadcast([P, CT, P]), ALU.mult).then_inc(s_ready, 1)

            def divide(t, g):
                dve.wait_ge(av_mm, H1 * t + HH * g + HH)
                o = ps[:, 1 + 6 * g, 0:CT * HH * (HD + 1)].rearrange("p (t h c) -> p t h c", t=CT, h=HH)
                link(dve.tensor_scalar(den1[:, :, :], o[:, :, :, HD], 1e-8, None, ALU.add))
                link(dve.reciprocal(den1[:, :, :], den1[:, :, :]))
                if t >= 1:
                    dve.wait_ge(on_turned, t)
                dve.tensor_tensor(
                    on[:, :, HH * HD * g:HH * HD * g + HH * HD].rearrange("p t (h d) -> p t h d", h=HH),
                    o[:, :, :, 0:HD], den1[:, :, :].unsqueeze(3).to_broadcast([P, CT, HH, HD]), ALU.mult)\
                   .then_inc(on_ready, 1)

            def residual(t):
                dve.wait_ge(y1_mm, t + 1)
                xc = X[:, CT * t:CT * t + CT, :]
                dve.tensor_tensor(xc, ps[:, 0, :].rearrange("p (t d) -> p t d", t=CT), xc, ALU.add)\
                   .then_inc(y1_read, 1)
                dve.wait_ge(y1_read, t + 1)
                stats_of(4 * CH + t, x_row(t))

            wide = [P, CT, E]

            def over(r, at):
                return red[:, r, at].unsqueeze(2).to_broadcast(wide)

            def shift_logits(t):
                at = slice(CT * t, CT * t + CT)
                dve.wait_ge(lg_mm, t + 1)
                logits = ps[:, 0, 0:CT * E].rearrange("p (t e) -> p t e", t=CT)
                link(dve.tensor_reduce(red[:, 0, at], logits, AX.X, ALU.max))
                dve.tensor_tensor(lg[:, at, :], logits, over(0, at), ALU.subtract).then_inc(r_shift, 1)

            def choose(t):
                at = slice(CT * t, CT * t + CT)
                dve.wait_ge(r_exped, t + 1)
                link(dve.tensor_reduce(red[:, 1, at], gates[:, at, :], AX.X, ALU.add))
                link(dve.reciprocal(red[:, 2, at], red[:, 1, at]))
                link(dve.tensor_tensor(gates[:, at, :], gates[:, at, :], over(2, at), ALU.mult))
                src = gates[:, at, :]
                for k in range(2):
                    link(dve.tensor_reduce(wsel[:, k, at], src, AX.X, ALU.max))
                    link(dve.tensor_tensor(sel[:, k, at, :], src, wsel[:, k, at].unsqueeze(2).to_broadcast(wide),
                                           ALU.is_equal))
                    link(dve.tensor_tensor(sel[:, k, at, :], sel[:, k, at, :], rank8[:, at, :], ALU.mult))
                    link(dve.tensor_reduce(red[:, 3 + k, at], sel[:, k, at, :], AX.X, ALU.max))
                    link(dve.tensor_tensor(hot[:, k, at, :], sel[:, k, at, :], over(3 + k, at), ALU.is_equal))
                    if k == 0:
                        link(dve.scalar_tensor_tensor(lg[:, at, :], hot[:, 0, at, :], -2.0, src, ALU.mult, ALU.add))
                        src = lg[:, at, :]
                dve.tensor_tensor(chosen[:, at, 0:E], hot[:, 0, at, :], hot[:, 1, at, :], ALU.add).then_inc(r_mask, 1)

            def slots(t):
                at = slice(CT * t, CT * t + CT)
                dve.wait_ge(pos_mm, t + 1)
                place = ps[:, 0, 0:CT * (E + 1)].rearrange("p (t e) -> p t e", t=CT)
                dve.tensor_copy(nrm[:, at, D:D + 2], wsel[:, :, at].rearrange("p k t -> p t k"))
                dve.tensor_copy(nrm[:, at, D + 2:D + 3], place[:, :, E:E + 1])
                dve.tensor_copy(nrm[:, at, D + 3], red[:, 3, at])
                both = red[:, 5:7, at]
                link(dve.tensor_tensor(sel[:, :, at, :], hot[:, :, at, :],
                                       place[:, :, 0:E].unsqueeze(1).to_broadcast([P, 2, CT, E]), ALU.mult))
                link(dve.tensor_reduce(both, sel[:, :, at, :], AX.X, ALU.add))
                link(dve.tensor_scalar(red[:, 7:9, at], red[:, 3:5, at], float(-CAP), float(E * CAP - 1),
                                       ALU.mult, ALU.add))
                link(dve.tensor_scalar(red[:, 9:11, at], both, float(CAP), float(SLOTS), ALU.is_gt, ALU.mult))
                link(dve.tensor_tensor(slotf[:, :, at], red[:, 7:9, at], both, ALU.add))
                link(dve.tensor_tensor(slotf[:, :, at], slotf[:, :, at], red[:, 9:11, at], ALU.add))
                dve.tensor_copy(slot_w[:, :, at], slotf[:, :, at]).then_inc(slots_ready, 1)

            def between(t, h):
                if h == 0 and t >= 2:
                    shift_logits(t - 2)
                if h == 0 and 1 <= t <= CH:
                    divide(t - 1, 1)
                if h == 1 and t >= 2:
                    choose(t - 2)
                if h == 3 and 1 <= t <= CH:
                    residual(t - 1)
                if h == 6 and t >= 2:
                    slots(t - 2)
                if h == 5 and 1 <= t <= CH:
                    normalise(4 * CH + t - 1, t - 1, x_row(t - 1), nrm_row(t - 1), nrm_ready)
                if h == 5 and t < CH:
                    divide(t, 0)

            feature(0)
            for t in range(CH + 2):
                for h in range(H1):
                    if t < CH:
                        same_block(H1 * t + h)
                        if H1 * t + h + 1 < H1 * CH:
                            feature(H1 * t + h + 1)
                    between(t, h)

            for s in slots_loaded:
                dve.wait_ge(s, 16 * 2)
            dve.wait_ge(consts, 4)
            wide3 = [P, E, ET]
            w_a, w_b, number, rank = (slotrows[:, :, :, D + n] for n in range(META))
            first, second = smeta[:, 0, :, :], smeta[:, 1, :, :]
            link(dve.tensor_tensor(first, rank, rank8[:, 0, :].unsqueeze(2).to_broadcast(wide3), ALU.is_equal))
            link(dve.tensor_scalar(second, first, -1.0, 1.0, ALU.mult, ALU.add))
            link(dve.tensor_tensor(smeta[:, 2, :, :], first, w_a, ALU.mult))
            link(dve.tensor_tensor(smeta[:, 3, :, :], second, w_b, ALU.mult))
            link(dve.tensor_tensor(smeta[:, 2, :, :], smeta[:, 2, :, :], smeta[:, 3, :, :], ALU.add))
            link(dve.tensor_scalar(second, second, float(S), -1.0, ALU.mult, ALU.add))
            link(dve.tensor_tensor(second, second, number, ALU.add))
            link(dve.tensor_scalar(smeta[:, 4, :, :], number, 0.0, float(2 * S), ALU.is_equal, ALU.mult))
            link(dve.tensor_tensor(smeta[:, 5, :, :], second, smeta[:, 4, :, :], ALU.add))
            dve.tensor_copy(to_row[:, :, :], smeta[:, 5, :, :]).then_inc(meta_ready, 1)
            weight = smeta[:, 2, :, :]

            for e in range(E):
                dve.wait_ge(e2_mm, e + 1)
                if e >= 2:
                    dve.wait_ge(eo_sent[e % 2], 16 * ET * (e // 2))
                for n in range(ET):
                    m = min(P, CAP - P * n)
                    ins = dve.tensor_scalar(eo[0:m, e % 2, n, :], ps[0:m, 6 + e % 2, P * n:P * n + P],
                                            weight[0:m, e, n:n + 1], None, ALU.mult)
                ins.then_inc(eo_ready, 1)
            for t in range(CH):
                dve.wait_ge(picked_loaded[t], 16 * 2)
                at = slice(CT * t, CT * t + CT)
                gc = gath[:, 0, at, :]
                link(dve.tensor_tensor(gc, gc, gath[:, 1, at, :], ALU.add))
                link(dve.tensor_tensor(gc, gc, gate[:, 3:4, :].to_broadcast([P, CT, D]), ALU.mult))
                xc = X[:, at, :]
                dve.tensor_tensor(xc, xc, gc, ALU.add).then_inc(out_ready, 1)

        @block.tensor
        def _(pe):
            def mm(o, lhsT, rhs, start=True, stop=True):
                return pe.matmul(o, lhsT, rhs, start=start, stop=stop, skip_group_check=True)

            pe.wait_ge(silu_ready, 2)
            for l in range(2):
                for n, which in enumerate((0, 1, 3, 4)):
                    mm(ps[:, 7, 4 * l + n:4 * l + n + 1], wmod[:, l, D * which:D * which + D], scol[:, l:l + 1])
                for n, which in enumerate((2, 5)):
                    ins = mm(ps[:, 6, D * (2 * l + n):D * (2 * l + n) + D], smat[:, l, :],
                             wmod[:, l, D * which:D * which + D])
            ins.then_inc(mod_mm, 1)

            def turn(m, t, bank):
                pe.wait_ge(nrm_ready, CH * m + t + 1)
                for i in range(CT):
                    ins = pe.transpose(ps[:, bank, P * i:P * i + P], nrm[:, CT * t + i, 0:D], identf[:, :])
                ins.then_inc(tposed, 1)

            pe.wait_ge(consts, 1)
            turn(0, 0, 0)
            pe.wait_ge(w_loaded, 16 * 4)
            for t in range(CH):
                if t + 1 < CH:
                    if t >= 1:
                        pe.wait_ge(hT_ready, t)
                    turn(0, t + 1, (t + 1) % 2)
                pe.wait_ge(hT_ready, t + 1)
                rows = hT[:, 0, 1 + CW * t:1 + CW * t + CW]
                for k in range(2):
                    if t >= 1:
                        pe.wait_ge(qk_rest, 2 * t + k - 1)
                    mm(ps[:, 2 + k, :], wq[:, k, :], rows).then_inc(qk_mm, 1)
                if t >= 1:
                    pe.wait_ge(v_ready, t)
                for i in range(CT):
                    ins = mm(ps[:, 4, P * i:P * i + P], rows[:, P * i:P * i + P], wq[:, 2, :])
                ins.then_inc(v1_mm, 1)

            pe.wait_ge(w2_loaded, 16 * 20)
            pe.wait_ge(qk_rest, 2 * CH)
            pe.wait_ge(v_ready, CH)
            for g in range(2 * H1 // 4):
                for n in range(4 * g, 4 * g + 4):
                    ins = mm(ps[:, g, P * (n % 4):P * (n % 4) + P], wqkv16[:, n, :], proj_s[:, n % H1, :])
                ins.then_inc(fold_mm, 1)
            pe.transpose(ps[:, 4, 0:P], wvrow[:, :], identf[:, :])
            pe.transpose(ps[:, 4, P:2 * P], woutr, identf[:, :]).then_inc(fold_mm, 1)
            pe.wait_ge(fold_ready, 10)

            pieces_reg = nc.alloc_register(pe.engine, "pieces_before")
            heads_reg = nc.alloc_register(pe.engine, "heads_before")
            with pe.Fori(0, GROUPS // 2) as i:
                pe.reg_mov(pieces_reg, A_TOTAL * i)
                pe.reg_mov(heads_reg, HG * UNITS * i)
                pieces_before = pe.snap(pieces_reg, min_val=0, max_val=A_TOTAL)
                heads_before = pe.snap(heads_reg, min_val=0, max_val=HG * UNITS)

                def score_piece(it, n):
                    g, c, qi, j, kc = pieces(it)[n]
                    a = a_start[it] + n
                    w = CW if kc < c else P * (qi + 1)
                    if a >= 3:
                        pe.wait_ge(a_maxed, pieces_before + a - 2)
                    o = ps[:, 3 + a % 3, 0:w]
                    ins = mm(o, QS[0:ROWS, g, j, P * (CT * c + qi):P * (CT * c + qi) + P],
                             KS[0:ROWS, g, j, CW * kc:CW * kc + w], True, kc < c)
                    if kc == c:
                        ins = mm(o[:, w - P:w], identb[:, :], causal[:, :], False, True)
                    ins.then_inc(a_ready, 1)

                def turn_maxima(it):
                    pe.wait_ge(m_parts, ITEMS * i + it + 1)
                    if it >= 2:
                        pe.wait_ge(o_normed, ITEMS * i + it - 1)
                    for qi in range(CT):
                        ins = pe.transpose(mps[ROWS:ROWS + 2 * HG, P * qi:P * qi + P],
                                           mhl[:, qi, :, :].rearrange("p h c -> p (h c)"), identb[:, :])
                    ins.then_inc(m_turned, 1)

                def scores(u, j):
                    it, kb = units[u]
                    g, c = items[it]
                    off = P * max(0, kb - CT * c)
                    n = HG * u + j
                    if n >= 3:
                        pe.wait_ge(b_exped, heads_before + n - 2)
                    mm(ps[:, n % 3, off:CW], KS[0:ROWS + 2 * HG, g, j, P * kb:P * kb + P],
                       QS[0:ROWS + 2 * HG, g, j, CW * c + off:CW * c + CW]).then_inc(b_ready, 1)

                def values(u, j):
                    it, kb = units[u]
                    g, c = items[it]
                    off = P * max(0, kb - CT * c)
                    if u == last_unit[it]:
                        pe.wait_ge(b_exped, heads_before + HG * u + j + 1)
                    if j == 0:
                        if u in diag_no:
                            pe.wait_ge(diag_cut, DIAGS * i + diag_no[u] + 1)
                        if kb == 0 and it > 0:
                            pe.wait_ge(o_copied, ITEMS * i + it)
                    ins = mm(ps[32 * j:32 * j + 32, 7, off:CW], Vg[:, g, kb, j, :], pT[:, u % 3, j, off:CW],
                             kb == 0, kb == CT * c + CT - 1)
                    if j == HG - 1:
                        ins.then_inc(pv_done, 1)

                def turn_item(it):
                    pe.wait_ge(o_copied, ITEMS * i + it + 1)
                    pe.wait_ge(m_rows, ITEMS * i + min(it + 2, ITEMS))
                    for q in range(CT):
                        ins = pe.transpose(ps[:, 6, P * q:P * q + P], oT[:, it % 2, P * q:P * q + P], identf[:, :])
                        if q == 0 and it == CH - 1:
                            ins.then_inc(heads_free[0], 1)
                    ins.then_inc(o_turned, 1)

                for b in range(2):
                    pe.wait_ge(heads_loaded[b], 16 * 12 * i + 16 * (HG + 12))
                    pe.wait_ge(vg_ready, 2 * i + b + 1)
                    if b == 0:
                        for n in range(len(pieces(0))):
                            score_piece(0, n)
                        turn_maxima(0)
                    for it in range(CH * b, CH * b + CH):
                        if b == 0 and it == CH - 1:
                            pe.wait_ge(heads_loaded[1], 16 * 12 * i + 16 * (HG + 12))
                        first = units.index((it, 0))
                        nu = CT * (items[it][1] + 1)
                        pe.wait_ge(m_rows, ITEMS * i + it + 1)
                        for k in range(nu):
                            if k == 2 and it > 0:
                                turn_item(it - 1)
                            steps = [(scores, first + k, j) for j in range(HG)]
                            if k >= 1:
                                steps += [(values, first + k - 1, j) for j in range(HG)]
                            hs = hosted(it, k)
                            for n, (what, u, j) in enumerate(steps):
                                what(u, j)
                                for h in hs[len(hs) * n // len(steps):len(hs) * (n + 1) // len(steps)]:
                                    score_piece(it + 1, h)
                        if it + 1 < ITEMS:
                            turn_maxima(it + 1)
                        for j in range(HG):
                            values(first + nu - 1, j)
                turn_item(ITEMS - 1)
                pe.wait_ge(o_normed, ITEMS * i + ITEMS)
                pe.transpose(mps[0:2 * HG, 0:P], mhl[:, 0, :, :].rearrange("p h c -> p (h c)"), identb[:, :])\
                  .then_inc(heads_free[1], 1)

            def turn_attn(t):
                for i in range(CT):
                    ins = pe.transpose(ps[:, t % 2, P * i:P * i + P], attn[:, CT * t + i, :], identf[:, :])
                ins.then_inc(at_turned, 1)

            pe.wait_ge(o_normed, ITEMS * (GROUPS // 2))
            turn_attn(0)
            for t in range(CH):
                if t + 1 < CH:
                    if t >= 1:
                        pe.wait_ge(at_ready, t)
                    turn_attn(t + 1)
                pe.wait_ge(at_ready, t + 1)
                if t >= 2:
                    pe.wait_ge(y_read, t - 1)
                for i in range(CT):
                    ins = mm(ps[:, 2 + t % 2, P * i:P * i + P], cT[:, t % 2, P * i:P * i + P], wog[:, :])
                ins.then_inc(y_mm, 1)
                if t >= 1:
                    if t >= 3:
                        pe.wait_ge(hT_ready, CH + t - 2)
                    turn(1, t - 1, 4 + (t - 1) % 2)
            pe.wait_ge(hT_ready, CH + 2)
            turn(1, CH - 1, 4 + (CH - 1) % 2)

            pe.wait_ge(consts, 2)
            for t in range(CH):
                xm = cT[:, t % 2, :]
                pe.wait_ge(conv_ready, t + 1)
                if t == 0:
                    pe.wait_ge(hT_ready, 2 * CH)
                if t >= 1:
                    pe.wait_ge(hot_copied, 2 * t)
                mm(ps[0:DM, 7, :], wo1[:, :], xm).then_inc(u_mm, 1)
                if t >= 1:
                    pe.wait_ge(hid_ready, NG * t)
                for g in range(NG):
                    ins = mm(ps[0:GR, g, :], w1s[:, PG * g:PG * g + PG, :].rearrange("p a m -> p (a m)"), xm)
                ins.then_inc(hid_mm, 1)
                pe.wait_ge(t_ready, t + 1)
                for i in range(CT):
                    ins = mm(ps[:, 7, NP * i:NP * i + NP], taug[:, P * i:P * i + P], wo2[:, :])
                ins.then_inc(sc_mm, 1)
                pe.wait_ge(hot_ready, t + 1)
                for i in range(CT):
                    ins = pe.transpose(hps[0:16, CW + P * i:CW + P * i + P], hot9[:, i, :], identb[:, :])
                ins.then_inc(hot_turned, 1)
                pe.wait_ge(hot_copied, 2 * t + 2)
                if t >= 1:
                    pe.wait_ge(hsel_ready, t)
                for g in range(NG):
                    ins = mm(ps[0:GR, 3 + g, :], spread[:, PG * g:PG * g + PG, :].rearrange("p a m -> p (a m)"),
                             hotT[:, :])
                ins.then_inc(mask_mm, 1)
                pe.wait_ge(hsel_ready, t + 1)
                if t >= 1:
                    pe.wait_ge(ffn_read, t)
                for i in range(CT):
                    o = ps[:, 6, P * i:P * i + P]
                    s_ = slice(P * i, P * i + P)
                    mm(o, hT[:, 1, 1 + CW * t + P * i:1 + CW * t + P * i + P], identf[:, :], True, False)
                    mm(o, hotTf[:, s_], b2s[:, :], False, False)
                    for g in range(NG):
                        ins = mm(o, hsel[:, g, s_], w2s[:, g, :], False, g == NG - 1)
                ins.then_inc(ffn_mm, 1)

            def turn2(which, t):
                pe.wait_ge(nrm_ready, CH * (2 + which) + t + 1)
                for i in range(CT):
                    ins = pe.transpose(ps[:, 0, P * i:P * i + P], nrm[:, CT * t + i, 0:D], identf[:, :])
                ins.then_inc(turned2[which], 1)

            def project_values(t):
                pe.wait_ge(hT2_ready[0], t + 1)
                rows = hT[:, 0, 1 + CW * t:1 + CW * t + CW]
                for i in range(CT):
                    ins = mm(ps[:, 0, P * i:P * i + P], rows[:, P * i:P * i + P], wvT[:, :])
                ins.then_inc(v2_mm, 1)

            def features(n):
                t, h = n // H1, n % H1
                if h == 0:
                    pe.wait_ge(hT2_ready[0], t + 1)
                if n >= 2:
                    pe.wait_ge(f_ready, n - 1)
                for k in range(2):
                    ins = mm(ps[:, 2 + 2 * (n % 2) + k, :], pfold[:, H1 * k + h, :],
                             hT[:, 0, 1 + CW * t:1 + CW * t + CW])
                ins.then_inc(f_mm, 1)

            def block_scores(n):
                pe.wait_ge(f_ready, n + 1)
                if n >= 1:
                    pe.wait_ge(s_ready, n)
                for i in range(CT):
                    s_ = slice(P * i, P * i + P)
                    ins = mm(ps[:, 6, s_], feat[:, n % 2, 1, s_], feat[:, n % 2, 0, s_])
                ins.then_inc(s_mm, 1)

            def block_values(n):
                t, h = n // H1, n % H1
                g = h // HH
                pe.wait_ge(s_ready, n + 1)
                if h == 0:
                    pe.wait_ge(v2_ready, t + 1)
                if h % HH == 0 and t >= 1:
                    pe.wait_ge(on_ready, 2 * (t - 1) + g + 1)
                for i in range(CT):
                    at = (HD + 1) * (HH * i + h % HH)
                    ins = mm(ps[:, 1 + 6 * g, at:at + HD + 1], am[:, n % 2, P * i:P * i + P], vone[:, t % 2, i, h, :])
                ins.then_inc(av_mm, 1)

            def between(t, h):
                if h == 0 and t >= 2:
                    pe.wait_ge(hT2_ready[1], t - 1)
                    for i in range(CT):
                        n = CT * (t - 2) + i
                        o = ps[:, 0, E * i:E * i + E]
                        mm(o, hT[:, 1, 1 + P * n:1 + P * n + P], rw[:, :], True, False)
                        ins = mm(o, onesf[0:1, :], rb[:, :], False, True)
                    ins.then_inc(lg_mm, 1)
                if h == 1 and 1 <= t <= CH:
                    pe.wait_ge(on_ready, 2 * t)
                    if t == 1:
                        pe.wait_ge(v2_ready, 2)
                    else:
                        pe.wait_ge(r_shift, t - 1)
                    for i in range(CT):
                        ins = pe.transpose(ps[:, 0, P * i:P * i + P], on[:, i, :], identf[:, :])
                    ins.then_inc(on_turned, 1)
                if h == 3 and 1 <= t <= CH:
                    pe.wait_ge(onT_ready, t)
                    for i in range(CT):
                        o = ps[:, 0, P * i:P * i + P]
                        mm(o, onT[:, P * i:P * i + P], woutT[:, :], True, False)
                        ins = mm(o, onesf[0:1, :], browg[:, :], False, True)
                    ins.then_inc(y1_mm, 1)
                if h == 4 and t + 1 < CH:
                    if t >= 1:
                        pe.wait_ge(y1_read, t)
                    turn2(0, t + 1)
                if h == 5 and t + 1 < CH:
                    project_values(t + 1)
                if h == 6 and t >= 2:
                    n0 = CT * (t - 2)
                    pe.wait_ge(r_mask, t - 1)
                    if t + 1 < CH:
                        pe.wait_ge(v2_ready, t + 2)
                    elif t <= CH:
                        pe.wait_ge(y1_read, t)
                    o = ps[:, 0, 0:CT * (E + 1)]
                    ch = chosen[:, n0:n0 + CT, :].rearrange("p t e -> p (t e)")
                    ins = mm(o, upto[:, :], ch, True, False)
                    for k in range(1, CT):
                        ins = mm(o[:, (E + 1) * k:], onesb[:, :], ch[:, 0:(E + 1) * (CT - k)], False,
                                 k == CT - 1 and n0 == 0)
                    for n in range(n0):
                        ins = mm(o.rearrange("p (t e) -> p t e", t=CT), onesb[:, :],
                                 chosen[:, n:n + 1, :].to_broadcast([P, CT, E + 1]), False, n == n0 - 1)
                    ins.then_inc(pos_mm, 1)
                if h == 7 and 1 <= t <= CH:
                    if t == 1:
                        pe.wait_ge(v2_ready, t + 2)
                    else:
                        pe.wait_ge(slots_ready, t - 1)
                    turn2(1, t - 1)

            pe.wait_ge(ffn_read, CH)
            turn2(0, 0)
            project_values(0)
            features(0)
            features(1)
            for t in range(CH + 2):
                for h in range(H1):
                    n = H1 * t + h
                    if n < H1 * CH:
                        block_scores(n)
                    if n + 2 < H1 * CH:
                        features(n + 2)
                    if 1 <= n <= H1 * CH:
                        block_values(n - 1)
                    between(t, h)

            for e in range(E):
                pe.wait_ge(slots_loaded[e], 16 * 2)
                if e >= 2:
                    pe.wait_ge(xs_ready, e - 1)
                for n in range(ET):
                    m = min(P, CAP - P * n)
                    ins = pe.transpose(ps[:, e % 2, P * n:P * n + m], slotrows[0:m, e, n, 0:D], identf[0:m, 0:m])
                ins.then_inc(xs_turned, 1)
            pe.wait_ge(ex_loaded, 32)

            def expert_up(e):
                pe.wait_ge(xs_ready, e + 1)
                for c in range(HC):
                    if e >= 1:
                        pe.wait_ge(gelu_ready, HC * (e - 1) + c + 1)
                    mm(ps[:, 2 + c, 0:CAP], ew1s[:, e, P * c:P * c + P], xsT[:, CAP * e:CAP * e + CAP])\
                        .then_inc(e1_mm, 1)

            def expert_down(e):
                pe.wait_ge(gelu_ready, HC * (e + 1))
                if e >= 2:
                    pe.wait_ge(eo_ready, e - 1)
                for s_ in range(ET):
                    m = min(P, CAP - P * s_)
                    o = ps[0:m, 6 + e % 2, P * s_:P * s_ + P]
                    for c in range(HC):
                        mm(o, gT[:, e % 2, c, P * s_:P * s_ + m], ew2s[:, e, c, :], c == 0, False)
                    ins = mm(o, onesf[0:1, 0:m], eb2r[:, e, :], False, True)
                ins.then_inc(e2_mm, 1)

            expert_up(0)
            for e in range(E):
                if e + 1 < E:
                    expert_up(e + 1)
                expert_down(e)


_INS = ['L0_attn_x', 'L0_attn_WQ', 'L0_attn_WK', 'L0_attn_WV', 'L0_attn_WO', 'L0_ffn_mix_kernel', 'L0_ffn_W1',
        'L0_ffn_b1', 'L0_ffn_W2', 'L0_ffn_b2', 'L0_ffn_Wo1', 'L0_ffn_bo1', 'L0_ffn_Wo2', 'L0_ffn_bo2',
        'L0_ffn_gamma', 'L0_ffn_beta', 'L0_c', 'L0_wmod', 'w_qkv_heads', 'w_v', 'L1_attn_w_out', 'L1_attn_b_out',
        'L1_attn_proj', 'L1_ffn_router_w', 'L1_ffn_router_b', 'L1_ffn_w1', 'L1_ffn_b1', 'L1_ffn_w2',
        'L1_ffn_b2', 'L1_c', 'L1_wmod']


def _laid_out(a):
    import numpy as np

    a = {n: np.asarray(v) for n, v in a.items()}
    a['L0_ffn_mix_kernel'] = a['L0_ffn_mix_kernel'].T
    a['L0_ffn_W1'] = a['L0_ffn_W1'].transpose(1, 0, 2)
    a['L0_ffn_b1'] = a['L0_ffn_b1'].reshape(3, 96).T
    a['L0_ffn_W2'] = a['L0_ffn_W2'].reshape(3, 96, 128).transpose(1, 0, 2)
    w = a.pop('L1_attn_w_qkv')
    a['w_qkv_heads'] = w.reshape(24, 16, 128).transpose(1, 0, 2)
    a['w_v'] = w[256:]
    a['L1_attn_proj'] = a['L1_attn_proj'].transpose(1, 0, 2)
    a['L1_ffn_w1'] = a['L1_ffn_w1'].transpose(1, 0, 2)
    a['L1_ffn_b1'] = a['L1_ffn_b1'].reshape(8, 4, 128).transpose(2, 0, 1)
    a['L1_ffn_w2'] = a['L1_ffn_w2'].reshape(8, 4, 128, 128).transpose(2, 0, 1, 3)
    return a


_OUTS = [((1, 2048, 128), 'float32')]


def kernel(**inputs):
    import numpy as _np
    import concourse.bacc as _bacc
    from concourse import mybir as _mybir
    from concourse.bass_utils import run_bass_kernel_spmd as _run

    nc = _bacc.Bacc("TRN2", target_bir_lowering=False, num_devices=1)
    arrays, args = {}, []
    inputs = _laid_out(inputs)
    for name in _INS:
        a = _np.ascontiguousarray(inputs[name])
        arrays[f"in_{name}_dram"] = a
        args.append(nc.dram_tensor(f"in_{name}_dram", a.shape, _mybir.dt.from_np(a.dtype), kind="ExternalInput").ap())
    for i, (shape, dtype) in enumerate(_OUTS):
        dt = _mybir.dt.from_np(_np.dtype(dtype))
        args.append(nc.dram_tensor(f"out_{i}_dram", shape, dt, kind="ExternalOutput").ap())
    adaln_two_layers(nc, *args)
    r = _run(nc, [arrays], core_ids=[0])
    got = tuple(r.results[0][f"out_{i}_dram"] for i in range(len(_OUTS)))
    return got[0]
```

```python
from contextlib import ExitStack

import concourse.bass as bass
from concourse import mybir

P = 128
ALU = mybir.AluOpType
ACT = mybir.ActivationFunctionType
AX = mybir.AxisListType
F32 = mybir.dt.float32
BF16 = mybir.dt.bfloat16
I32 = mybir.dt.int32
U32 = mybir.dt.uint32
EPS = 1e-5
MASKED = -1e30


def adaln_two_layers(
    nc: bass.Bass, x, WQ, WK, WV, WO, mix_kernel, W1, b1, W2, b2, Wo1, bo1, Wo2, bo2, gamma, beta,
    c0, wmod0, w_qkv_heads, w_v, w_out, b_out, proj, router_w, router_b, ew1, eb1, ew2, eb2, c1, wmod1, out,
):
    S, D = x.shape[1], x.shape[2]
    TILES = S // P
    CH = 4
    CT = TILES // CH
    CW = CT * P
    H0, DK = 16, D // 16
    HG = 4
    GROUPS = H0 // HG
    ROWS = 96
    SCALE = float(DK) ** -0.5
    NP, DM = W1.shape[1], W1.shape[2]
    PG = 3
    NG = NP // PG
    GR = PG * DM
    HD, H1 = proj.shape[0], proj.shape[1]
    BLK = 32
    E, HID = ew1.shape[1], ew1.shape[2]
    HH = H1 // 2
    HC = HID // P
    CAP = max(1, -(-S * 5 // (E * 4)))
    SLOTS = E * CAP
    ET = -(-CAP // P)
    LAST = CAP - P * (ET - 1)
    META = 4
    assert 2 * H1 == 4 * CH and CH == 4
    assert SLOTS % P == 0 and D == P and TILES == CH * CT and LAST % 32 == 0

    ctx = ExitStack()
    with ctx:
        def sb(name, shape, dt=F32):
            return ctx.enter_context(nc.sbuf_tensor(name, shape, dt))

        def sem(name):
            return ctx.enter_context(nc.semaphore(name))

        qk_dram = nc.dram_tensor("qk_parts_dram", (2, H0, 3, DK, S), BF16, kind="Internal").ap()
        slot_in = nc.dram_tensor("slot_in_dram", (SLOTS, D + META), F32, kind="Internal").ap()
        picked = nc.dram_tensor("picked_dram", (2 * S, D), F32, kind="Internal").ap()

        ps = ctx.enter_context(nc.psum_tensor("ps", [P, 8, 512], F32))

        X = sb("X", [P, TILES, D])
        nrm = sb("nrm", [P, TILES, D + META])
        zeros = sb("zeros", [P, D + META])
        hT = sb("hT", [P, 2, S + 2])
        stats = sb("stats", [P, CT, 6])
        mv = sb("mv", [P, 2, CT, 2])
        ve = sb("ve", [P, 2, CT])
        rstd = sb("rstd", [P, 2, CT])
        cT = sb("cT", [P, 2, CW])
        identf = sb("identf", [P, P])
        identb = sb("identb", [P, P], BF16)
        onesf = sb("onesf", [P, P])
        onesb = sb("onesb", [P, P], BF16)
        causal = sb("causal", [P, P], BF16)
        blockmask = sb("blockmask", [P, P])
        upto = sb("upto", [P, P], BF16)
        spread = sb("spread", [NP, NP, DM], BF16)
        rank9 = sb("rank9", [P, CT, NP])
        rank8 = sb("rank8", [P, TILES, E])
        neghalf = sb("neghalf", [P, CT])
        onerow = hT[0:2, 1, 1:1 + S // 2].bitcast(BF16)
        ccol = sb("ccol", [P, 2])
        cexp = sb("cexp", [P, 2])
        cden = sb("cden", [P, 2])
        crec = sb("crec", [P, 2])
        scol = sb("scol", [P, 2])
        smat = sb("smat", [P, 2, P])
        wmod = sb("wmod", [P, 2, 6 * D])
        modc = sb("modc", [P, 2, 4])
        gate = sb("gate", [P, 4, D])
        wq = sb("wq", [P, 4, D])
        wog = sb("wog", [P, D])
        mixc = sb("mixc", [P, 3])
        w1s = sb("w1s", [P, NP, DM])
        b1c = sb("b1c", [GR, NG])
        w2s = sb("w2s", [GR + NP, NG, D])
        wo1 = sb("wo1", [P, DM])
        bo1c = sb("bo1c", [DM, 1])
        wo2 = sb("wo2", [DM + 1, NP])
        gb_rows = sb("gb_rows", [P, 2, D])
        gbg = sb("gbg", [P, 2, D])
        wvrow = sb("wvrow", [P, D])
        wvT = sb("wvT", [P, D])
        pfold = sb("pfold", [P, 2 * H1, P])
        woutT = sb("woutT", [P, D])
        brow = sb("brow", [P, D])
        browg = sb("browg", [P, D])
        rw = sb("rw", [P, E])
        rb = sb("rb", [P, E])
        eb1c = sb("eb1c", [P, E, HC])
        KS = sb("KS", [P, 2, HG, S], BF16)
        QS = sb("QS", [P, 2, HG, S], BF16)
        vtok = sb("vtok", [P, TILES, D])
        Vg = sb("Vg", [P, 2, TILES, HG, 32])
        pT = sb("pT", [P, 3, HG, CW])
        tmax = sb("tmax", [P, 2, CT * HG, CH])
        negm = sb("negm", [P, CT * HG])
        mhl = sb("mhl", [P, CT, HG, 2], BF16)
        rden = sb("rden", [P, CT, HG])
        den1 = sb("den1", [P, CT, HH])
        shared = sb("shared", [P, 8 * CW])
        parts = shared[:, 0:6 * CW].bitcast(BF16).rearrange(
            "p (a k b s) -> p a k b s", a=3, k=2, b=2)
        rest = shared[:, 6 * CW:8 * CW].rearrange("p (k s) -> p k s", k=2)
        oT = shared[:, 0:2 * CW].rearrange("p (b s) -> p b s", b=2)
        attn = shared[:, 2 * CW:6 * CW].rearrange("p (t d) -> p t d", t=TILES)
        taug = shared[0:DM + 1, 6 * CW:7 * CW]
        gsgn = rest[:, 0, :].rearrange("p (g d) -> p g d", g=4)
        gneg, gabs = (cT[:, b, :].rearrange("p (g d) -> p g d", g=4) for b in range(2))
        early = pT[:, :, :, :].rearrange("p a h s -> p (a h s)")
        wqkv16 = early[0:HD, 0:3 * H1 * D].rearrange("p (h d) -> p h d", h=3 * H1)
        proj_s = early[0:HD, 3 * H1 * D:4 * H1 * D].rearrange("p (h d) -> p h d", h=H1)
        woutr = early[:, 4 * H1 * D:4 * H1 * D + D]
        eq9 = sb("eq9", [P, CT, NP])
        top9 = sb("top9", [P, CT])
        best9 = sb("best9", [P, CT])
        hot9 = sb("hot9", [P, CT, 16], BF16)
        hotT = sb("hotT", [NP, 2, CW], BF16)

        KSf = KS[:, :, :, :].rearrange("p b h s -> p (b h s)").bitcast(F32)
        QSf = QS[:, :, :, :].rearrange("p b h s -> p (b h s)").bitcast(F32)
        assert H0 * S // 4 >= E * HC * D
        eb2b = attn[:, 0:E, :]
        attnT = pT[:, 0, :, :]
        hid = pT[0:GR, 0, 0:NG, :]
        hsel = pT[0:GR + NP, 1, 0:NG, :]
        fsum = pT[:, 2, 0:2, :].rearrange("p b (t d) -> p b t d", t=CT)
        expq = KSf[:, 0:2 * 2 * CW].rearrange("p (b k s) -> p b k s", b=2, k=2)
        feat = KSf[:, 2 * 2 * CW:4 * 2 * CW].rearrange("p (b k s) -> p b k s", b=2, k=2)
        am = pT[:, 0, 0:2, :]
        onT = pT[:, 0, 2, :]
        on = pT[:, 1, 0, :].rearrange("p (t d) -> p t d", t=CT)
        vgf = Vg[:, :, :, :, :].rearrange("p a t h c -> p (a t h c)")
        vone = vgf[:, SLOTS:SLOTS + 2 * CT * H1 * (HD + 1)].rearrange(
            "p (b t h c) -> p b t h c", b=2, t=CT, h=H1)
        ew1s = QSf[:, 0:E * HID].rearrange("p (e h) -> p e h", e=E)
        ew2s = QSf[:, E * HID:2 * E * HID].rearrange("p (e c d) -> p e c d", e=E, c=HC)

        x_loaded = [sem(f"x_loaded{i}") for i in range(CH)]
        mod_loaded = [sem(f"mod_loaded{i}") for i in range(3)]
        fold_loaded = sem("fold_loaded")
        w_loaded = sem("w_loaded")
        w2_loaded = sem("w2_loaded")
        ex_loaded = sem("ex_loaded")
        consts = sem("consts")
        pchain = sem("pchain")
        dchain = sem("dchain")
        achain = sem("achain")
        c_exp = sem("c_exp")
        silu_ready = sem("silu_ready")
        mod_mm = sem("mod_mm")
        mod_ready = sem("mod_ready")
        fold_mm = sem("fold_mm")
        fold_ready = sem("fold_ready")
        ve_ready = sem("ve_ready")
        rstd_ready = sem("rstd_ready")
        nrm_ready = sem("nrm_ready")
        tposed = sem("tposed")
        hT_ready = sem("hT_ready")
        qk_mm = sem("qk_mm")
        qk_hi = sem("qk_hi")
        qk_rest = sem("qk_rest")
        qk_mid = sem("qk_mid")
        qk_lo = sem("qk_lo")
        qk_stored = [sem(f"qk_stored{i}") for i in range(2)]
        v_ready = sem("v_ready")
        heads_loaded = [sem(f"heads_loaded{i}") for i in range(2)]
        last_chunk_loaded = sem("last_chunk_loaded")
        vg_ready = sem("vg_ready")
        heads_free = [sem(f"heads_free{i}") for i in range(2)]
        a_ready = sem("a_ready")
        a_maxed = sem("a_maxed")
        m_parts = sem("m_parts")
        m_turned = sem("m_turned")
        m_rows = sem("m_rows")
        m_neg = sem("m_neg")
        b_ready = sem("b_ready")
        b_exped = sem("b_exped")
        diag_cut = sem("diag_cut")
        pv_done = sem("pv_done")
        o_copied = sem("o_copied")
        o_turned = sem("o_turned")
        o_rden = sem("o_rden")
        o_normed = sem("o_normed")
        at_turned = sem("at_turned")
        at_ready = sem("at_ready")
        y_mm = sem("y_mm")
        y_read = sem("y_read")
        conv_first = sem("conv_first")
        conv_ready = sem("conv_ready")
        u_mm = sem("u_mm")
        t_ready = sem("t_ready")
        hid_mm = sem("hid_mm")
        hid_ready = sem("hid_ready")
        sc_mm = sem("sc_mm")
        hot_ready = sem("hot_ready")
        hot_turned = sem("hot_turned")
        hot_copied = sem("hot_copied")
        mask_mm = sem("mask_mm")
        hsel_ready = sem("hsel_ready")
        ffn_mm = sem("ffn_mm")
        ffn_copied = sem("ffn_copied")
        ffn_read = sem("ffn_read")
        v1_mm = sem("v1_mm")
        v2_mm = sem("v2_mm")
        v2_ready = sem("v2_ready")
        f_mm = sem("f_mm")
        f_exp = sem("f_exp")
        f_ready = sem("f_ready")
        s_mm = sem("s_mm")
        s_ready = sem("s_ready")
        av_mm = sem("av_mm")
        on_ready = sem("on_ready")
        on_turned = sem("on_turned")
        onT_ready = sem("onT_ready")
        turned2 = [sem(f"turned2_{i}") for i in range(2)]
        hT2_ready = [sem(f"hT2_ready{i}") for i in range(2)]
        y1_mm = sem("y1_mm")
        y1_read = sem("y1_read")
        bias_added = sem("bias_added")
        lg_mm = sem("lg_mm")
        r_exped = sem("r_exped")
        r_shift = sem("r_shift")
        r_mask = sem("r_mask")
        pos_mm = sem("pos_mm")
        slots_ready = sem("slots_ready")
        zero_filled = sem("zero_filled")
        scattered = sem("scattered")
        slots_loaded = [sem(f"slots_loaded{i}") for i in range(E)]
        meta_ready = sem("meta_ready")
        xs_turned = sem("xs_turned")
        xs_ready = sem("xs_ready")
        e1_mm = sem("e1_mm")
        gelu_ready = sem("gelu_ready")
        e2_mm = sem("e2_mm")
        eo_ready = sem("eo_ready")
        eo_sent = [sem(f"eo_sent{i}") for i in range(2)]
        picked_loaded = [sem(f"picked_loaded{i}") for i in range(CH)]
        out_ready = sem("out_ready")
        out_stored = sem("out_stored")

        lg = sb("lg", [P, TILES, E])
        gates = sb("gates", [P, TILES, E])
        red = sb("red", [P, 12, TILES])
        hot = sb("hot", [P, 2, TILES, E])
        sel = sb("sel", [P, 2, TILES, E])
        chosen = sb("chosen", [P, TILES, E + 1], BF16)
        slotf = sb("slotf", [P, 2, TILES])
        slot_w = sb("slot_w", [P, 2, TILES], U32)
        wsel = sb("wsel", [P, 2, TILES])
        smeta = sb("smeta", [P, 6, E, ET])
        to_row = sb("to_row", [P, E, ET], U32)
        slotrows = KSf[:, 4 * 2 * CW:4 * 2 * CW + E * ET * (D + META)].rearrange(
            "p (e t d) -> p e t d", e=E, t=ET)
        gath = KSf[:, 0:2 * TILES * D].rearrange("p (k t d) -> p k t d", k=2, t=TILES)
        xsT = vgf[:, 0:SLOTS]
        gT = pT[:, :, :, :].rearrange("p a h s -> p (a h s)")[:, 0:2 * HC * CAP].rearrange(
            "p (b c s) -> p b c s", b=2, c=HC)
        eo = oT[:, :, 0:ET * D].rearrange("p b (s d) -> p b s d", s=ET)

        RUNS = ([(0, 3)] * 3, [(0, 3), (1, 2), (0, 1), (2, 1), (0, 2)])
        pairs = list(zip(*[[p for a, n in runs for p in range(a, a + n)] for runs in RUNS]))
        assert sorted(pairs) == [(k, q) for k in range(3) for q in range(3)] and DK * len(pairs) <= ROWS
        LOADS = sum(len(runs) for runs in RUNS)

        def heads_there(g):
            return 16 * (HG + LOADS * (g // 2 + 1))

        items = [(0, c) for c in range(CH)] + [(g, c) for g in range(1, GROUPS) for c in reversed(range(CH))]
        ITEMS = len(items)
        units = [(it, kb) for it in range(ITEMS) for kb in range(CT * (items[it][1] + 1))]
        UNITS = len(units)
        first_unit = [units.index((it, 0)) for it in range(ITEMS)] + [UNITS]
        diag_no = {u: n for n, u in enumerate(u for u, (it, kb) in enumerate(units) if kb >= CT * items[it][1])}
        pieces = [(it, qi, j, kc) for it in range(ITEMS) for qi in range(CT) for j in range(HG)
                  for kc in range(items[it][1] + 1)]
        piece_end = [sum(CT * HG * (c + 1) for g, c in items[:it + 1]) for it in range(ITEMS)]

        LEAD = 3
        done_by = [0] * UNITS
        u0, n0 = 0, piece_end[0]
        while n0 < piece_end[-1]:
            slope, u1, n1 = max(((piece_end[it] - n0) / (first_unit[it] - LEAD - u0), first_unit[it] - LEAD,
                                 piece_end[it]) for it in range(ITEMS) if first_unit[it] - LEAD > u0)
            for u in range(u0, u1):
                done_by[u] = min(n1, n0 + int(-(-(n1 - n0) * (u + 1 - u0) // (u1 - u0))))
            u0, n0 = u1, n1
        for u in range(u0, UNITS):
            done_by[u] = n0

        def hosted(u):
            return range(done_by[u - 1] if u else piece_end[0], done_by[u])

        found = {u: [it for it in range(1, ITEMS) if piece_end[it] in range(hosted(u).start + 1, done_by[u] + 1)]
                 for u in range(UNITS)}
        turns = {u: [('output', it) for it in range(ITEMS - 1) if first_unit[it + 1] + 2 == u]
                 + [('maxima', it) for it in (found[u - 1] if u else [])] for u in range(UNITS)}
        turn_order = [('maxima', 0)] + [e for u in range(UNITS) for e in turns[u]] + [('output', ITEMS - 1)]
        assert all(len(f) < 2 for f in found.values())

        def pos_bank(t):
            return 0 if t < CH - 2 else 1

        mps = ps[:, 6, :].bitcast(BF16)
        hps = ps[:, 7, :].bitcast(BF16)

        block = ctx.enter_context(nc.Block())

        @block.sync
        def _(sp):
            def load(dst, src, s):
                sp.dma_start(dst, src).then_inc(s, 16)

            def row(v):
                return v.rearrange("(a n) -> a n", a=1)

            xt = x[0].rearrange("(t p) d -> p t d", p=P)
            def load_x(t):
                load(X[:, CT * t:CT * t + CT, :], xt[:, CT * t:CT * t + CT, :], x_loaded[t])

            load_x(0)
            load(ccol[:, 0:1], c0.rearrange("a d -> d a"), mod_loaded[0])
            load(ccol[:, 1:2], c1.rearrange("a d -> d a"), mod_loaded[0])
            load(wmod[:, 0, :], wmod0, mod_loaded[1])
            load_x(1)
            for i, w in enumerate((WQ, WK, WV, WO)):
                load(wq[:, i, :], w, w_loaded)
            load_x(2)
            load_x(3)
            load(wmod[:, 1, :], wmod1, mod_loaded[2])
            load(wqkv16[:, :, :], w_qkv_heads, fold_loaded)
            load(proj_s[:, :, :], proj, fold_loaded)
            load(wvrow[:, :], w_v, fold_loaded)
            load(woutr, w_out, fold_loaded)
            load(brow[:, :], row(b_out).to_broadcast([P, D]), fold_loaded)
            load(gb_rows[:, 0, :], row(gamma).to_broadcast([P, D]), fold_loaded)
            load(gb_rows[:, 1, :], row(beta).to_broadcast([P, D]), fold_loaded)

            def store_parts(t):
                for k in range(2):
                    sp.wait_ge(qk_lo, 2 * t + k + 1)
                    for a in range(3):
                        load(qk_dram[k, :, a, :, CW * t:CW * t + CW], parts[:, a, k, t % 2, :], qk_stored[t % 2])

            def load_heads(b, first, lo, hi, s):
                for k, dst in ((1, KS), (0, QS)):
                    at = 0
                    for a, n in RUNS[1 - k]:
                        src = qk_dram[k, first:first + HG, a:a + n, :, lo:hi].rearrange("j a d s -> (a d) j s")
                        load(dst[at:at + DK * n, b, :, lo:hi], src, s)
                        at += DK * n

            def load_ones(b):
                sp.wait_ge(heads_free[b], 1)
                for j in range(HG):
                    load(KS[ROWS + 2 * j:ROWS + 2 * j + 2, b, j, :], onerow[:, :], heads_loaded[b])

            for t in range(CH - 1):
                store_parts(t)
            load_ones(0)
            sp.wait_ge(qk_stored[0], 16 * 6 * 2)
            sp.wait_ge(qk_stored[1], 16 * 6)
            load_heads(0, 0, 0, CW * (CH - 1), heads_loaded[0])
            store_parts(CH - 1)
            sp.wait_ge(qk_stored[1], 16 * 6 * 2)
            load_heads(0, 0, CW * (CH - 1), S, last_chunk_loaded)
            load_ones(1)
            load_heads(1, HG, 0, S, heads_loaded[1])
            load(mixc[:, :], mix_kernel, w2_loaded)
            load(w1s[:, :, :], W1, w2_loaded)
            load(b1c[:, :], b1, w2_loaded)
            load(w2s[0:GR, :, :], W2, w2_loaded)
            load(w2s[GR:GR + NP, 0, :], b2, w2_loaded)
            load(wo1[:, :], Wo1, w2_loaded)
            load(bo1c[:, :], bo1.rearrange("(n a) -> n a", a=1), w2_loaded)
            load(wo2[0:DM, :], Wo2, w2_loaded)
            load(wo2[DM:DM + 1, :], row(bo2), w2_loaded)
            load(rw[:, :], router_w, w2_loaded)
            load(rb[:, :], row(router_b).to_broadcast([P, E]), w2_loaded)
            load(eb1c[:, :, :], eb1, w2_loaded)
            sp.wait_ge(consts, 1)
            for dst in (slot_in, picked):
                n = dst.shape[0] // P
                load(dst.rearrange("(t p) d -> p t d", p=P),
                     zeros[:, 0:dst.shape[1]].unsqueeze(1).to_broadcast([P, n, dst.shape[1]]), zero_filled)
            for g in range(2, GROUPS):
                sp.wait_ge(heads_free[g % 2], g // 2 + 1)
                load_heads(g % 2, HG * g, 0, S, heads_loaded[g % 2])
            for s in heads_free:
                sp.wait_ge(s, GROUPS // 2 + 1)
            load(ew1s, ew1, ex_loaded)
            load(ew2s, ew2, ex_loaded)
            sp.wait_ge(at_turned, CH)
            load(eb2b, eb2.rearrange("(a e) d -> a e d", a=1).to_broadcast([P, E, D]), ex_loaded)
            sp.wait_ge(scattered, 16 * 2 * TILES)
            for e in range(E):
                src = slot_in[CAP * e:CAP * e + CAP, :]
                load(slotrows[:, e, 0:ET - 1, :], src[0:P * (ET - 1), :].rearrange("(t p) d -> p t d", p=P),
                     slots_loaded[e])
                load(slotrows[0:LAST, e, ET - 1, :], src[P * (ET - 1):CAP, :], slots_loaded[e])
            for n, s in enumerate(eo_sent):
                sp.wait_ge(s, 16 * ET * E // 2)
            for t in range(CH):
                for k in range(2):
                    load(gath[:, k, CT * t:CT * t + CT, :],
                         picked[S * k + CW * t:S * k + CW * t + CW, :].rearrange("(t p) d -> p t d", p=P),
                         picked_loaded[t])
            for t in range(CH):
                sp.wait_ge(out_ready, t + 1)
                load(out[0].rearrange("(t p) d -> p t d", p=P)[:, CT * t:CT * t + CT, :],
                     X[:, CT * t:CT * t + CT, :], out_stored)
            sp.wait_ge(out_stored, 16 * CH)

        @block.gpsimd
        def _(pool):
            step = [0]

            def link(ins):
                step[0] += 1
                ins.then_inc(pchain, 1)
                pool.wait_ge(pchain, step[0])

            def pattern(t, base, pat, cm, op, fill):
                link(pool.affine_select(out=t, in_=t, compare_op=op, fill=fill, base=base, pattern=pat,
                                        channel_multiplier=cm))

            pool.memset(neghalf[:, :], -0.5).then_inc(pchain, 1)
            step[0] += 1
            link(pool.memset(identf[:, :], 0.0))
            pattern(identf[:, :], 0, [[-1, P]], 1, ALU.not_equal, 1.0)
            link(pool.memset(onesf[:, :], 1.0))
            link(pool.memset(zeros[:, :], 0.0))
            pool.memset(onesb[:, :], 1.0).then_inc(consts, 1)
            pool.wait_ge(consts, 1)

            def rstd_of(k):
                pool.wait_ge(ve_ready, k + 1)
                pool.tensor_tensor(rstd[:, k % 2, :], ve[:, k % 2, :], neghalf[:, :], ALU.pow).then_inc(rstd_ready, 1)
                pool.wait_ge(rstd_ready, k + 1)

            def clear(t, b):
                link(pool.memset(t[:, b, :, :].rearrange("p h s -> p (h s)").bitcast(F32), 0.0))

            clear(KS, 0)
            rstd_of(0)
            rstd_of(1)
            clear(QS, 0)
            rstd_of(2)
            rstd_of(3)
            link(pool.memset(identb[:, :], 0.0))
            pattern(identb[:, :], 0, [[-1, P]], 1, ALU.not_equal, 1.0)
            link(pool.memset(causal[:, :], 0.0))
            pattern(causal[:, :], 0, [[-1, P]], 1, ALU.is_ge, MASKED)
            link(pool.memset(onerow[:, :], 1.0))
            for b in range(2):
                if b == 1:
                    clear(KS, b)
                    clear(QS, b)
                link(pool.memset(Vg[:, b, :, :, :], 0.0))
                link(pool.memset(Vg[:, b, :, :, DK:DK + 1], 1.0))
                pool.memset(hT[:, b, 0:S + 2:S + 1], 0.0).then_inc(heads_free[b], 1)
                pool.wait_ge(heads_free[b], 1)

            def copy_v(g):
                pool.wait_ge(heads_free[g % 2], g // 2 + 1)
                at = HG * DK * g
                pool.tensor_copy(Vg[:, g % 2, :, :, 0:DK], vtok[:, :, at:at + HG * DK].rearrange(
                    "p t (h c) -> p t h c", h=HG)).then_inc(vg_ready, 1)
                pool.wait_ge(vg_ready, g + 1)

            pool.wait_ge(v_ready, CH)
            def later_constants():
                link(pool.memset(blockmask[:, :], 0.0))
                for j in range(P // BLK):
                    link(pool.memset(blockmask[BLK * j:BLK * j + BLK, BLK * j:BLK * j + BLK], 1.0))
                link(pool.memset(upto[:, :], 1.0))
                pattern(upto[:, :], 0, [[1, P]], -1, ALU.is_ge, 0.0)
                link(pool.memset(spread[:, :, :], 0.0))
                pattern(spread[:, :, :], 0, [[-1, NP], [0, DM]], 1, ALU.not_equal, 1.0)
                for p in range(NP):
                    link(pool.memset(rank9[:, :, p:p + 1], float(NP - p)))
                for e in range(E):
                    link(pool.memset(rank8[:, :, e:e + 1], float(E - e)))
                link(pool.memset(hot9[:, :, :], 0.0))
                link(pool.memset(chosen[:, :, :], 1.0))
                pool.memset(taug[DM:DM + 1, :], 1.0).then_inc(consts, 1)
                pool.wait_ge(consts, 2)

            copy_v(0)
            copy_v(1)
            for u, n in diag_no.items():
                it, kb = units[u]
                g, c = items[it]
                if kb == CT * c and c == CH - 1 and 1 <= g < GROUPS - 1:
                    copy_v(g + 1)
                off = P * (kb - CT * c)
                pool.wait_ge(b_exped, HG * (u + 1))
                pm = pT[:, u % 3, :, off:off + P]
                pool.affine_select(out=pm, in_=pm, compare_op=ALU.is_ge, fill=0.0, base=0,
                                   pattern=[[0, HG], [1, P]], channel_multiplier=-1).then_inc(diag_cut, 1)
                pool.wait_ge(diag_cut, n + 1)
                if u + 1 == first_unit[CH + 1]:
                    later_constants()
            for k in range(CH, 4 * CH):
                if k == CH + 1:
                    pool.memset(vone[:, :, :, :, HD:HD + 1].rearrange("p b t h c -> p (b t h c)"), 1.0)\
                        .then_inc(consts, 1)
                    pool.wait_ge(consts, 3)
                    pool.memset(slotrows[LAST:P, :, ET - 1, :], 0.0).then_inc(consts, 1)
                    pool.wait_ge(consts, 4)
                rstd_of(k)

            def dispatch(t):
                pool.wait_ge(slots_ready, t + 1)
                if t == 0:
                    pool.wait_ge(zero_filled, 16 * 2)
                for i in range(CT * t, CT * t + CT):
                    for k in range(2):
                        pool.indirect_dma_start(
                            slot_in[:, :], bass.IndirectOffsetOnAxis(ap=slot_w[:, k, i:i + 1], axis=0),
                            nrm[:, i, :], None, bounds_check=SLOTS - 1, oob_is_err=False).then_inc(scattered, 16)

            for t in range(CH):
                pool.wait_ge(nrm_ready, CH * 2 + t + 1)
                xc = X[:, CT * t:CT * t + CT, :]
                pool.tensor_tensor(xc, xc, browg[:, :].unsqueeze(1).to_broadcast([P, CT, D]), ALU.add)\
                    .then_inc(bias_added, 1)
                pool.wait_ge(bias_added, t + 1)
            for t in range(CH):
                rstd_of(4 * CH + t)
                if t >= 1:
                    dispatch(t - 1)
            dispatch(CH - 1)
            pool.wait_ge(meta_ready, 1)
            for e in range(E):
                for n in range(ET):
                    pool.wait_ge(eo_ready, ET * e + n + 1)
                    m = min(P, CAP - P * n)
                    pool.indirect_dma_start(
                        picked[:, :], bass.IndirectOffsetOnAxis(ap=to_row[0:m, e, n:n + 1], axis=0),
                        eo[0:m, e % 2, n, :], None, bounds_check=2 * S - 1, oob_is_err=False)\
                        .then_inc(eo_sent[e % 2], 16)

        @block.scalar
        def _(act):
            step = [0]

            def link(ins):
                step[0] += 1
                ins.then_inc(achain, 1)
                act.wait_ge(achain, step[0])

            act.wait_ge(mod_loaded[0], 16 * 2)
            act.activation(cexp[:, :], ccol[:, :], ACT.Exp, scale=-1.0).then_inc(c_exp, 1)

            def modulate(m, t, layer, which, bank):
                act.wait_ge(tposed, CH * m + t + 1)
                if m == 0 and t == 0:
                    act.wait_ge(mod_ready, 1)
                act.activation(hT[:, m % 2, 1 + CW * t:1 + CW * t + CW], ps[:, bank, :], ACT.Identity,
                               bias=modc[:, layer, 2 * which:2 * which + 1],
                               scale=modc[:, layer, 2 * which + 1:2 * which + 2]).then_inc(hT_ready, 1)

            modulate(0, 0, 0, 0, 0)
            for t in range(CH):
                for k in range(2):
                    act.wait_ge(qk_mm, 2 * t + k + 1)
                    if t >= 2:
                        act.wait_ge(qk_stored[t % 2], 16 * 6 * (t // 2))
                    act.activation(parts[:, 0, k, t % 2, :], ps[:, 2 + k, :], ACT.Copy).then_inc(qk_hi, 1)
                if t + 1 < CH:
                    modulate(0, t + 1, 0, 0, (t + 1) % 2)
                for k in range(2):
                    act.wait_ge(qk_rest, 2 * t + k + 1)
                    act.activation(parts[:, 1, k, t % 2, :], rest[:, k, :], ACT.Copy).then_inc(qk_mid, 1)
                act.wait_ge(v1_mm, t + 1)
                act.activation(vtok[:, CT * t:CT * t + CT, :], ps[:, 4, :].rearrange("p (t d) -> p t d", t=CT),
                               ACT.Copy).then_inc(v_ready, 1)
                act.wait_ge(fold_mm, t + 1)
                act.activation(pfold[:, 4 * t:4 * t + 4, :], ps[:, 5, :].rearrange("p (h f) -> p h f", h=4),
                               ACT.Copy).then_inc(fold_ready, 1)

            for u, (it, kb) in enumerate(units):
                off = P * max(0, kb - CT * items[it][1])
                if u >= 3:
                    act.wait_ge(pv_done, u - 2)
                for j in range(HG):
                    n = HG * u + j
                    act.wait_ge(b_ready, n + 1)
                    act.activation(pT[:, u % 3, j, off:CW], ps[:, n % 3, off:CW], ACT.Exp, scale=SCALE)\
                       .then_inc(b_exped, 1)

            for t in range(CH):
                act.wait_ge(at_turned, t + 1)
                act.activation(attnT[:, t, :], ps[:, t % 2, :], ACT.Copy).then_inc(at_ready, 1)
            def mix_first(t):
                act.wait_ge(hT_ready, CH + t + 1)
                if t >= 2:
                    act.wait_ge(hid_mm, t - 1)
                act.activation(cT[:, t % 2, :], hT[:, 1, 1 + CW * t:1 + CW * t + CW], ACT.Copy,
                               scale=mixc[:, 1:2]).then_inc(conv_first, 1)

            def hidden(t):
                act.wait_ge(u_mm, t + 1)
                act.activation(taug[0:DM, :], ps[0:DM, 7, :], ACT.Tanh, bias=bo1c[:, 0:1])\
                   .then_inc(t_ready, 1)
                act.wait_ge(hid_mm, t + 1)
                if t >= 1:
                    act.wait_ge(hsel_ready, t)
                for g in range(NG):
                    act.activation(hid[:, g, :], ps[0:GR, g, :], ACT.Identity, bias=b1c[:, g:g + 1])\
                       .then_inc(hid_ready, 1)

            def modulate2(which, t, bank):
                act.wait_ge(turned2[which], t + 1)
                act.activation(hT[:, which, 1 + CW * t:1 + CW * t + CW], ps[:, bank, :], ACT.Identity,
                               bias=modc[:, 1, 2 * which:2 * which + 1],
                               scale=modc[:, 1, 2 * which + 1:2 * which + 2]).then_inc(hT2_ready[which], 1)

            def copy_values(t):
                act.wait_ge(v2_mm, t + 1)
                act.wait_ge(consts, 3)
                if t >= 2:
                    act.wait_ge(av_mm, H1 * (t - 1))
                act.activation(vone[:, t % 2, :, :, 0:HD], ps[:, 0, :].rearrange("p (t h d) -> p t h d", t=CT, h=H1),
                               ACT.Copy).then_inc(v2_ready, 1)

            act.wait_ge(w2_loaded, 16 * 12)
            modulate(1, 0, 0, 1, 4)
            modulate(1, 1, 0, 1, 5)
            mix_first(0)
            hidden(0)
            modulate(1, 2, 0, 1, 4)
            mix_first(1)
            modulate(1, 3, 0, 1, 5)
            for t in range(CH):
                if t + 2 < CH:
                    mix_first(t + 2)
                if t + 1 < CH:
                    hidden(t + 1)
                else:
                    modulate2(0, 0, 0)
                    copy_values(0)
                act.wait_ge(ffn_mm, t + 1)
                if t >= 2:
                    act.wait_ge(ffn_read, t - 1)
                act.activation(fsum[:, t % 2, :, :], ps[:, 6, :].rearrange("p (t d) -> p t d", t=CT), ACT.Copy)\
                   .then_inc(ffn_copied, 1)

            def exp_min(n):
                act.wait_ge(f_mm, n + 1)
                if n >= 2:
                    act.wait_ge(f_ready, n - 1)
                eq_ = expq[:, n % 2, :, :]
                link(act.activation(eq_, ps[:, 2 + 2 * (n % 2):4 + 2 * (n % 2), :], ACT.Relu, scale=-1.0))
                act.activation(eq_, eq_, ACT.Exp, scale=-1.0).then_inc(f_exp, 1)

            def between(t, h):
                if h == 1 and 1 <= t <= CH:
                    act.wait_ge(on_turned, t)
                    if t >= 2:
                        act.wait_ge(y1_mm, t - 1)
                    act.activation(onT, ps[:, 0, :], ACT.Copy).then_inc(onT_ready, 1)
                if h == 3 and t + 1 < CH:
                    modulate2(0, t + 1, 0)
                if h == 4 and t + 1 < CH:
                    copy_values(t + 1)
                if h == (6 if t < CH else 4) and 1 <= t <= CH:
                    modulate2(1, t - 1, 0)
                if h == 0 and t >= 2:
                    act.wait_ge(r_shift, t - 1)
                    at = slice(CT * (t - 2), CT * (t - 1))
                    act.activation(gates[:, at, :], lg[:, at, :], ACT.Exp).then_inc(r_exped, 1)

            exp_min(0)
            exp_min(1)
            for t in range(CH + 2):
                for h in range(H1):
                    if H1 * t + h + 2 < H1 * CH:
                        exp_min(H1 * t + h + 2)
                    between(t, h)
            def modulate_slots(e):
                act.wait_ge(xs_turned, e + 1)
                act.activation(xsT[:, CAP * e:CAP * e + CAP], ps[:, e % 2, 0:CAP], ACT.Identity,
                               bias=modc[:, 1, 2:3], scale=modc[:, 1, 3:4]).then_inc(xs_ready, 1)

            modulate_slots(0)
            modulate_slots(1)
            for e in range(E):
                for c in range(HC):
                    act.wait_ge(e1_mm, HC * e + c + 1)
                    if e >= 2 and c == 0:
                        act.wait_ge(e2_mm, ET * (e - 1))
                    act.activation(gT[:, e % 2, c, :], ps[:, 2 + c, 0:CAP], ACT.Gelu, bias=eb1c[:, e, c:c + 1])\
                       .then_inc(gelu_ready, 1)
                if e + 2 < E:
                    modulate_slots(e + 2)

        @block.vector
        def _(dve):
            step = [0]

            def link(ins):
                step[0] += 1
                ins.then_inc(dchain, 1)
                dve.wait_ge(dchain, step[0])

            def stats_of(k, rows):
                for i in range(CT):
                    ins = dve.bn_stats(stats[:, i, :], rows(i))
                    step[0] += 1
                    ins.then_inc(dchain, 1)
                dve.wait_ge(dchain, step[0])
                for i in range(CT):
                    ins = dve.bn_aggr(mv[:, k % 2, i, :], stats[:, i, :])
                    step[0] += 1
                    ins.then_inc(dchain, 1)
                dve.wait_ge(dchain, step[0])
                dve.tensor_scalar(ve[:, k % 2, :], mv[:, k % 2, :, 1], EPS, None, ALU.add).then_inc(ve_ready, 1)

            def normalise(k, t, rows, dst, done):
                dve.wait_ge(rstd_ready, k + 1)
                for i in range(CT):
                    ins = dve.tensor_scalar(dst(i), rows(i), mv[:, k % 2, i, 0:1],
                                            rstd[:, k % 2, i:i + 1], ALU.subtract, ALU.mult)
                    if done is None:
                        step[0] += 1
                        ins.then_inc(dchain, 1)
                if done is None:
                    dve.wait_ge(dchain, step[0])
                else:
                    ins.then_inc(done, 1)

            def x_row(t):
                return lambda i: X[:, CT * t + i, :]

            def nrm_row(t):
                return lambda i: nrm[:, CT * t + i, 0:D]

            dve.wait_ge(c_exp, 1)
            link(dve.tensor_scalar(cden[:, :], cexp[:, :], 1.0, None, ALU.add))
            link(dve.reciprocal(crec[:, :], cden[:, :]))
            link(dve.tensor_tensor(scol[:, :], ccol[:, :], crec[:, :], ALU.mult))
            dve.wait_ge(consts, 1)
            for l in range(2):
                ins = dve.tensor_scalar(smat[:, l, :], onesf[:, :], scol[:, l:l + 1], None, ALU.mult)
                ins.then_inc(silu_ready, 1)

            def x_stats(t):
                dve.wait_ge(x_loaded[t], 16)
                stats_of(t, x_row(t))

            x_stats(0)
            x_stats(1)

            def shift_and_scale(l):
                cols = ps[:, 7, 4 * l:4 * l + 4]
                link(dve.tensor_copy(modc[:, l, :], cols))
                dve.tensor_scalar(modc[:, l, 1:4:2], cols[:, 1:4:2], 1.0, None, ALU.add).then_inc(mod_ready, 1)

            dve.wait_ge(mod_mm, 1)
            shift_and_scale(0)

            def split(t):
                for k in range(2):
                    dve.wait_ge(qk_hi, 2 * t + k + 1)
                    if t >= 1:
                        dve.wait_ge(qk_lo, 2 * t + k - 1)
                    dve.tensor_tensor(rest[:, k, :], ps[:, 2 + k, :], parts[:, 0, k, t % 2, :], ALU.subtract)\
                       .then_inc(qk_rest, 1)
                if t + 2 < CH:
                    normalise(t + 2, t + 2, x_row(t + 2), nrm_row(t + 2), nrm_ready)
                for k in range(2):
                    dve.wait_ge(qk_mid, 2 * t + k + 1)
                    dve.tensor_tensor(parts[:, 2, k, t % 2, :], rest[:, k, :], parts[:, 1, k, t % 2, :],
                                      ALU.subtract).then_inc(qk_lo, 1)
                if t + 3 < CH:
                    x_stats(t + 3)

            normalise(0, 0, x_row(0), nrm_row(0), nrm_ready)
            x_stats(2)
            normalise(1, 1, x_row(1), nrm_row(1), nrm_ready)
            for t in range(CH):
                split(t)
            dve.wait_ge(mod_mm, 2)
            shift_and_scale(1)
            g4 = ps[:, 6, :].rearrange("p (g d) -> p g d", g=4)
            link(dve.tensor_scalar(gneg[:, :, :], g4, -1.0, 0.25, ALU.mult, ALU.max))
            link(dve.tensor_tensor(gabs[:, :, :], g4, gneg[:, :, :], ALU.max))
            link(dve.tensor_scalar(gsgn[:, :, :], g4, 0.0, 2.0, ALU.is_ge, ALU.mult))
            link(dve.scalar_tensor_tensor(gate[:, :, :], gsgn[:, :, :], -1.0, gabs[:, :, :], ALU.add, ALU.mult))

            dve.wait_ge(fold_loaded, 16 * 7)
            dve.wait_ge(w_loaded, 16 * 4)
            dve.wait_ge(fold_mm, 2 * H1 // 4 + 1)
            dve.tensor_tensor(wog[:, :], wq[:, 3, :], gate[:, 0, :], ALU.mult).then_inc(fold_ready, 1)
            dve.tensor_copy(wvT[:, :], ps[:, 5, 0:P]).then_inc(fold_ready, 1)
            dve.tensor_tensor(woutT[:, :], ps[:, 5, P:2 * P], gate[:, 2, :], ALU.mult).then_inc(fold_ready, 1)
            for g in range(2):
                dve.tensor_tensor(gbg[:, g, :], gb_rows[:, g, :], gate[:, 1, :], ALU.mult).then_inc(fold_ready, 1)
            dve.tensor_tensor(browg[:, :], brow[:, :], gate[:, 2, :], ALU.mult).then_inc(fold_ready, 1)

            def maxima(numbers):
                for a in numbers:
                    it, qi, j, kc = pieces[a]
                    w = CW if kc < items[it][1] else P * (qi + 1)
                    dve.wait_ge(a_ready, a + 1)
                    dve.tensor_reduce(tmax[:, it % 2, HG * qi + j, kc:kc + 1], ps[:, 3 + a % 3, 0:w],
                                      AX.X, ALU.max).then_inc(a_maxed, 1)

            def split_maxima(it):
                dve.wait_ge(a_maxed, piece_end[it])
                dve.tensor_reduce(negm[:, :], tmax[:, it % 2, :, 0:items[it][1] + 1], AX.X, ALU.max, negate=True)\
                   .then_inc(m_neg, 1)
                dve.wait_ge(m_neg, 2 * it + 1)
                nm = negm[:, :].rearrange("p (t h) -> p t h", h=HG)
                dve.tensor_copy(mhl[:, :, :, 0], nm).then_inc(m_neg, 1)
                dve.wait_ge(m_neg, 2 * it + 2)
                dve.tensor_tensor(mhl[:, :, :, 1], nm, mhl[:, :, :, 0], ALU.subtract).then_inc(m_parts, 1)

            def maxima_rows(it):
                g, c = items[it]
                dve.wait_ge(m_turned, it + 1)
                dve.tensor_copy(QS[ROWS:ROWS + 2 * HG, g % 2, :, CW * c:CW * c + CW],
                                mps[ROWS:ROWS + 2 * HG, 0:CW].unsqueeze(1).to_broadcast([2 * HG, HG, CW]))\
                   .then_inc(m_rows, 1)

            def copy_item(it):
                dve.wait_ge(pv_done, first_unit[it + 1])
                if it == 0:
                    for s in qk_stored:
                        dve.wait_ge(s, 16 * 6 * 2)
                dve.tensor_copy(oT[:, it % 2, :], ps[:, 7, :]).then_inc(o_copied, 1)

            def finish_item(it):
                g, c = items[it]
                dve.wait_ge(o_turned, it + 1)
                o4 = ps[:, 6, :].rearrange("p (t h c) -> p t h c", t=CT, h=HG)
                if it > 0:
                    dve.wait_ge(o_normed, it)
                dve.reciprocal(rden[:, :, :], o4[:, :, :, DK]).then_inc(o_rden, 1)
                dve.wait_ge(o_rden, it + 1)
                dve.tensor_tensor(
                    attn[:, CT * c:CT * c + CT, HG * DK * g:HG * DK * g + HG * DK].rearrange(
                        "p t (h c) -> p t h c", h=HG),
                    o4[:, :, :, 0:DK], rden[:, :, :].unsqueeze(3).to_broadcast([P, CT, HG, DK]), ALU.mult)\
                   .then_inc(o_normed, 1)

            maxima(range(piece_end[0]))
            split_maxima(0)
            maxima_rows(0)
            for u, (it, kb) in enumerate(units):
                maxima(hosted(u))
                if kb == 1 and it > 0:
                    copy_item(it - 1)
                for what, n in turns[u]:
                    if what == 'maxima':
                        maxima_rows(n)
                    else:
                        finish_item(n)
                for n in found[u]:
                    split_maxima(n)
            copy_item(ITEMS - 1)
            finish_item(ITEMS - 1)

            for t in range(CH):
                dve.wait_ge(y_mm, t + 1)
                xc = X[:, CT * t:CT * t + CT, :]
                dve.tensor_tensor(xc, ps[:, 2 + t % 2, :].rearrange("p (t d) -> p t d", t=CT), xc, ALU.add)\
                   .then_inc(y_read, 1)
                dve.wait_ge(y_read, t + 1)
                stats_of(CH + t, x_row(t))
                if 1 <= t < CH - 1:
                    normalise(CH + t - 1, t - 1, x_row(t - 1), nrm_row(t - 1), nrm_ready)

            def mix_rest(t):
                dve.wait_ge(conv_first, t + 1)
                dve.wait_ge(hT_ready, CH + min(t + 2, CH))
                xm = cT[:, t % 2, :]
                link(dve.scalar_tensor_tensor(xm, hT[:, 1, CW * t:CW * t + CW], mixc[:, 0:1], xm, ALU.mult, ALU.add))
                dve.scalar_tensor_tensor(xm, hT[:, 1, CW * t + 2:CW * t + 2 + CW], mixc[:, 2:3], xm,
                                         ALU.mult, ALU.add).then_inc(conv_ready, 1)

            def best_path(t):
                dve.wait_ge(sc_mm, t + 1)
                s9 = ps[:, 7, 0:CT * NP].rearrange("p (t k) -> p t k", t=CT)
                wide = [P, CT, NP]
                link(dve.tensor_reduce(top9[:, :], s9, AX.X, ALU.max))
                link(dve.tensor_tensor(eq9[:, :, :], s9, top9[:, :].unsqueeze(2).to_broadcast(wide), ALU.is_equal))
                link(dve.tensor_tensor(eq9[:, :, :], eq9[:, :, :], rank9[:, :, :], ALU.mult))
                link(dve.tensor_reduce(best9[:, :], eq9[:, :, :], AX.X, ALU.max))
                dve.tensor_tensor(hot9[:, :, 0:NP], eq9[:, :, :], best9[:, :].unsqueeze(2).to_broadcast(wide),
                                  ALU.is_equal).then_inc(hot_ready, 1)

            def copy_hot(t):
                dve.wait_ge(hot_turned, t + 1)
                dve.tensor_copy(hotT[:, t % 2, :], hps[0:NP, CW:2 * CW]).then_inc(hot_copied, 1)

            def select(t):
                dve.wait_ge(mask_mm, t + 1)
                dve.wait_ge(hid_ready, NG * (t + 1))
                for g in range(NG):
                    dve.tensor_tensor(hsel[0:GR, g, :], hid[:, g, :], ps[0:GR, 3 + g, :], ALU.mult)
                dve.wait_ge(hot_copied, t + 1)
                dve.tensor_copy(hsel[GR:GR + NP, 0, :], hotT[:, t % 2, :]).then_inc(hsel_ready, 1)

            def sum_stats(t):
                dve.wait_ge(ffn_copied, t + 1)
                stats_of(2 * CH + 2 * t, lambda i: fsum[:, t % 2, i, :])

            def norm_sum(t):
                tmp = fsum[:, t % 2, :, :]
                normalise(2 * CH + 2 * t, t, lambda i: tmp[:, i, :], lambda i: tmp[:, i, :], None)
                four = [P, CT, D]
                link(dve.tensor_tensor(tmp, tmp, gbg[:, 0:1, :].to_broadcast(four), ALU.mult))
                link(dve.tensor_tensor(tmp, tmp, gbg[:, 1:2, :].to_broadcast(four), ALU.add))

            def add_sum(t):
                xc = X[:, CT * t:CT * t + CT, :]
                dve.tensor_tensor(xc, xc, fsum[:, t % 2, :, :], ALU.add).then_inc(ffn_read, 1)
                dve.wait_ge(ffn_read, t + 1)
                stats_of(2 * CH + 2 * t + 1, x_row(t))

            def norm2(t):
                normalise(2 * CH + 2 * t + 1, t, x_row(t), nrm_row(t), nrm_ready)

            mix_rest(0)
            for t in (CH - 2, CH - 1):
                normalise(CH + t, t, x_row(t), nrm_row(t), nrm_ready)
            best_path(0)
            copy_hot(0)
            mix_rest(1)
            for t in range(CH):
                select(t)
                if t >= 2:
                    norm2(t - 2)
                if t >= 1:
                    sum_stats(t - 1)
                if t + 1 < CH:
                    best_path(t + 1)
                if t + 2 < CH:
                    mix_rest(t + 2)
                if t + 1 < CH:
                    copy_hot(t + 1)
                if t >= 1:
                    norm_sum(t - 1)
                    add_sum(t - 1)
            def feature(n):
                dve.wait_ge(f_exp, n + 1)
                if n >= 2:
                    dve.wait_ge(s_mm, n - 1)
                dve.scalar_tensor_tensor(feat[:, n % 2, :, :], ps[:, 2 + 2 * (n % 2):4 + 2 * (n % 2), :],
                                         1.0, expq[:, n % 2, :, :], ALU.add, ALU.max).then_inc(f_ready, 1)

            def same_block(n):
                dve.wait_ge(s_mm, n + 1)
                if n >= 2:
                    dve.wait_ge(av_mm, n - 1)
                dve.tensor_tensor(
                    am[:, n % 2, :].rearrange("p (t q) -> p t q", t=CT),
                    ps[:, 6, :].rearrange("p (t q) -> p t q", t=CT),
                    blockmask[:, :].unsqueeze(1).to_broadcast([P, CT, P]), ALU.mult).then_inc(s_ready, 1)

            def divide(t, g):
                dve.wait_ge(av_mm, H1 * t + HH * g + HH)
                o = ps[:, 1 + 6 * g, 0:CT * HH * (HD + 1)].rearrange("p (t h c) -> p t h c", t=CT, h=HH)
                link(dve.tensor_scalar(den1[:, :, :], o[:, :, :, HD], 1e-8, None, ALU.add))
                link(dve.reciprocal(den1[:, :, :], den1[:, :, :]))
                if t >= 1:
                    dve.wait_ge(on_turned, t)
                dve.tensor_tensor(
                    on[:, :, HH * HD * g:HH * HD * g + HH * HD].rearrange("p t (h d) -> p t h d", h=HH),
                    o[:, :, :, 0:HD], den1[:, :, :].unsqueeze(3).to_broadcast([P, CT, HH, HD]), ALU.mult)\
                   .then_inc(on_ready, 1)

            def residual(t):
                dve.wait_ge(y1_mm, t + 1)
                dve.wait_ge(bias_added, t + 1)
                xc = X[:, CT * t:CT * t + CT, :]
                dve.tensor_tensor(xc, ps[:, 0, :].rearrange("p (t d) -> p t d", t=CT), xc, ALU.add)\
                   .then_inc(y1_read, 1)
                dve.wait_ge(y1_read, t + 1)
                stats_of(4 * CH + t, x_row(t))

            wide = [P, CT, E]

            def over(r, at):
                return red[:, r, at].unsqueeze(2).to_broadcast(wide)

            def shift_logits(t):
                at = slice(CT * t, CT * t + CT)
                dve.wait_ge(lg_mm, t + 1)
                logits = ps[:, 0, 0:CT * E].rearrange("p (t e) -> p t e", t=CT)
                if t == 0:
                    dve.wait_ge(w2_loaded, 16 * 12)
                link(dve.tensor_tensor(lg[:, at, :], logits, rb[:, :].unsqueeze(1).to_broadcast(wide), ALU.add))
                link(dve.tensor_reduce(red[:, 0, at], lg[:, at, :], AX.X, ALU.max))
                dve.tensor_tensor(lg[:, at, :], lg[:, at, :], over(0, at), ALU.subtract).then_inc(r_shift, 1)

            def find_highest(k, at, src):
                link(dve.tensor_reduce(wsel[:, k, at], src, AX.X, ALU.max))
                link(dve.tensor_tensor(sel[:, k, at, :], src, wsel[:, k, at].unsqueeze(2).to_broadcast(wide),
                                       ALU.is_equal))
                link(dve.tensor_tensor(sel[:, k, at, :], sel[:, k, at, :], rank8[:, at, :], ALU.mult))
                link(dve.tensor_reduce(red[:, 3 + k, at], sel[:, k, at, :], AX.X, ALU.max))
                link(dve.tensor_tensor(hot[:, k, at, :], sel[:, k, at, :], over(3 + k, at), ALU.is_equal))

            def choose_first(t):
                at = slice(CT * t, CT * t + CT)
                dve.wait_ge(r_exped, t + 1)
                link(dve.tensor_reduce(red[:, 1, at], gates[:, at, :], AX.X, ALU.add))
                link(dve.reciprocal(red[:, 2, at], red[:, 1, at]))
                link(dve.tensor_tensor(gates[:, at, :], gates[:, at, :], over(2, at), ALU.mult))
                find_highest(0, at, gates[:, at, :])

            def choose_second(t):
                at = slice(CT * t, CT * t + CT)
                link(dve.scalar_tensor_tensor(lg[:, at, :], hot[:, 0, at, :], -2.0, gates[:, at, :],
                                              ALU.mult, ALU.add))
                find_highest(1, at, lg[:, at, :])
                dve.tensor_tensor(chosen[:, at, 0:E], hot[:, 0, at, :], hot[:, 1, at, :], ALU.add).then_inc(r_mask, 1)

            def slots(t):
                at = slice(CT * t, CT * t + CT)
                dve.tensor_copy(nrm[:, at, D:D + 2], wsel[:, :, at].rearrange("p k t -> p t k"))
                dve.tensor_copy(nrm[:, at, D + 3], red[:, 3, at])
                link(dve.tensor_scalar(red[:, 7:9, at], red[:, 3:5, at], float(-CAP), float(E * CAP - 1),
                                       ALU.mult, ALU.add))
                dve.wait_ge(pos_mm, t + 1)
                place = ps[:, pos_bank(t), 0:CT * (E + 1)].rearrange("p (t e) -> p t e", t=CT)
                dve.tensor_copy(nrm[:, at, D + 2:D + 3], place[:, :, E:E + 1])
                both = red[:, 5:7, at]
                link(dve.tensor_tensor(sel[:, :, at, :], hot[:, :, at, :],
                                       place[:, :, 0:E].unsqueeze(1).to_broadcast([P, 2, CT, E]), ALU.mult))
                link(dve.tensor_reduce(both, sel[:, :, at, :], AX.X, ALU.add))
                link(dve.tensor_scalar(red[:, 9:11, at], both, float(CAP), float(SLOTS), ALU.is_gt, ALU.mult))
                link(dve.tensor_tensor(slotf[:, :, at], red[:, 7:9, at], both, ALU.add))
                dve.tensor_tensor(slot_w[:, :, at], slotf[:, :, at], red[:, 9:11, at], ALU.add).then_inc(slots_ready, 1)

            def between(t, h):
                if t == 0 and h == 0:
                    norm2(CH - 2)
                    sum_stats(CH - 1)
                if t == 0 and h == 1:
                    norm_sum(CH - 1)
                if t == 0 and h == 2:
                    add_sum(CH - 1)
                if t == 0 and h == 3:
                    norm2(CH - 1)
                if h == 0 and 1 <= t <= CH:
                    divide(t - 1, 1)
                if h == 1 and t >= 2:
                    choose_first(t - 2)
                if h == 2 and 1 <= t <= CH:
                    residual(t - 1)
                if h == 3 and t >= 2:
                    choose_second(t - 2)
                if h == 4 and 1 <= t <= CH:
                    normalise(4 * CH + t - 1, t - 1, x_row(t - 1), nrm_row(t - 1), nrm_ready)
                if h == 5 and t < CH:
                    divide(t, 0)
                if h == 5 and t >= 2:
                    slots(t - 2)
                if h == 7 and 1 <= t <= CH:
                    shift_logits(t - 1)

            feature(0)
            for t in range(CH + 2):
                for h in range(H1):
                    if t < CH:
                        same_block(H1 * t + h)
                        if H1 * t + h + 1 < H1 * CH:
                            feature(H1 * t + h + 1)
                    between(t, h)

            for s in slots_loaded:
                dve.wait_ge(s, 16 * 2)
            dve.wait_ge(consts, 4)
            wide3 = [P, E, ET]
            w_a, w_b, number, rank = (slotrows[:, :, :, D + n] for n in range(META))
            first, second = smeta[:, 0, :, :], smeta[:, 1, :, :]
            link(dve.tensor_tensor(first, rank, rank8[:, 0, :].unsqueeze(2).to_broadcast(wide3), ALU.is_equal))
            link(dve.tensor_scalar(second, first, -1.0, 1.0, ALU.mult, ALU.add))
            link(dve.tensor_tensor(smeta[:, 2, :, :], first, w_a, ALU.mult))
            link(dve.tensor_tensor(smeta[:, 3, :, :], second, w_b, ALU.mult))
            link(dve.tensor_tensor(smeta[:, 2, :, :], smeta[:, 2, :, :], smeta[:, 3, :, :], ALU.add))
            link(dve.tensor_scalar(second, second, float(S), -1.0, ALU.mult, ALU.add))
            link(dve.tensor_tensor(second, second, number, ALU.add))
            link(dve.tensor_scalar(smeta[:, 4, :, :], number, 0.0, float(2 * S), ALU.is_equal, ALU.mult))
            link(dve.tensor_tensor(smeta[:, 5, :, :], second, smeta[:, 4, :, :], ALU.add))
            dve.tensor_copy(to_row[:, :, :], smeta[:, 5, :, :]).then_inc(meta_ready, 1)
            weight = smeta[:, 2, :, :]

            for e in range(E):
                if e >= 2:
                    dve.wait_ge(eo_sent[e % 2], 16 * ET * (e // 2))
                for n in range(ET):
                    tile = ET * e + n
                    m = min(P, CAP - P * n)
                    dve.wait_ge(e2_mm, tile + 1)
                    biased = eo[0:m, e % 2, n, :]
                    link(dve.tensor_tensor(biased, ps[0:m, 6 + tile % 2, 0:P], eb2b[0:m, e, :], ALU.add))
                    dve.scalar_tensor_tensor(biased, biased,
                                             weight[0:m, e, n:n + 1], gate[0:m, 3, :], ALU.mult, ALU.mult)\
                       .then_inc(eo_ready, 1)
            for t in range(CH):
                dve.wait_ge(picked_loaded[t], 16 * 2)
                at = slice(CT * t, CT * t + CT)
                xc = X[:, at, :]
                gc = gath[:, 0, at, :]
                link(dve.tensor_tensor(gc, gc, gath[:, 1, at, :], ALU.add))
                dve.tensor_tensor(xc, xc, gc, ALU.add).then_inc(out_ready, 1)

        @block.tensor
        def _(pe):
            def mm(o, lhsT, rhs, start=True, stop=True):
                return pe.matmul(o, lhsT, rhs, start=start, stop=stop, skip_group_check=True)

            pe.wait_ge(silu_ready, 2)

            def mod_columns(l):
                pe.wait_ge(mod_loaded[1 + l], 16)
                for n, which in enumerate((0, 1, 3, 4)):
                    ins = mm(ps[:, 7, 4 * l + n:4 * l + n + 1], wmod[:, l, D * which:D * which + D], scol[:, l:l + 1])
                return ins

            mod_columns(0).then_inc(mod_mm, 1)

            def turn(m, t, bank):
                pe.wait_ge(nrm_ready, CH * m + t + 1)
                for i in range(CT):
                    ins = pe.transpose(ps[:, bank, P * i:P * i + P], nrm[:, CT * t + i, 0:D], identf[:, :])
                ins.then_inc(tposed, 1)

            pe.wait_ge(consts, 1)
            turn(0, 0, 0)
            pe.wait_ge(w_loaded, 16 * 4)
            for t in range(CH):
                pe.wait_ge(hT_ready, t + 1)
                rows = hT[:, 0, 1 + CW * t:1 + CW * t + CW]
                for k in range(2):
                    if t >= 1:
                        pe.wait_ge(qk_rest, 2 * t + k - 1)
                    mm(ps[:, 2 + k, :], wq[:, k, :], rows).then_inc(qk_mm, 1)
                if t + 1 < CH:
                    turn(0, t + 1, (t + 1) % 2)
                if t >= 1:
                    pe.wait_ge(v_ready, t)
                for i in range(CT):
                    ins = mm(ps[:, 4, P * i:P * i + P], rows[:, P * i:P * i + P], wq[:, 2, :])
                ins.then_inc(v1_mm, 1)
                if t == 0:
                    pe.wait_ge(fold_loaded, 16 * 7)
                else:
                    pe.wait_ge(fold_ready, t)
                for n in range(4 * t, 4 * t + 4):
                    ins = mm(ps[:, 5, P * (n % 4):P * (n % 4) + P], wqkv16[:, n, :], proj_s[:, n % H1, :])
                ins.then_inc(fold_mm, 1)
            mod_columns(1)
            for l in range(2):
                for n, which in enumerate((2, 5)):
                    ins = mm(ps[:, 6, D * (2 * l + n):D * (2 * l + n) + D], smat[:, l, :],
                             wmod[:, l, D * which:D * which + D])
            ins.then_inc(mod_mm, 1)
            pe.wait_ge(fold_ready, CH)
            pe.transpose(ps[:, 5, 0:P], wvrow[:, :], identf[:, :])
            pe.transpose(ps[:, 5, P:2 * P], woutr, identf[:, :]).then_inc(fold_mm, 1)
            pe.wait_ge(fold_ready, 10)

            def score_piece(a):
                it, qi, j, kc = pieces[a]
                g, c = items[it]
                w = CW if kc < c else P * (qi + 1)
                if a >= 3:
                    pe.wait_ge(a_maxed, a - 2)
                o = ps[:, 3 + a % 3, 0:w]
                ins = mm(o, QS[0:ROWS, g % 2, j, P * (CT * c + qi):P * (CT * c + qi) + P],
                         KS[0:ROWS, g % 2, j, CW * kc:CW * kc + w], True, kc < c)
                if kc == c:
                    ins = mm(o[:, w - P:w], identb[:, :], causal[:, :], False, True)
                ins.then_inc(a_ready, 1)

            def bank6_read(what, it):
                before = turn_order.index((what, it)) - 1
                if before >= 0:
                    last, n = turn_order[before]
                    pe.wait_ge(m_rows if last == 'maxima' else o_normed, n + 1)

            def turn_maxima(it):
                pe.wait_ge(m_parts, it + 1)
                bank6_read('maxima', it)
                for qi in range(CT):
                    ins = pe.transpose(mps[ROWS:ROWS + 2 * HG, P * qi:P * qi + P],
                                       mhl[:, qi, :, :].rearrange("p h c -> p (h c)"), identb[:, :])
                ins.then_inc(m_turned, 1)

            def turn_output(it):
                pe.wait_ge(o_copied, it + 1)
                bank6_read('output', it)
                for q in range(CT):
                    ins = pe.transpose(ps[:, 6, P * q:P * q + P], oT[:, it % 2, P * q:P * q + P], identf[:, :])
                    if q == 0 and it % CH == CH - 1:
                        ins.then_inc(heads_free[items[it][0] % 2], 1)
                ins.then_inc(o_turned, 1)

            def scores(u, j):
                it, kb = units[u]
                g, c = items[it]
                off = P * max(0, kb - CT * c)
                n = HG * u + j
                if n >= 3:
                    pe.wait_ge(b_exped, n - 2)
                mm(ps[:, n % 3, off:CW], KS[0:ROWS + 2 * HG, g % 2, j, P * kb:P * kb + P],
                   QS[0:ROWS + 2 * HG, g % 2, j, CW * c + off:CW * c + CW]).then_inc(b_ready, 1)

            def values(u, j):
                it, kb = units[u]
                g, c = items[it]
                off = P * max(0, kb - CT * c)
                if j == 0:
                    pe.wait_ge(b_exped, HG * u + HG)
                    if u in diag_no:
                        pe.wait_ge(diag_cut, diag_no[u] + 1)
                    if kb == 0 and it > 0:
                        pe.wait_ge(o_copied, it)
                ins = mm(ps[32 * j:32 * j + 32, 7, off:CW], Vg[:, g % 2, kb, j, :], pT[:, u % 3, j, off:CW],
                         kb == 0, kb == CT * c + CT - 1)
                if j == HG - 1:
                    ins.then_inc(pv_done, 1)

            pe.wait_ge(heads_loaded[0], heads_there(0))
            for a in range(piece_end[0]):
                score_piece(a)
            turn_maxima(0)
            for u, (it, kb) in enumerate(units):
                g, c = items[it]
                if kb == 0:
                    pe.wait_ge(m_rows, it + 1)
                if u == first_unit[CH * g]:
                    pe.wait_ge(vg_ready, g + 1)
                hs = hosted(u)
                for j in range(HG):
                    scores(u, j)
                    if j == 3 and u >= 2:
                        for k in range(HG):
                            values(u - 2, k)
                    for a in hs[-(-len(hs) * j // HG):-(-len(hs) * (j + 1) // HG)]:
                        if a in piece_end[CH - 1::CH]:
                            new = items[pieces[a][0]][0]
                            pe.wait_ge(heads_loaded[new % 2], heads_there(new))
                        if a == piece_end[CH - 2]:
                            pe.wait_ge(last_chunk_loaded, 16 * LOADS)
                        score_piece(a)
                for what, n in turns[u]:
                    if what == 'maxima':
                        turn_maxima(n)
                    else:
                        turn_output(n)
            for u in (UNITS - 2, UNITS - 1):
                for j in range(HG):
                    values(u, j)
            turn_output(ITEMS - 1)

            def turn_attn(t):
                for i in range(CT):
                    ins = pe.transpose(ps[:, t % 2, P * i:P * i + P], attn[:, CT * t + i, :], identf[:, :])
                ins.then_inc(at_turned, 1)

            pe.wait_ge(o_normed, ITEMS)
            turn_attn(0)
            turn_attn(1)
            for t in range(CH):
                pe.wait_ge(at_ready, t + 1)
                if t >= 2:
                    pe.wait_ge(y_read, t - 1)
                for i in range(CT):
                    ins = mm(ps[:, 2 + t % 2, P * i:P * i + P], attnT[:, t, P * i:P * i + P], wog[:, :])
                ins.then_inc(y_mm, 1)
                if t + 2 < CH:
                    turn_attn(t + 2)
            turn(1, 0, 4)
            turn(1, 1, 5)

            def path_scores(t):
                xm = cT[:, t % 2, :]
                pe.wait_ge(conv_ready, t + 1)
                mm(ps[0:DM, 7, :], wo1[:, :], xm).then_inc(u_mm, 1)
                if t >= 1:
                    pe.wait_ge(hid_ready, NG * t)
                for g in range(NG):
                    ins = mm(ps[0:GR, g, :], w1s[:, PG * g:PG * g + PG, :].rearrange("p a m -> p (a m)"), xm)
                ins.then_inc(hid_mm, 1)
                pe.wait_ge(t_ready, t + 1)
                for i in range(CT):
                    ins = mm(ps[:, 7, NP * i:NP * i + NP], taug[:, P * i:P * i + P], wo2[:, :])
                ins.then_inc(sc_mm, 1)

            def turn_hot(t):
                pe.wait_ge(hot_ready, t + 1)
                for i in range(CT):
                    ins = pe.transpose(hps[0:16, CW + P * i:CW + P * i + P], hot9[:, i, :], identb[:, :])
                ins.then_inc(hot_turned, 1)

            def turn2(which, t):
                pe.wait_ge(nrm_ready, CH * (2 + which) + t + 1)
                for i in range(CT):
                    ins = pe.transpose(ps[:, 0, P * i:P * i + P], nrm[:, CT * t + i, 0:D], identf[:, :])
                ins.then_inc(turned2[which], 1)

            def project_values(t):
                pe.wait_ge(hT2_ready[0], t + 1)
                rows = hT[:, 0, 1 + CW * t:1 + CW * t + CW]
                for i in range(CT):
                    ins = mm(ps[:, 0, P * i:P * i + P], rows[:, P * i:P * i + P], wvT[:, :])
                ins.then_inc(v2_mm, 1)

            pe.wait_ge(consts, 2)
            path_scores(0)
            for t in (2, 3):
                pe.wait_ge(hT_ready, CH + t - 1)
                turn(1, t, 4 + t % 2)
            turn_hot(0)
            pe.wait_ge(hT_ready, 2 * CH)
            for t in range(CH):
                pe.wait_ge(hot_copied, t + 1)
                for g in range(NG):
                    ins = mm(ps[0:GR, 3 + g, :], spread[:, PG * g:PG * g + PG, :].rearrange("p a m -> p (a m)"),
                             hotT[:, t % 2, :])
                ins.then_inc(mask_mm, 1)
                if t + 1 < CH:
                    path_scores(t + 1)
                else:
                    pe.wait_ge(hid_ready, NG * CH)
                    turn2(0, 0)
                    project_values(0)
                pe.wait_ge(hsel_ready, t + 1)
                if t >= 1:
                    pe.wait_ge(ffn_copied, t)
                for i in range(CT):
                    o = ps[:, 6, P * i:P * i + P]
                    s_ = slice(P * i, P * i + P)
                    mm(o, hT[:, 1, 1 + CW * t + P * i:1 + CW * t + P * i + P], identf[:, :], True, False)
                    for g in range(NG):
                        rows = GR + NP if g == 0 else GR
                        ins = mm(o, hsel[0:rows, g, s_], w2s[0:rows, g, :], False, g == NG - 1)
                    if i == CT // 2 - 1 and t + 1 < CH:
                        turn_hot(t + 1)
                ins.then_inc(ffn_mm, 1)

            def features(n):
                t, h = n // H1, n % H1
                if h == 0:
                    pe.wait_ge(hT2_ready[0], t + 1)
                if n >= 2:
                    pe.wait_ge(f_ready, n - 1)
                for k in range(2):
                    ins = mm(ps[:, 2 + 2 * (n % 2) + k, :], pfold[:, H1 * k + h, :],
                             hT[:, 0, 1 + CW * t:1 + CW * t + CW])
                ins.then_inc(f_mm, 1)

            def block_scores(n):
                pe.wait_ge(f_ready, n + 1)
                if n >= 1:
                    pe.wait_ge(s_ready, n)
                for i in range(CT):
                    s_ = slice(P * i, P * i + P)
                    ins = mm(ps[:, 6, s_], feat[:, n % 2, 1, s_], feat[:, n % 2, 0, s_])
                ins.then_inc(s_mm, 1)

            def block_values(n):
                t, h = n // H1, n % H1
                g = h // HH
                pe.wait_ge(s_ready, n + 1)
                if h == 0:
                    pe.wait_ge(v2_ready, t + 1)
                if h % HH == 0 and t >= 1:
                    pe.wait_ge(on_ready, 2 * (t - 1) + g + 1)
                for i in range(CT):
                    at = (HD + 1) * (HH * i + h % HH)
                    ins = mm(ps[:, 1 + 6 * g, at:at + HD + 1], am[:, n % 2, P * i:P * i + P], vone[:, t % 2, i, h, :])
                ins.then_inc(av_mm, 1)

            def between(t, h):
                if h == 1 and 1 <= t <= CH:
                    pe.wait_ge(on_ready, 2 * t)
                    if t == 1:
                        pe.wait_ge(v2_ready, 2)
                    else:
                        pe.wait_ge(r_shift, t - 1)
                    for i in range(CT):
                        ins = pe.transpose(ps[:, 0, P * i:P * i + P], on[:, i, :], identf[:, :])
                    ins.then_inc(on_turned, 1)
                if h == 2 and 1 <= t <= CH:
                    pe.wait_ge(onT_ready, t)
                    for i in range(CT):
                        o = ps[:, 0, P * i:P * i + P]
                        ins = mm(o, onT[:, P * i:P * i + P], woutT[:, :])
                    ins.then_inc(y1_mm, 1)
                if h == 3 and t + 1 < CH:
                    if t >= 1:
                        pe.wait_ge(y1_read, t)
                    turn2(0, t + 1)
                if h == 4 and t + 1 < CH:
                    project_values(t + 1)
                if h == 5 and t >= 2:
                    n0 = CT * (t - 2)
                    pe.wait_ge(r_mask, t - 1)
                    if t + 1 < CH:
                        pe.wait_ge(v2_ready, t + 2)
                    elif t < CH:
                        pe.wait_ge(y1_read, t)
                    elif t > CH:
                        pe.wait_ge(slots_ready, t - 2)
                    o = ps[:, pos_bank(t - 2), 0:CT * (E + 1)]
                    ch = chosen[:, n0:n0 + CT, :].rearrange("p t e -> p (t e)")
                    ins = mm(o, upto[:, :], ch, True, False)
                    for k in range(1, CT):
                        ins = mm(o[:, (E + 1) * k:], onesb[:, :], ch[:, 0:(E + 1) * (CT - k)], False,
                                 k == CT - 1 and n0 == 0)
                    for n in range(n0):
                        ins = mm(o.rearrange("p (t e) -> p t e", t=CT), onesb[:, :],
                                 chosen[:, n:n + 1, :].to_broadcast([P, CT, E + 1]), False, n == n0 - 1)
                    ins.then_inc(pos_mm, 1)
                if h == (6 if t < CH else 4) and 1 <= t <= CH:
                    if t == 1:
                        pe.wait_ge(v2_ready, t + 2)
                    elif t < CH:
                        pe.wait_ge(slots_ready, t - 1)
                    turn2(1, t - 1)
                if h == 7 and 1 <= t <= CH:
                    pe.wait_ge(hT2_ready[1], t)
                    for i in range(CT):
                        n = CT * (t - 1) + i
                        o = ps[:, 0, E * i:E * i + E]
                        ins = mm(o, hT[:, 1, 1 + P * n:1 + P * n + P], rw[:, :])
                    ins.then_inc(lg_mm, 1)

            features(0)
            features(1)
            for t in range(CH + 2):
                for h in range(H1):
                    n = H1 * t + h
                    if n < H1 * CH:
                        block_scores(n)
                    if n + 2 < H1 * CH:
                        features(n + 2)
                    if 1 <= n <= H1 * CH:
                        block_values(n - 1)
                    between(t, h)

            def turn_slots(e):
                pe.wait_ge(slots_loaded[e], 16 * 2)
                if e >= 2:
                    pe.wait_ge(xs_ready, e - 1)
                for n in range(ET):
                    m = min(P, CAP - P * n)
                    ins = pe.transpose(ps[:, e % 2, P * n:P * n + m], slotrows[0:m, e, n, 0:D], identf[0:m, 0:m])
                ins.then_inc(xs_turned, 1)

            def expert_up(e):
                pe.wait_ge(xs_ready, e + 1)
                for c in range(HC):
                    if e >= 1:
                        pe.wait_ge(gelu_ready, HC * (e - 1) + c + 1)
                    mm(ps[:, 2 + c, 0:CAP], ew1s[:, e, P * c:P * c + P], xsT[:, CAP * e:CAP * e + CAP])\
                        .then_inc(e1_mm, 1)

            def expert_down(e):
                pe.wait_ge(gelu_ready, HC * (e + 1))
                for n in range(ET):
                    tile = ET * e + n
                    if tile >= 2:
                        pe.wait_ge(eo_ready, tile - 1)
                    m = min(P, CAP - P * n)
                    o = ps[0:m, 6 + tile % 2, 0:P]
                    for c in range(HC):
                        ins = mm(o, gT[:, e % 2, c, P * n:P * n + m], ew2s[:, e, c, :], c == 0, c == HC - 1)
                    ins.then_inc(e2_mm, 1)

            turn_slots(0)
            turn_slots(1)
            pe.wait_ge(ex_loaded, 16 * 3)
            expert_up(0)
            for e in range(E):
                if e + 2 < E:
                    turn_slots(e + 2)
                if e + 1 < E:
                    expert_up(e + 1)
                expert_down(e)


_INS = ['L0_attn_x', 'L0_attn_WQ', 'L0_attn_WK', 'L0_attn_WV', 'L0_attn_WO', 'L0_ffn_mix_kernel', 'L0_ffn_W1',
        'L0_ffn_b1', 'L0_ffn_W2', 'L0_ffn_b2', 'L0_ffn_Wo1', 'L0_ffn_bo1', 'L0_ffn_Wo2', 'L0_ffn_bo2',
        'L0_ffn_gamma', 'L0_ffn_beta', 'L0_c', 'L0_wmod', 'w_qkv_heads', 'w_v', 'L1_attn_w_out', 'L1_attn_b_out',
        'L1_attn_proj', 'L1_ffn_router_w', 'L1_ffn_router_b', 'L1_ffn_w1', 'L1_ffn_b1', 'L1_ffn_w2',
        'L1_ffn_b2', 'L1_c', 'L1_wmod']


def _laid_out(a):
    import numpy as np

    a = {n: np.asarray(v) for n, v in a.items()}
    a['L0_ffn_mix_kernel'] = a['L0_ffn_mix_kernel'].T
    a['L0_ffn_W1'] = a['L0_ffn_W1'].transpose(1, 0, 2)
    a['L0_ffn_b1'] = a['L0_ffn_b1'].reshape(3, 96).T
    a['L0_ffn_W2'] = a['L0_ffn_W2'].reshape(3, 96, 128).transpose(1, 0, 2)
    w = a.pop('L1_attn_w_qkv')
    a['w_qkv_heads'] = w.reshape(24, 16, 128).transpose(1, 0, 2)
    a['w_v'] = w[256:]
    a['L1_attn_proj'] = a['L1_attn_proj'].transpose(1, 0, 2)
    a['L1_ffn_w1'] = a['L1_ffn_w1'].transpose(1, 0, 2)
    a['L1_ffn_b1'] = a['L1_ffn_b1'].reshape(8, 4, 128).transpose(2, 0, 1)
    a['L1_ffn_w2'] = a['L1_ffn_w2'].reshape(8, 4, 128, 128).transpose(2, 0, 1, 3)
    return a


_OUTS = [((1, 2048, 128), 'float32')]


def kernel(**inputs):
    import numpy as _np
    import concourse.bacc as _bacc
    from concourse import mybir as _mybir
    from concourse.bass_utils import run_bass_kernel_spmd as _run

    nc = _bacc.Bacc("TRN2", target_bir_lowering=False, num_devices=1)
    arrays, args = {}, []
    inputs = _laid_out(inputs)
    for name in _INS:
        a = _np.ascontiguousarray(inputs[name])
        arrays[f"in_{name}_dram"] = a
        args.append(nc.dram_tensor(f"in_{name}_dram", a.shape, _mybir.dt.from_np(a.dtype), kind="ExternalInput").ap())
    for i, (shape, dtype) in enumerate(_OUTS):
        dt = _mybir.dt.from_np(_np.dtype(dtype))
        args.append(nc.dram_tensor(f"out_{i}_dram", shape, dt, kind="ExternalOutput").ap())
    adaln_two_layers(nc, *args)
    r = _run(nc, [arrays], core_ids=[0])
    got = tuple(r.results[0][f"out_{i}_dram"] for i in range(len(_OUTS)))
    return got[0]
```
